# Optimizing a Trainium2 kernel written in Bass

```python
import numpy as np
import jax
import jax.numpy as jnp

def _softmax(x, axis=-1):
    return jax.nn.softmax(x, axis=axis)

def _gelu(x):
    return jax.nn.gelu(x, approximate=True)

def _silu(x):
    return jax.nn.silu(x)

def _sigmoid(x):
    return jax.nn.sigmoid(x)

def _layernorm(x, axis=-1, eps=1e-05):
    m = jnp.mean(x, axis=axis, keepdims=True)
    v = jnp.var(x, axis=axis, keepdims=True)
    return (x - m) / jnp.sqrt(v + eps)

def _scatter_add(tgt, idx, src, axis=0):
    return tgt.at[idx].add(src)

def _segment_sum(src, seg, n):
    return jax.ops.segment_sum(src, seg, n)
kernel_name = 'mk_lm_tower_d4_tok_ids512_r4_36b264'

def setup_inputs(seed: int=0):
    np.random.seed(seed)
    _w = jnp.asarray

    def _rec_inputs():
        import jax
        import jax.numpy as jnp
        _rk = jax.random.key(seed)
        x = jax.random.randint(jax.random.fold_in(_rk, 1), (32, 128), 0, 12564, jnp.int32)
        return x
    x = _rec_inputs()

    def _L0_tok_setup():
        import jax, jax.numpy as jnp
        import numpy as np
        VOCAB = 50257
        UNITS = 128
        key = jax.random.key(seed)
        k_ids, k_w = jax.random.split(key)
        ids = jax.random.randint(k_ids, (8, 512), 0, VOCAB, dtype=jnp.int32)
        w = jax.random.normal(k_w, (VOCAB, UNITS), dtype=jnp.float32) * 0.05
        return {'input': ids, 'w': w}
    _L0_tok_all = _L0_tok_setup()
    _L0_tok_in = {k: v for k, v in _L0_tok_all.items() if k in ('w',)}
    del _L0_tok_all

    def _L0_attn_setup():
        import jax, jax.numpy as jnp
        import numpy as np
        DEPTH, S4_DEPTH, DIM, N2, FF = (4, 2, 128, 32, 512)
        B, L = (16, 512)

        def _layer_norm(x, w, b):
            mu = jnp.mean(x, axis=-1, keepdims=True)
            var = jnp.var(x, axis=-1, keepdims=True)
            return (x - mu) * jax.lax.rsqrt(var + 1e-05) * w + b

        def _s4_layer(u, logA_re, A_im, C_re, C_im, log_dt, D, ow, ob):
            Lq = u.shape[1]
            dt = jnp.exp(log_dt)
            A = -jnp.exp(logA_re) + 1j * A_im
            dtA = A * dt[:, None]
            C = (C_re + 1j * C_im) * (jnp.exp(dtA) - 1.0) / A
            K = 2.0 * jnp.einsum('hn,hnl->hl', C, jnp.exp(dtA[:, :, None] * jnp.arange(Lq))).real
            n = 2 * Lq
            y = jnp.fft.irfft(jnp.fft.rfft(u, n=n, axis=1) * jnp.fft.rfft(K.T, n=n, axis=0)[None], n=n, axis=1)[:, :Lq]
            y = jax.nn.gelu(y + u * D)
            z = y @ ow.T + ob
            a, g = jnp.split(z, 2, axis=-1)
            return a * jax.nn.sigmoid(g)
        key = jax.random.key(seed)
        ks = jax.random.split(key, 10)
        f = jax.random.normal
        a_im = jnp.broadcast_to(np.pi * jnp.arange(N2, dtype=jnp.float32), (DEPTH, S4_DEPTH, DIM, N2)) * 1.0
        return {'x': f(ks[0], (B, L, DIM), jnp.float32), 'ln1_w': jnp.ones((DEPTH, DIM), jnp.float32), 'ln1_b': jnp.zeros((DEPTH, DIM), jnp.float32), 'ln2_w': jnp.ones((DEPTH, DIM), jnp.float32), 'ln2_b': jnp.zeros((DEPTH, DIM), jnp.float32), 's4_log_A_real': jnp.full((DEPTH, S4_DEPTH, DIM, N2), np.log(0.5), jnp.float32), 's4_A_imag': a_im, 's4_C_re': f(ks[1], (DEPTH, S4_DEPTH, DIM, N2), jnp.float32) * 0.5, 's4_C_im': f(ks[2], (DEPTH, S4_DEPTH, DIM, N2), jnp.float32) * 0.5, 's4_log_dt': jax.random.uniform(ks[3], (DEPTH, S4_DEPTH, DIM), jnp.float32, np.log(0.001), np.log(0.1)), 's4_D': f(ks[4], (DEPTH, S4_DEPTH, DIM), jnp.float32), 's4_out_w': f(ks[5], (DEPTH, S4_DEPTH, 2 * DIM, DIM), jnp.float32) * 0.02, 's4_out_b': jnp.zeros((DEPTH, S4_DEPTH, 2 * DIM), jnp.float32), 'ff_w1': f(ks[6], (DEPTH, 2 * FF, DIM), jnp.float32) * 0.02, 'ff_b1': jnp.zeros((DEPTH, 2 * FF), jnp.float32), 'ff_w2': f(ks[7], (DEPTH, DIM, FF), jnp.float32) * 0.02, 'ff_b2': jnp.zeros((DEPTH, DIM), jnp.float32)}
    _L0_attn_all = _L0_attn_setup()
    _L0_attn_in = {k: v for k, v in _L0_attn_all.items() if k in ('ln1_w', 'ln1_b', 'ln2_w', 'ln2_b', 's4_log_A_real', 's4_A_imag', 's4_C_re', 's4_C_im', 's4_log_dt', 's4_D', 's4_out_w', 's4_out_b', 'ff_w1', 'ff_b1', 'ff_w2', 'ff_b2')}
    del _L0_attn_all

    def _L0_ffn_setup():
        import jax, jax.numpy as jnp
        import numpy as np
        EPS = 1e-05
        NUM_HEADS = 8
        TOP_K = 2
        CAP_FACTOR = 2

        def layernorm(x, g, b):
            m = jnp.mean(x, axis=-1, keepdims=True)
            v = jnp.var(x, axis=-1, keepdims=True)
            return (x - m) * jax.lax.rsqrt(v + EPS) * g + b
        key = jax.random.key(seed)
        ks = jax.random.split(key, 16)
        B, S, H, E, F = (2, 512, 128, 64, 512)
        s = 0.02
        return {'x': jax.random.normal(ks[0], (B, S, H), jnp.float32), 'ln1_g': jnp.ones((H,), jnp.float32), 'ln1_b': jnp.zeros((H,), jnp.float32), 'wq': jax.random.normal(ks[1], (H, H), jnp.float32) * s, 'wk': jax.random.normal(ks[2], (H, H), jnp.float32) * s, 'wv': jax.random.normal(ks[3], (H, H), jnp.float32) * s, 'wo': jax.random.normal(ks[4], (H, H), jnp.float32) * s, 'ln2_g': jnp.ones((H,), jnp.float32), 'ln2_b': jnp.zeros((H,), jnp.float32), 'wr': jax.random.normal(ks[5], (H, E), jnp.float32) * s, 'w1': jax.random.normal(ks[6], (E, H, F), jnp.float32) * s, 'b1': jnp.zeros((E, F), jnp.float32), 'w2': jax.random.normal(ks[7], (E, F, H), jnp.float32) * s, 'b2': jnp.zeros((E, H), jnp.float32)}
    _L0_ffn_all = _L0_ffn_setup()
    _L0_ffn_in = {k: v for k, v in _L0_ffn_all.items() if k in ('ln1_g', 'ln1_b', 'wq', 'wk', 'wv', 'wo', 'ln2_g', 'ln2_b', 'wr', 'w1', 'b1', 'w2', 'b2')}
    del _L0_ffn_all

    def _L1_attn_setup():
        import jax, jax.numpy as jnp
        import numpy as np
        THRE = 4.0
        EPS = 1e-05

        @jax.custom_vjp
        def spike(x):
            return jnp.floor(jnp.clip(x, 0.0, THRE) + 0.5)

        def _spike_fwd(x):
            return (spike(x), x)

        def _spike_bwd(x, g):
            return (g * ((x > 0) & (x < THRE)).astype(g.dtype),)
        spike.defvjp(_spike_fwd, _spike_bwd)
        key = jax.random.key(seed)
        k0, k1, k2 = jax.random.split(key, 3)
        B, N, C = (4, 256, 128)
        x = jax.random.normal(k0, (B, N, C), jnp.float32)
        Wqkv = jax.random.normal(k1, (3 * C, C), jnp.float32) * C ** (-0.5)
        gamma = jnp.ones((3 * C,), jnp.float32)
        beta = jnp.zeros((3 * C,), jnp.float32)
        Wproj = jax.random.normal(k2, (C, C), jnp.float32) * C ** (-0.5)
        bproj = jnp.zeros((C,), jnp.float32)
        return {'x': x, 'Wqkv': Wqkv, 'gamma': gamma, 'beta': beta, 'Wproj': Wproj, 'bproj': bproj}
    _L1_attn_all = _L1_attn_setup()
    _L1_attn_in = {k: v for k, v in _L1_attn_all.items() if k in ('Wqkv', 'gamma', 'beta', 'Wproj', 'bproj')}
    del _L1_attn_all

    def _L1_ffn_setup():
        import jax, jax.numpy as jnp
        import numpy as np
        B, S, D, H, E = (4, 512, 128, 8, 8)
        FF = 4 * D
        HD = D // H
        EPS = 1e-05

        def _layernorm(x, g, b):
            mu = jnp.mean(x, axis=-1, keepdims=True)
            var = jnp.mean((x - mu) ** 2, axis=-1, keepdims=True)
            return (x - mu) * jax.lax.rsqrt(var + EPS) * g + b
        key = jax.random.key(seed)
        ks = jax.random.split(key, 16)
        s = 0.02
        return {'x': jax.random.normal(ks[0], (B, S, D), dtype=jnp.float32), 'ln1_g': jnp.ones((D,), jnp.float32), 'ln1_b': jnp.zeros((D,), jnp.float32), 'Wq': jax.random.normal(ks[1], (D, D), jnp.float32) * s, 'bq': jnp.zeros((D,), jnp.float32), 'Wk': jax.random.normal(ks[2], (D, D), jnp.float32) * s, 'bk': jnp.zeros((D,), jnp.float32), 'Wv': jax.random.normal(ks[3], (D, D), jnp.float32) * s, 'bv': jnp.zeros((D,), jnp.float32), 'Wo': jax.random.normal(ks[4], (D, D), jnp.float32) * s, 'bo': jnp.zeros((D,), jnp.float32), 'gate_W': jax.random.normal(ks[5], (D, E), jnp.float32) * s, 'gate_b': jnp.zeros((E,), jnp.float32), 'W1': jax.random.normal(ks[6], (E, D, FF), jnp.float32) * s, 'b1': jnp.zeros((E, FF), jnp.float32), 'W2': jax.random.normal(ks[7], (E, FF, D), jnp.float32) * s, 'b2': jnp.zeros((E, D), jnp.float32)}
    _L1_ffn_all = _L1_ffn_setup()
    _L1_ffn_in = {k: v for k, v in _L1_ffn_all.items() if k in ('ln1_g', 'ln1_b', 'Wq', 'bq', 'Wk', 'bk', 'Wv', 'bv', 'Wo', 'bo', 'gate_W', 'gate_b', 'W1', 'b1', 'W2', 'b2')}
    del _L1_ffn_all

    def _L2_attn_setup():
        import jax, jax.numpy as jnp
        import numpy as np
        NUM_HEADS = 8
        MAX_DEPTH = 4
        ENTROPY_THRESHOLD = 0.8

        def _attn_level(x, w_qkv, b_qkv):
            B, T, D = x.shape
            H = NUM_HEADS
            hd = D // H
            qkv = (x @ w_qkv + b_qkv).reshape(B, T, 3, H, hd)
            qkv = jnp.transpose(qkv, (2, 0, 3, 1, 4))
            q, k, v = (qkv[0], qkv[1], qkv[2])
            scores = jnp.einsum('bhtd,bhsd->bhts', q, k) * D ** (-0.5)
            attn = jax.nn.softmax(scores, axis=-1)
            max_ent = jnp.log(jnp.float32(T))
            entropy = jnp.mean(-jnp.sum(attn * jnp.log(attn), axis=-1) / max_ent)
            out = jnp.einsum('bhts,bhsd->bhtd', attn, v)
            out = jnp.transpose(out, (0, 2, 1, 3)).reshape(B, T, D)
            return (out, entropy)

        def _fractal(x, w_qkv, b_qkv, depth):
            out, entropy = _attn_level(x, w_qkv, b_qkv)
            if depth < MAX_DEPTH:
                gate = (entropy < ENTROPY_THRESHOLD).astype(x.dtype)
                deeper = _fractal(out, w_qkv, b_qkv, depth + 1)
                return out + gate * deeper
            return out
        key = jax.random.key(seed)
        ks = jax.random.split(key, 5)
        B, T, D = (4, 256, 128)
        return {'x': jax.random.normal(ks[0], (B, T, D), dtype=jnp.float32), 'w_qkv': jax.random.normal(ks[1], (D, 3 * D), dtype=jnp.float32) * D ** (-0.5), 'b_qkv': jax.random.normal(ks[2], (3 * D,), dtype=jnp.float32) * 0.01, 'w_out': jax.random.normal(ks[3], (D, D), dtype=jnp.float32) * D ** (-0.5), 'b_out': jax.random.normal(ks[4], (D,), dtype=jnp.float32) * 0.01}
    _L2_attn_all = _L2_attn_setup()
    _L2_attn_in = {k: v for k, v in _L2_attn_all.items() if k in ('w_qkv', 'b_qkv', 'w_out', 'b_out')}
    del _L2_attn_all

    def _L2_ffn_setup():
        import jax, jax.numpy as jnp
        import numpy as np
        EPS = 1e-05
        TOP_K = 2

        def _moe_forward(x, Wg, W1, b1, W2, b2, gamma, beta):
            B, S, D = x.shape
            xf = x.reshape(-1, D)
            logits = xf @ Wg
            topv, topi = jax.lax.top_k(logits, TOP_K)
            gate_w = jax.nn.softmax(topv, axis=-1)
            h = jax.nn.relu(jnp.einsum('td,edh->teh', xf, W1) + b1[None])
            y = jnp.einsum('teh,ehd->ted', h, W2) + b2[None]
            mu = jnp.mean(y, axis=-1, keepdims=True)
            var = jnp.mean((y - mu) ** 2, axis=-1, keepdims=True)
            y = (y - mu) / jnp.sqrt(var + EPS) * gamma[None] + beta[None]
            y_sel = jnp.take_along_axis(y, topi[:, :, None], axis=1)
            out = jnp.sum(gate_w[:, :, None] * y_sel, axis=1)
            return out.reshape(B, S, D)
        key = jax.random.key(seed)
        ks = jax.random.split(key, 8)
        B, S, D, H, E = (4, 512, 128, 128, 8)
        sd = lambda fan_in: 1.0 / np.sqrt(fan_in)
        x = jax.random.normal(ks[0], (B, S, D), dtype=jnp.float32)
        Wg = jax.random.uniform(ks[1], (D, E), jnp.float32, -sd(D), sd(D))
        W1 = jax.random.uniform(ks[2], (E, D, H), jnp.float32, -sd(D), sd(D))
        b1 = jax.random.uniform(ks[3], (E, H), jnp.float32, -sd(D), sd(D))
        W2 = jax.random.uniform(ks[4], (E, H, D), jnp.float32, -sd(H), sd(H))
        b2 = jax.random.uniform(ks[5], (E, D), jnp.float32, -sd(H), sd(H))
        gamma = jnp.ones((E, D), jnp.float32)
        beta = jnp.zeros((E, D), jnp.float32)
        return {'x': x, 'Wg': Wg, 'W1': W1, 'b1': b1, 'W2': W2, 'b2': b2, 'gamma': gamma, 'beta': beta}
    _L2_ffn_all = _L2_ffn_setup()
    _L2_ffn_in = {k: v for k, v in _L2_ffn_all.items() if k in ('Wg', 'W1', 'b1', 'W2', 'b2', 'gamma', 'beta')}
    del _L2_ffn_all

    def _L3_attn_setup():
        import jax, jax.numpy as jnp
        import numpy as np
        import math
        HEADS = 8
        key = jax.random.key(seed)
        ks = jax.random.split(key, 9)
        B, T, E = (2, 512, 128)
        s = 1.0 / math.sqrt(E)
        return {'x': jax.random.normal(ks[0], (B, T, E), jnp.float32), 'wq': jax.random.normal(ks[1], (E, E), jnp.float32) * s, 'bq': jax.random.normal(ks[2], (E,), jnp.float32) * s, 'wk': jax.random.normal(ks[3], (E, E), jnp.float32) * s, 'bk': jax.random.normal(ks[4], (E,), jnp.float32) * s, 'wv': jax.random.normal(ks[5], (E, E), jnp.float32) * s, 'bv': jax.random.normal(ks[6], (E,), jnp.float32) * s, 'wg': jax.random.normal(ks[7], (E, E), jnp.float32) * s, 'bg': jax.random.normal(ks[8], (E,), jnp.float32) * s}
    _L3_attn_all = _L3_attn_setup()
    _L3_attn_in = {k: v for k, v in _L3_attn_all.items() if k in ('wq', 'bq', 'wk', 'bk', 'wv', 'bv', 'wg', 'bg')}
    del _L3_attn_all

    def _L3_ffn_setup():
        import jax, jax.numpy as jnp
        import numpy as np
        H = 128
        F = 512
        E = 16
        SHARED = 2
        TOP_K = 4
        B, S = (2, 512)

        def _mlp(x, w1, b1, w2, b2):
            return jax.nn.gelu(x @ w1 + b1, approximate=False) @ w2 + b2
        key = jax.random.key(seed)
        ks = jax.random.split(key, 10)
        sc = 0.02
        return {'hidden_states': jax.random.normal(ks[0], (B, S, H), dtype=jnp.float32), 'gate_w': jax.random.normal(ks[1], (E, H), dtype=jnp.float32) * sc, 're_w1': jax.random.normal(ks[2], (E, H, F), dtype=jnp.float32) * sc, 're_b1': jnp.zeros((E, F), dtype=jnp.float32), 're_w2': jax.random.normal(ks[3], (E, F, H), dtype=jnp.float32) * sc, 're_b2': jnp.zeros((E, H), dtype=jnp.float32), 'se_w1': jax.random.normal(ks[4], (SHARED, H, F), dtype=jnp.float32) * sc, 'se_b1': jnp.zeros((SHARED, F), dtype=jnp.float32), 'se_w2': jax.random.normal(ks[5], (SHARED, F, H), dtype=jnp.float32) * sc, 'se_b2': jnp.zeros((SHARED, H), dtype=jnp.float32)}
    _L3_ffn_all = _L3_ffn_setup()
    _L3_ffn_in = {k: v for k, v in _L3_ffn_all.items() if k in ('gate_w', 're_w1', 're_b1', 're_w2', 're_b2', 'se_w1', 'se_b1', 'se_w2', 'se_b2')}
    del _L3_ffn_all
    return {'x': x, 'L0_tok_w': _L0_tok_in['w'], 'L0_attn_ln1_w': _L0_attn_in['ln1_w'], 'L0_attn_ln1_b': _L0_attn_in['ln1_b'], 'L0_attn_ln2_w': _L0_attn_in['ln2_w'], 'L0_attn_ln2_b': _L0_attn_in['ln2_b'], 'L0_attn_s4_log_A_real': _L0_attn_in['s4_log_A_real'], 'L0_attn_s4_A_imag': _L0_attn_in['s4_A_imag'], 'L0_attn_s4_C_re': _L0_attn_in['s4_C_re'], 'L0_attn_s4_C_im': _L0_attn_in['s4_C_im'], 'L0_attn_s4_log_dt': _L0_attn_in['s4_log_dt'], 'L0_attn_s4_D': _L0_attn_in['s4_D'], 'L0_attn_s4_out_w': _L0_attn_in['s4_out_w'], 'L0_attn_s4_out_b': _L0_attn_in['s4_out_b'], 'L0_attn_ff_w1': _L0_attn_in['ff_w1'], 'L0_attn_ff_b1': _L0_attn_in['ff_b1'], 'L0_attn_ff_w2': _L0_attn_in['ff_w2'], 'L0_attn_ff_b2': _L0_attn_in['ff_b2'], 'L0_ffn_ln1_g': _L0_ffn_in['ln1_g'], 'L0_ffn_ln1_b': _L0_ffn_in['ln1_b'], 'L0_ffn_wq': _L0_ffn_in['wq'], 'L0_ffn_wk': _L0_ffn_in['wk'], 'L0_ffn_wv': _L0_ffn_in['wv'], 'L0_ffn_wo': _L0_ffn_in['wo'], 'L0_ffn_ln2_g': _L0_ffn_in['ln2_g'], 'L0_ffn_ln2_b': _L0_ffn_in['ln2_b'], 'L0_ffn_wr': _L0_ffn_in['wr'], 'L0_ffn_w1': _L0_ffn_in['w1'], 'L0_ffn_b1': _L0_ffn_in['b1'], 'L0_ffn_w2': _L0_ffn_in['w2'], 'L0_ffn_b2': _L0_ffn_in['b2'], 'L1_attn_Wqkv': _L1_attn_in['Wqkv'], 'L1_attn_gamma': _L1_attn_in['gamma'], 'L1_attn_beta': _L1_attn_in['beta'], 'L1_attn_Wproj': _L1_attn_in['Wproj'], 'L1_attn_bproj': _L1_attn_in['bproj'], 'L1_ffn_ln1_g': _L1_ffn_in['ln1_g'], 'L1_ffn_ln1_b': _L1_ffn_in['ln1_b'], 'L1_ffn_Wq': _L1_ffn_in['Wq'], 'L1_ffn_bq': _L1_ffn_in['bq'], 'L1_ffn_Wk': _L1_ffn_in['Wk'], 'L1_ffn_bk': _L1_ffn_in['bk'], 'L1_ffn_Wv': _L1_ffn_in['Wv'], 'L1_ffn_bv': _L1_ffn_in['bv'], 'L1_ffn_Wo': _L1_ffn_in['Wo'], 'L1_ffn_bo': _L1_ffn_in['bo'], 'L1_ffn_gate_W': _L1_ffn_in['gate_W'], 'L1_ffn_gate_b': _L1_ffn_in['gate_b'], 'L1_ffn_W1': _L1_ffn_in['W1'], 'L1_ffn_b1': _L1_ffn_in['b1'], 'L1_ffn_W2': _L1_ffn_in['W2'], 'L1_ffn_b2': _L1_ffn_in['b2'], 'L2_attn_w_qkv': _L2_attn_in['w_qkv'], 'L2_attn_b_qkv': _L2_attn_in['b_qkv'], 'L2_attn_w_out': _L2_attn_in['w_out'], 'L2_attn_b_out': _L2_attn_in['b_out'], 'L2_ffn_Wg': _L2_ffn_in['Wg'], 'L2_ffn_W1': _L2_ffn_in['W1'], 'L2_ffn_b1': _L2_ffn_in['b1'], 'L2_ffn_W2': _L2_ffn_in['W2'], 'L2_ffn_b2': _L2_ffn_in['b2'], 'L2_ffn_gamma': _L2_ffn_in['gamma'], 'L2_ffn_beta': _L2_ffn_in['beta'], 'L3_attn_wq': _L3_attn_in['wq'], 'L3_attn_bq': _L3_attn_in['bq'], 'L3_attn_wk': _L3_attn_in['wk'], 'L3_attn_bk': _L3_attn_in['bk'], 'L3_attn_wv': _L3_attn_in['wv'], 'L3_attn_bv': _L3_attn_in['bv'], 'L3_attn_wg': _L3_attn_in['wg'], 'L3_attn_bg': _L3_attn_in['bg'], 'L3_ffn_gate_w': _L3_ffn_in['gate_w'], 'L3_ffn_re_w1': _L3_ffn_in['re_w1'], 'L3_ffn_re_b1': _L3_ffn_in['re_b1'], 'L3_ffn_re_w2': _L3_ffn_in['re_w2'], 'L3_ffn_re_b2': _L3_ffn_in['re_b2'], 'L3_ffn_se_w1': _L3_ffn_in['se_w1'], 'L3_ffn_se_b1': _L3_ffn_in['se_b1'], 'L3_ffn_se_w2': _L3_ffn_in['se_w2'], 'L3_ffn_se_b2': _L3_ffn_in['se_b2']}

def reference(x, L0_tok_w, L0_attn_ln1_w, L0_attn_ln1_b, L0_attn_ln2_w, L0_attn_ln2_b, L0_attn_s4_log_A_real, L0_attn_s4_A_imag, L0_attn_s4_C_re, L0_attn_s4_C_im, L0_attn_s4_log_dt, L0_attn_s4_D, L0_attn_s4_out_w, L0_attn_s4_out_b, L0_attn_ff_w1, L0_attn_ff_b1, L0_attn_ff_w2, L0_attn_ff_b2, L0_ffn_ln1_g, L0_ffn_ln1_b, L0_ffn_wq, L0_ffn_wk, L0_ffn_wv, L0_ffn_wo, L0_ffn_ln2_g, L0_ffn_ln2_b, L0_ffn_wr, L0_ffn_w1, L0_ffn_b1, L0_ffn_w2, L0_ffn_b2, L1_attn_Wqkv, L1_attn_gamma, L1_attn_beta, L1_attn_Wproj, L1_attn_bproj, L1_ffn_ln1_g, L1_ffn_ln1_b, L1_ffn_Wq, L1_ffn_bq, L1_ffn_Wk, L1_ffn_bk, L1_ffn_Wv, L1_ffn_bv, L1_ffn_Wo, L1_ffn_bo, L1_ffn_gate_W, L1_ffn_gate_b, L1_ffn_W1, L1_ffn_b1, L1_ffn_W2, L1_ffn_b2, L2_attn_w_qkv, L2_attn_b_qkv, L2_attn_w_out, L2_attn_b_out, L2_ffn_Wg, L2_ffn_W1, L2_ffn_b1, L2_ffn_W2, L2_ffn_b2, L2_ffn_gamma, L2_ffn_beta, L3_attn_wq, L3_attn_bq, L3_attn_wk, L3_attn_bk, L3_attn_wv, L3_attn_bv, L3_attn_wg, L3_attn_bg, L3_ffn_gate_w, L3_ffn_re_w1, L3_ffn_re_b1, L3_ffn_re_w2, L3_ffn_re_b2, L3_ffn_se_w1, L3_ffn_se_b1, L3_ffn_se_w2, L3_ffn_se_b2):
    import jax
    import jax.numpy as jnp

    def _L0_tok_ref(input, w):
        import jax, jax.numpy as jnp
        import numpy as np
        VOCAB = 50257
        UNITS = 128
        return jnp.take(w, input, axis=0)

    def _L0_attn_ref(x, ln1_w, ln1_b, ln2_w, ln2_b, s4_log_A_real, s4_A_imag, s4_C_re, s4_C_im, s4_log_dt, s4_D, s4_out_w, s4_out_b, ff_w1, ff_b1, ff_w2, ff_b2):
        import jax, jax.numpy as jnp
        import numpy as np
        DEPTH, S4_DEPTH, DIM, N2, FF = (4, 2, 128, 32, 512)
        B, L = (16, 512)

        def _layer_norm(x, w, b):
            mu = jnp.mean(x, axis=-1, keepdims=True)
            var = jnp.var(x, axis=-1, keepdims=True)
            return (x - mu) * jax.lax.rsqrt(var + 1e-05) * w + b

        def _s4_layer(u, logA_re, A_im, C_re, C_im, log_dt, D, ow, ob):
            Lq = u.shape[1]
            dt = jnp.exp(log_dt)
            A = -jnp.exp(logA_re) + 1j * A_im
            dtA = A * dt[:, None]
            C = (C_re + 1j * C_im) * (jnp.exp(dtA) - 1.0) / A
            K = 2.0 * jnp.einsum('hn,hnl->hl', C, jnp.exp(dtA[:, :, None] * jnp.arange(Lq))).real
            n = 2 * Lq
            y = jnp.fft.irfft(jnp.fft.rfft(u, n=n, axis=1) * jnp.fft.rfft(K.T, n=n, axis=0)[None], n=n, axis=1)[:, :Lq]
            y = jax.nn.gelu(y + u * D)
            z = y @ ow.T + ob
            a, g = jnp.split(z, 2, axis=-1)
            return a * jax.nn.sigmoid(g)
        for i in range(DEPTH):
            h = _layer_norm(x, ln1_w[i], ln1_b[i])
            for j in range(S4_DEPTH):
                h = _s4_layer(h, s4_log_A_real[i, j], s4_A_imag[i, j], s4_C_re[i, j], s4_C_im[i, j], s4_log_dt[i, j], s4_D[i, j], s4_out_w[i, j], s4_out_b[i, j])
            x = h + x
            h = _layer_norm(x, ln2_w[i], ln2_b[i])
            z = h @ ff_w1[i].T + ff_b1[i]
            a, g = jnp.split(z, 2, axis=-1)
            x = a * jax.nn.silu(g) @ ff_w2[i].T + ff_b2[i] + x
        return x

    def _L0_ffn_ref(x, ln1_g, ln1_b, wq, wk, wv, wo, ln2_g, ln2_b, wr, w1, b1, w2, b2):
        import jax, jax.numpy as jnp
        import numpy as np
        EPS = 1e-05
        NUM_HEADS = 8
        TOP_K = 2
        CAP_FACTOR = 2

        def layernorm(x, g, b):
            m = jnp.mean(x, axis=-1, keepdims=True)
            v = jnp.var(x, axis=-1, keepdims=True)
            return (x - m) * jax.lax.rsqrt(v + EPS) * g + b
        B, S, H = x.shape
        NH = NUM_HEADS
        dh = H // NH
        x1 = layernorm(x, ln1_g, ln1_b)
        q = (x1 @ wq).reshape(B, S, NH, dh)
        k = (x1 @ wk).reshape(B, S, NH, dh)
        v = (x1 @ wv).reshape(B, S, NH, dh)
        scores = jnp.einsum('bqhd,bkhd->bhqk', q, k) * dh ** (-0.5)
        p = jax.nn.softmax(scores, axis=-1)
        attn_out = jnp.einsum('bhqk,bkhd->bqhd', p, v).reshape(B, S, H) @ wo
        x = x + attn_out
        x2 = layernorm(x, ln2_g, ln2_b).reshape(B * S, H)
        T = B * S
        E = wr.shape[1]
        C = CAP_FACTOR * (T * TOP_K // E)
        probs = jax.nn.softmax(x2 @ wr, axis=-1)
        gate_v, gate_i = jax.lax.top_k(probs, TOP_K)
        gate_v = gate_v / jnp.sum(gate_v, axis=-1, keepdims=True)
        ef = gate_i.reshape(-1)
        gf = gate_v.reshape(-1)
        oh = jax.nn.one_hot(ef, E, dtype=x2.dtype)
        pos = jnp.sum((jnp.cumsum(oh, axis=0) - oh) * oh, axis=1).astype(jnp.int32)
        keep = (pos < C).astype(x2.dtype)
        posc = jnp.minimum(pos, C - 1)
        tok = jnp.repeat(x2, TOP_K, axis=0) * keep[:, None]
        buf = jnp.zeros((E, C, H), x2.dtype).at[ef, posc].add(tok)
        h = jax.nn.gelu(jnp.einsum('ech,ehf->ecf', buf, w1) + b1[:, None, :])
        y = jnp.einsum('ecf,efh->ech', h, w2) + b2[:, None, :]
        ys = y[ef, posc] * (gf * keep)[:, None]
        moe_out = ys.reshape(T, TOP_K, H).sum(axis=1).reshape(B, S, H)
        return x + moe_out

    def _L1_attn_ref(x, Wqkv, gamma, beta, Wproj, bproj):
        import jax, jax.numpy as jnp
        import numpy as np
        THRE = 4.0
        EPS = 1e-05

        @jax.custom_vjp
        def spike(x):
            return jnp.floor(jnp.clip(x, 0.0, THRE) + 0.5)

        def _spike_fwd(x):
            return (spike(x), x)

        def _spike_bwd(x, g):
            return (g * ((x > 0) & (x < THRE)).astype(g.dtype),)
        spike.defvjp(_spike_fwd, _spike_bwd)
        B, N, C = x.shape
        H = 8
        hd = C // H
        scale = hd ** (-0.5)
        xs = spike(x)
        qkv = jnp.einsum('bnc,dc->bnd', xs, Wqkv)
        mu = qkv.mean(axis=(0, 1))
        var = qkv.var(axis=(0, 1))
        qkv = (qkv - mu) * jax.lax.rsqrt(var + EPS) * gamma + beta
        qkv = qkv.reshape(B, N, 3, H, hd).transpose(2, 0, 3, 1, 4)
        q = spike(qkv[0])
        k = spike(qkv[1])
        v = spike(qkv[2])
        attn = jnp.einsum('bhnd,bhmd->bhnm', q, k)
        attn = spike(attn)
        out = jnp.einsum('bhnm,bhmd->bhnd', attn, v) * scale
        out = out.transpose(0, 2, 1, 3).reshape(B, N, C)
        out = spike(out)
        return jnp.einsum('bnc,dc->bnd', out, Wproj) + bproj

    def _L1_ffn_ref(x, ln1_g, ln1_b, Wq, bq, Wk, bk, Wv, bv, Wo, bo, gate_W, gate_b, W1, b1, W2, b2):
        import jax, jax.numpy as jnp
        import numpy as np
        B, S, D, H, E = (4, 512, 128, 8, 8)
        FF = 4 * D
        HD = D // H
        EPS = 1e-05

        def _layernorm(x, g, b):
            mu = jnp.mean(x, axis=-1, keepdims=True)
            var = jnp.mean((x - mu) ** 2, axis=-1, keepdims=True)
            return (x - mu) * jax.lax.rsqrt(var + EPS) * g + b
        b, s, d = x.shape
        q = (x @ Wq + bq).reshape(b, s, H, HD)
        k = (x @ Wk + bk).reshape(b, s, H, HD)
        v = (x @ Wv + bv).reshape(b, s, H, HD)
        scores = jnp.einsum('bqhd,bkhd->bhqk', q, k) / jnp.sqrt(jnp.float32(HD))
        attn = jax.nn.softmax(scores, axis=-1)
        o = jnp.einsum('bhqk,bkhd->bqhd', attn, v).reshape(b, s, d) @ Wo + bo
        h = _layernorm(x + o, ln1_g, ln1_b)
        t = h.reshape(b * s, d)
        probs = jax.nn.softmax(t @ gate_W + gate_b, axis=-1)
        idx = jnp.argmax(probs, axis=-1)
        gw = jnp.max(probs, axis=-1)
        hid = jax.nn.gelu(jnp.einsum('nd,edf->enf', t, W1) + b1[:, None, :])
        out_all = jnp.einsum('enf,efd->end', hid, W2) + b2[:, None, :]
        onehot = jax.nn.one_hot(idx, E, dtype=t.dtype)
        out = jnp.einsum('ne,end->nd', onehot, out_all)
        out = out * gw[:, None]
        return out.reshape(b, s, d)

    def _L2_attn_ref(x, w_qkv, b_qkv, w_out, b_out):
        import jax, jax.numpy as jnp
        import numpy as np
        NUM_HEADS = 8
        MAX_DEPTH = 4
        ENTROPY_THRESHOLD = 0.8

        def _attn_level(x, w_qkv, b_qkv):
            B, T, D = x.shape
            H = NUM_HEADS
            hd = D // H
            qkv = (x @ w_qkv + b_qkv).reshape(B, T, 3, H, hd)
            qkv = jnp.transpose(qkv, (2, 0, 3, 1, 4))
            q, k, v = (qkv[0], qkv[1], qkv[2])
            scores = jnp.einsum('bhtd,bhsd->bhts', q, k) * D ** (-0.5)
            attn = jax.nn.softmax(scores, axis=-1)
            max_ent = jnp.log(jnp.float32(T))
            entropy = jnp.mean(-jnp.sum(attn * jnp.log(attn), axis=-1) / max_ent)
            out = jnp.einsum('bhts,bhsd->bhtd', attn, v)
            out = jnp.transpose(out, (0, 2, 1, 3)).reshape(B, T, D)
            return (out, entropy)

        def _fractal(x, w_qkv, b_qkv, depth):
            out, entropy = _attn_level(x, w_qkv, b_qkv)
            if depth < MAX_DEPTH:
                gate = (entropy < ENTROPY_THRESHOLD).astype(x.dtype)
                deeper = _fractal(out, w_qkv, b_qkv, depth + 1)
                return out + gate * deeper
            return out
        attn_out = _fractal(x, w_qkv, b_qkv, 0)
        return attn_out @ w_out + b_out

    def _L2_ffn_ref(x, Wg, W1, b1, W2, b2, gamma, beta):
        import jax, jax.numpy as jnp
        import numpy as np
        EPS = 1e-05
        TOP_K = 2

        def _moe_forward(x, Wg, W1, b1, W2, b2, gamma, beta):
            B, S, D = x.shape
            xf = x.reshape(-1, D)
            logits = xf @ Wg
            topv, topi = jax.lax.top_k(logits, TOP_K)
            gate_w = jax.nn.softmax(topv, axis=-1)
            h = jax.nn.relu(jnp.einsum('td,edh->teh', xf, W1) + b1[None])
            y = jnp.einsum('teh,ehd->ted', h, W2) + b2[None]
            mu = jnp.mean(y, axis=-1, keepdims=True)
            var = jnp.mean((y - mu) ** 2, axis=-1, keepdims=True)
            y = (y - mu) / jnp.sqrt(var + EPS) * gamma[None] + beta[None]
            y_sel = jnp.take_along_axis(y, topi[:, :, None], axis=1)
            out = jnp.sum(gate_w[:, :, None] * y_sel, axis=1)
            return out.reshape(B, S, D)
        return _moe_forward(x, Wg, W1, b1, W2, b2, gamma, beta)

    def _L3_attn_ref(x, wq, bq, wk, bk, wv, bv, wg, bg):
        import jax, jax.numpy as jnp
        import numpy as np
        import math
        HEADS = 8
        B, T, E = x.shape
        H = HEADS
        D = E // H
        gammas = 1.0 - 2.0 ** (-5.0 - jnp.arange(H, dtype=jnp.float32))
        q = (x @ wq.T + bq).reshape(B, T, H, D)
        k = (x @ wk.T + bk).reshape(B, T, H, D)
        v = (x @ wv.T + bv).reshape(B, T, H, D)
        idx = jnp.arange(T)
        rel = idx[None, :] - idx[:, None]
        decay = jnp.where(rel[None] >= 0, gammas[:, None, None] ** rel[None].astype(jnp.float32), 0.0)
        scores = jnp.einsum('bihd,bjhd->bhij', q, k) / math.sqrt(D)
        scores = scores * decay[None]
        out = jnp.einsum('bhij,bjhd->bihd', scores, v).reshape(B, T, E)
        gate = jax.nn.silu(x @ wg.T + bg)
        return gate * out

    def _L3_ffn_ref(hidden_states, gate_w, re_w1, re_b1, re_w2, re_b2, se_w1, se_b1, se_w2, se_b2):
        import jax, jax.numpy as jnp
        import numpy as np
        H = 128
        F = 512
        E = 16
        SHARED = 2
        TOP_K = 4
        B, S = (2, 512)

        def _mlp(x, w1, b1, w2, b2):
            return jax.nn.gelu(x @ w1 + b1, approximate=False) @ w2 + b2
        b, s, h = hidden_states.shape
        x = hidden_states.reshape(-1, h)
        gate_probs = jax.nn.softmax(x @ gate_w.T, axis=-1)
        top_v, top_i = jax.lax.top_k(gate_probs, TOP_K)
        top_v = jax.nn.softmax(top_v, axis=-1)
        combine = jnp.einsum('tk,tke->te', top_v, jax.nn.one_hot(top_i, E, dtype=x.dtype))
        routed = jnp.zeros_like(x)
        for e in range(E):
            routed = routed + combine[:, e:e + 1] * _mlp(x, re_w1[e], re_b1[e], re_w2[e], re_b2[e])
        shared = jnp.zeros_like(x)
        for j in range(SHARED):
            shared = shared + _mlp(x, se_w1[j], se_b1[j], se_w2[j], se_b2[j])
        shared = shared / SHARED
        return (routed + shared).reshape(b, s, h)
    h = _L0_tok_ref(x, L0_tok_w)
    h = h + _L0_attn_ref(_layernorm(h, axis=-1), L0_attn_ln1_w, L0_attn_ln1_b, L0_attn_ln2_w, L0_attn_ln2_b, L0_attn_s4_log_A_real, L0_attn_s4_A_imag, L0_attn_s4_C_re, L0_attn_s4_C_im, L0_attn_s4_log_dt, L0_attn_s4_D, L0_attn_s4_out_w, L0_attn_s4_out_b, L0_attn_ff_w1, L0_attn_ff_b1, L0_attn_ff_w2, L0_attn_ff_b2)
    h = h + _L0_ffn_ref(_layernorm(h, axis=-1), L0_ffn_ln1_g, L0_ffn_ln1_b, L0_ffn_wq, L0_ffn_wk, L0_ffn_wv, L0_ffn_wo, L0_ffn_ln2_g, L0_ffn_ln2_b, L0_ffn_wr, L0_ffn_w1, L0_ffn_b1, L0_ffn_w2, L0_ffn_b2)
    h = h + _L1_attn_ref(_layernorm(h, axis=-1), L1_attn_Wqkv, L1_attn_gamma, L1_attn_beta, L1_attn_Wproj, L1_attn_bproj)
    h = h + _L1_ffn_ref(_layernorm(h, axis=-1), L1_ffn_ln1_g, L1_ffn_ln1_b, L1_ffn_Wq, L1_ffn_bq, L1_ffn_Wk, L1_ffn_bk, L1_ffn_Wv, L1_ffn_bv, L1_ffn_Wo, L1_ffn_bo, L1_ffn_gate_W, L1_ffn_gate_b, L1_ffn_W1, L1_ffn_b1, L1_ffn_W2, L1_ffn_b2)
    h = h + _L2_attn_ref(_layernorm(h, axis=-1), L2_attn_w_qkv, L2_attn_b_qkv, L2_attn_w_out, L2_attn_b_out)
    h = h + _L2_ffn_ref(_layernorm(h, axis=-1), L2_ffn_Wg, L2_ffn_W1, L2_ffn_b1, L2_ffn_W2, L2_ffn_b2, L2_ffn_gamma, L2_ffn_beta)
    h = h + _L3_attn_ref(_layernorm(h, axis=-1), L3_attn_wq, L3_attn_bq, L3_attn_wk, L3_attn_bk, L3_attn_wv, L3_attn_bv, L3_attn_wg, L3_attn_bg)
    h = h + _L3_ffn_ref(_layernorm(h, axis=-1), L3_ffn_gate_w, L3_ffn_re_w1, L3_ffn_re_b1, L3_ffn_re_w2, L3_ffn_re_b2, L3_ffn_se_w1, L3_ffn_se_b1, L3_ffn_se_w2, L3_ffn_se_b2)
    return h

_drawn_inputs = setup_inputs


def setup_inputs(seed=0):
    import zlib

    import numpy as np

    out = dict(_drawn_inputs(seed))
    spreads = {'L0_attn_ln1_w': (1.0, 0.2),
     'L0_attn_ln1_b': (0.0, 0.311),
     'L0_attn_ln2_w': (1.0, 0.2),
     'L0_attn_ln2_b': (0.0, 0.1),
     'L0_attn_s4_log_A_real': (-0.6931471824645996, 0.6),
     'L0_attn_s4_out_b': (0.0, 0.1),
     'L0_attn_ff_b1': (0.0, 0.1),
     'L0_attn_ff_b2': (0.0, 0.1),
     'L0_ffn_ln1_g': (1.0, 0.2),
     'L0_ffn_ln1_b': (0.0, 0.1),
     'L0_ffn_ln2_g': (1.0, 0.2),
     'L0_ffn_ln2_b': (0.0, 0.1),
     'L0_ffn_b1': (0.0, 0.1),
     'L0_ffn_b2': (0.0, 0.1),
     'L1_attn_gamma': (1.0, 0.2),
     'L1_attn_beta': (0.0, 0.1),
     'L1_attn_bproj': (0.0, 0.1),
     'L1_ffn_ln1_g': (1.0, 0.6),
     'L1_ffn_ln1_b': (0.0, 0.8),
     'L1_ffn_bq': (0.0, 0.8),
     'L1_ffn_bk': (0.0, 2.0),
     'L1_ffn_bv': (0.0, 0.8),
     'L1_ffn_bo': (0.0, 0.8),
     'L1_ffn_gate_b': (0.0, 0.8),
     'L1_ffn_b1': (0.0, 0.8),
     'L1_ffn_b2': (0.0, 0.69),
     'L2_ffn_gamma': (1.0, 0.2),
     'L2_ffn_beta': (0.0, 0.311),
     'L3_ffn_re_b1': (0.0, 0.8),
     'L3_ffn_re_b2': (0.0, 2.0),
     'L3_ffn_se_b1': (0.0, 0.8),
     'L3_ffn_se_b2': (0.0, 2.0)}
    factors = {'L0_ffn_wq': 5.428,
     'L0_ffn_wk': 4.289,
     'L1_ffn_Wq': 8.0,
     'L1_ffn_Wk': 8.0,
     'L1_ffn_Wv': 8.0,
     'L1_ffn_Wo': 8.0,
     'L1_ffn_gate_W': 5.455,
     'L1_ffn_W1': 8.0,
     'L1_ffn_W2': 8.0,
     'L2_attn_b_qkv': 14.483,
     'L2_attn_b_out': 8.0,
     'L3_ffn_gate_w': 8.0,
     'L3_ffn_re_w1': 8.0,
     'L3_ffn_re_w2': 8.0,
     'L3_ffn_se_w1': 8.0,
     'L3_ffn_se_w2': 8.0}
    for name, (base, spread) in spreads.items():
        noise = np.random.default_rng([zlib.crc32(name.encode()), seed]).standard_normal(out[name].shape)
        drawn = base * np.exp(spread * noise) if base else spread * noise
        out[name] = jnp.asarray(drawn.astype(out[name].dtype))
    for name, factor in factors.items():
        out[name] = (out[name] * factor).astype(out[name].dtype)
    return out
```

```python
from contextlib import ExitStack

import numpy as np
import concourse.bass as bass
from concourse import mybir

F32 = mybir.dt.float32
BF16 = mybir.dt.bfloat16
I32 = mybir.dt.int32
U32 = mybir.dt.uint32
ALU = mybir.AluOpType
ACT = mybir.ActivationFunctionType
AX_X = mybir.AxisListType.X

P = 128
B = 32
G = 4
NCH = B // G
W = G * P
EPS = 1e-5
HEADS = 8
HD = P // HEADS
DEPTH = 4
NL = 2 * DEPTH
NS = 32
POOL_LAYERS = 3
NB_POW, NA_POW = 16, 8


def dft_tables():
    s, f = np.arange(P)[:, None], np.arange(P)[None, :]
    n = 2 * P
    angle = 2.0 * np.pi * ((s * f) % n) / n
    cos, sin = np.cos(angle), -np.sin(angle)
    alternating = np.where(np.arange(P) % 2 == 0, 1.0, -1.0)
    sin_nyq, cos_nyq = sin.copy(), cos.copy()
    sin_nyq[:, 0] = alternating
    cos_nyq[:, 0] = alternating
    inv_cos, inv_sin = 2.0 * cos.T / n, 2.0 * sin.T / n
    inv_cos[0, :] = 1.0 / n
    inv_sin[0, :] = alternating / n
    return np.stack([cos, sin_nyq, sin, cos_nyq, inv_cos, inv_sin], axis=1).astype(np.float32)


COS, SIN_NYQ, SIN, COS_NYQ, INV_COS, INV_SIN = range(6)


class Core:

    def __init__(self, nc, ctx, ins):
        self.nc, self.ins = nc, ins
        sb = lambda name, shape, dt=F32: ctx.enter_context(nc.sbuf_tensor(name, shape, dt))
        self.h = sb("h", [P, B, P])
        self.x = sb("x", [P, B, P])
        self.ident = sb("ident", [P, P])
        self.neg_half = sb("neg_half", [P, B])
        self.slots_in = nc.dram_tensor("slots_in", (SLOTS, P), F32).ap()
        self.slots_out = nc.dram_tensor("slots_out", (SLOTS, P), F32).ap()
        self.zero = sb("zero", [P, P])
        self.zeroed = ctx.enter_context(nc.semaphore("zeroed"))


def start_zeroing(core, sp):
    n = SLOTS // P
    sp.dma_start(core.slots_in.rearrange("(p n) d -> p n d", p=P),
                 core.zero[:, :].unsqueeze(1).broadcast_to((P, n, P))).then_inc(core.zeroed, 16)


class Stage:

    def __init__(self, core, name):
        self.nc, self.name, self.ctx, self.sems = core.nc, name, ExitStack(), []

    def __enter__(self):
        self.ctx.__enter__()
        return self

    def __exit__(self, *a):
        if self.sems and a[0] is None:
            self.nc.clear_and_free_semaphores(self.sems)
            self.nc.all_engine_barrier()
        return self.ctx.__exit__(*a)

    def sb(self, name, shape, dt=F32):
        return self.ctx.enter_context(self.nc.sbuf_tensor(f"{self.name}_{name}", shape, dt))

    def ps(self, name, shape, dt=F32):
        return self.ctx.enter_context(self.nc.psum_tensor(f"{self.name}_{name}", shape, dt))

    def sem(self, name):
        self.sems.append(self.nc.alloc_semaphore(f"{self.name}_{name}"))
        return self.sems[-1]


def chunk(t, c):
    return t[:, bass.ds(c * G, G), :]


def flat(ap):
    return ap.rearrange("p a b -> p (a b)")


def stage_setup(core, ids):
    nc, ins = core.nc, core.ins
    with Stage(core, "set") as st:
        ids_in, const_in, const_set = (st.sem(n) for n in ("ids_in", "const_in", "const_set"))
        with nc.Block() as block:
            @block.sync
            def _(sp):
                with nc.allow_non_contiguous_dma("token ids, one column per sequence"):
                    sp.dma_start(ids[:, :], ins["x"].rearrange("b s -> s b")).then_inc(ids_in, 16)
                sp.dma_start(core.ident[:, :], ins["ident"]).then_inc(const_in, 16)
                sp.wait_ge(const_in, 16)
                sp.wait_ge(ids_in, 16)

            @block.gpsimd
            def _(pool):
                nc.gpsimd.memset(core.zero[:, :], 0.0)
                nc.gpsimd.memset(core.neg_half[:, :], -0.5).then_inc(const_set, 1)
                pool.wait_ge(const_set, 1)


def stage_norm(core, name, src=None, dst=None, rows=None):
    src, dst = src or core.h, dst or core.x
    nc = core.nc
    with Stage(core, name) as st:
        stats, mv = st.sb("stats", [P, B, 6]), st.sb("mv", [P, B, 2])
        ve, rs = st.sb("ve", [P, B]), st.sb("rs", [P, B])
        gain_bias = st.sb("gain_bias", [P, 2, P])
        stats_done, var_done, rstd_done, rows_in, centred = (st.sem(n) for n in (
            "stats_done", "var_done", "rstd_done", "rows_in", "centred"))
        with nc.Block() as block:
            if rows:
                @block.sync
                def _(sp):
                    for k, row in enumerate(rows):
                        sp.dma_start(gain_bias[:, k, :], core.ins[row].partition_broadcast(P)).then_inc(rows_in, 16)

            @block.vector
            def _(dve):
                for c in range(NCH):
                    for b in range(G * c, G * c + G):
                        last = nc.vector.bn_stats(stats[:, b, :], src[:, b, :])
                    last.then_inc(stats_done, 1)
                for c in range(NCH):
                    dve.wait_ge(stats_done, c + 1)
                    for b in range(G * c, G * c + G):
                        last = nc.vector.bn_aggr(mv[:, b, :], stats[:, b, :])
                last.then_inc(stats_done, 1)
                dve.wait_ge(stats_done, NCH + 1)
                nc.vector.tensor_scalar(ve[:, :], mv[:, :, 1], EPS, None, ALU.add).then_inc(var_done, 1)
                if rows:
                    dve.wait_ge(rows_in, 32)
                    for b in range(B):
                        last = nc.vector.scalar_tensor_tensor(out=dst[:, b, :], in0=src[:, b, :], scalar=mv[:, b, 0:1],
                                                              in1=gain_bias[:, 0, :], op0=ALU.subtract, op1=ALU.mult)
                    last.then_inc(centred, 1)
                    dve.wait_ge(rstd_done, 1)
                    dve.wait_ge(centred, 1)
                    for b in range(B):
                        nc.vector.scalar_tensor_tensor(out=dst[:, b, :], in0=dst[:, b, :], scalar=rs[:, b:b + 1],
                                                       in1=gain_bias[:, 1, :], op0=ALU.mult, op1=ALU.add)
                    return
                dve.wait_ge(rstd_done, 1)
                for b in range(B):
                    nc.vector.tensor_scalar(dst[:, b, :], src[:, b, :], mv[:, b, 0:1], rs[:, b:b + 1],
                                            ALU.subtract, ALU.mult)

            @block.gpsimd
            def _(pool):
                pool.wait_ge(var_done, 1)
                nc.gpsimd.tensor_tensor(rs[:, :], ve[:, :], core.neg_half[:, :], ALU.pow).then_inc(rstd_done, 1)


def s4_kernels(core, kf, ids):
    nc, ins = core.nc, core.ins
    N = NL * NS
    with Stage(core, "s4k") as st:
        raw = st.sb("raw", [P, 3, N])
        skip = st.sb("skip", [P, NL])
        logs, exps = st.sb("logs", [P, N + NL]), st.sb("exps", [P, N + NL])
        small = st.sb("small", [P, 2 * N])
        whole, power_bits = st.sb("whole", [P, N + NL]), st.sb("power_bits", [P, N + NL], I32)
        expa, dt = exps[:, 0:N], exps[:, N:N + NL]
        dft = st.sb("dft", [P, 6, P])
        a_re, dta_re, dta_im = st.sb("a_re", [P, N]), st.sb("dta_re", [P, 2 * N]), st.sb("dta_im", [P, N])
        angles = st.sb("angles", [P, P // 2 * 2 * NS])
        ang, red, turns = (angles[:, 5 * N * k:5 * N * (k + 1)].rearrange("p (k n) -> p k n", n=N) for k in range(3))
        trig, mag = st.sb("trig", [P, 5, N]), st.sb("mag", [P, 2, N])
        mag_m1 = st.sb("mag_m1", [P, 2 * N])
        zb = st.sb("zb", [P, 2, NB_POW, N])
        za = st.sb("za", [P, 2, NA_POW, N])
        zm = st.sb("zm", [P, 2, N])
        sq = st.sb("sq", [P, 2, N])
        tmp = st.sb("tmp", [P, 4, 8 * N])
        num = st.sb("num", [P, 2, N])
        cc = st.sb("cc", [P, 2, N])
        den = st.sb("den", [P, 2, N])
        coef = st.sb("coef", [P, 2, NA_POW, N])
        prod = tmp[:, :, :].rearrange("p k n -> p (k n)").rearrange("p (l n) -> p l n", n=2 * NS)
        ker = st.sb("ker", [P, NL, P])
        ker_t = st.sb("ker_t", [P, NL, P])
        ps_t = st.ps("ps_t", [P, NL, P])
        ps_f = st.ps("ps_f", [P, 3, 512])
        raw_in, arg_done, trig_done, chain = (st.sem(n) for n in (
            "raw_in", "arg_done", "trig_done", "chain"))
        mul_done, ker_done, tr_done, trc_done, dft_done, kf_done = (st.sem(n) for n in (
            "mul_done", "ker_done", "tr_done", "trc_done", "dft_done", "kf_done"))
        rows_in, coef_done, pool_mul, reduced = (st.sem(n) for n in ("rows_in", "coef_done", "pool_mul", "reduced"))
        prod2 = [ap.rearrange("p (l n) -> p l n", n=2 * NS) for ap in (flat(core.x[:, :, :]), angles[:, :])]

        pool_rows = lambda a: prod2[a // 4][:, 16 * (a % 4):16 * (a % 4) + 16, :]

        def multiply(eng, to, layer):
            s = slice(layer * NS, (layer + 1) * NS)
            for a in range(NA_POW):
                for c in range(2):
                    made = eng.tensor_tensor(to(a)[:, :, c * NS:(c + 1) * NS],
                                             coef[:, c, a:a + 1, s].broadcast_to((P, NB_POW, NS)), zb[:, c, :, s], ALU.mult)
            return made

        with nc.Block() as block:
            @block.gpsimd
            def _(pool):
                for b in range(B):
                    nc.gpsimd.indirect_dma_start(core.h[:, b, :], None, ins["L0_tok_w"],
                                                 bass.IndirectOffsetOnAxis(ids[:, b:b + 1], 0)).then_inc(rows_in, 16)
                pool.wait_ge(rows_in, 16 * B)
                pool.wait_ge(coef_done, 1)
                for n, layer in enumerate(range(NL - POOL_LAYERS, NL)):
                    if n:
                        pool.wait_ge(reduced, n)
                    multiply(nc.gpsimd, pool_rows, layer).then_inc(pool_mul, 1)

            @block.sync
            def _(sp):
                for k, name in enumerate(("s4_log_A_real", "s4_A_imag", "s4_C_re", "s4_C_im")):
                    sp.dma_start((raw[:, k - 1, :] if k else logs[:, 0:N]).rearrange("p (l n) -> p l n", n=NS),
                                 ins["L0_attn_" + name].rearrange("i j h n -> h (i j) n")).then_inc(raw_in, 16)
                sp.dma_start(dft[:, :, :], ins["dft"]).then_inc(raw_in, 16)
                with nc.allow_non_contiguous_dma("one value per channel and layer"):
                    sp.dma_start(logs[:, N:N + NL], ins["L0_attn_s4_log_dt"].rearrange("i j h -> h (i j)")).then_inc(raw_in, 16)
                    sp.dma_start(skip[:, :], ins["L0_attn_s4_D"].rearrange("i j h -> h (i j)")).then_inc(raw_in, 16)
                sp.wait_ge(raw_in, 16 * 7)
                start_zeroing(core, sp)

            @block.scalar
            def _(act):
                act.wait_ge(arg_done, 1)
                nc.scalar.activation(flat(trig[:, :, :]), flat(red[:, :, :]), ACT.Sin).then_inc(trig_done, 1)

            @block.vector
            def _(dve):
                steps = [0]

                def then(*made):
                    made[-1].then_inc(chain, 1)
                    steps[0] += 1
                    dve.wait_ge(chain, steps[0])

                tt, ts = nc.vector.tensor_tensor, nc.vector.tensor_scalar

                def cmul(out, a, b, count, negate_im=False):
                    t = [tmp[:, k, 0:count * N].rearrange("p (k n) -> p k n", n=N) for k in range(4)]
                    then(tt(t[0], a[0], b[0], ALU.mult), tt(t[1], a[1], b[1], ALU.mult),
                         tt(t[2], a[0], b[1], ALU.mult), tt(t[3], a[1], b[0], ALU.mult))
                    if negate_im:
                        then(tt(out[0], t[0], t[1], ALU.subtract), nc.vector.scalar_tensor_tensor(
                            out=out[1], in0=t[2], scalar=-1.0, in1=t[3], op0=ALU.mult, op1=ALU.subtract))
                    else:
                        then(tt(out[0], t[0], t[1], ALU.subtract), tt(out[1], t[2], t[3], ALU.add))

                def expm1(out, x):
                    y = small[:, 0:x.shape[1]]
                    then(ts(y, x, -87.0, 87.0, ALU.max, ALU.min))
                    then(ts(y, y, 1.0 / 64.0, None, ALU.mult))
                    terms = 9
                    inverse = [1.0]
                    for k in range(1, terms + 1):
                        inverse.append(inverse[-1] / k)
                    then(ts(out, y, inverse[terms], None, ALU.mult))
                    for k in range(terms - 1, 0, -1):
                        then(nc.vector.scalar_tensor_tensor(out=out, in0=out, scalar=inverse[k], in1=y,
                                                            op0=ALU.add, op1=ALU.mult))
                    for _ in range(6):
                        then(nc.vector.scalar_tensor_tensor(out=out, in0=out, scalar=2.0, in1=out,
                                                            op0=ALU.add, op1=ALU.mult))

                def exp(out, x):
                    n = x.shape[1]
                    y, k, scale = small[:, 0:n], whole[:, 0:n], power_bits[:, 0:n]
                    ln2_hi = 0.693359375
                    ln2_lo = float(np.log(2.0) - ln2_hi)
                    then(ts(y, x, -87.0, 87.0, ALU.max, ALU.min))
                    then(ts(k, y, float(1.0 / np.log(2.0)), magic, ALU.mult, ALU.add))
                    then(ts(k, k, magic, None, ALU.subtract))
                    then(ts(scale, k, 127.0, None, ALU.add))
                    then(ts(scale, scale, 23, None, ALU.logical_shift_left))
                    for part in (ln2_hi, ln2_lo):
                        then(nc.vector.scalar_tensor_tensor(out=y, in0=k, scalar=-part, in1=y,
                                                            op0=ALU.mult, op1=ALU.add))
                    terms = 9
                    inverse = [1.0]
                    for j in range(1, terms + 1):
                        inverse.append(inverse[-1] / j)
                    then(ts(out, y, inverse[terms], None, ALU.mult))
                    for j in range(terms - 1, 0, -1):
                        then(nc.vector.scalar_tensor_tensor(out=out, in0=out, scalar=inverse[j], in1=y,
                                                            op0=ALU.add, op1=ALU.mult))
                    then(nc.vector.scalar_tensor_tensor(out=out, in0=out, scalar=1.0, in1=scale.bitcast(F32),
                                                        op0=ALU.add, op1=ALU.mult))

                magic = float(1.5 * 2 ** 23)
                dve.wait_ge(raw_in, 16 * 7)
                exp(exps[:, :], logs[:, :])
                dtb = dt.unsqueeze(2).broadcast_to((P, NL, NS))
                by_layer = lambda ap: ap.rearrange("p (l n) -> p l n", n=NS)
                then(ts(a_re[:, :], expa, -1.0, None, ALU.mult),
                     tt(by_layer(dta_im[:, :]), by_layer(raw[:, 0, :]), dtb, ALU.mult))
                then(tt(by_layer(dta_re[:, 0:N]), by_layer(a_re[:, :]), dtb, ALU.mult))
                then(ts(dta_re[:, N:2 * N], dta_re[:, 0:N], float(NB_POW), None, ALU.mult))
                expm1(mag_m1[:, :], dta_re[:, :])
                ts(flat(mag[:, :, :]), mag_m1[:, :], 1.0, None, ALU.add)
                two_pi = 2.0 * np.pi
                c1 = 6.28125
                c2 = float(np.float32(np.round((two_pi - c1) * 2 ** 22) / 2 ** 22))
                c3 = float(np.float32(two_pi - c1 - c2))
                nc.vector.tensor_copy(ang[:, 0:2, :], dta_im[:, :].unsqueeze(1).broadcast_to((P, 2, N)))
                ts(ang[:, 3:5, :], dta_im[:, :].unsqueeze(1).broadcast_to((P, 2, N)), float(NB_POW), None, ALU.mult)
                then(ts(ang[:, 2, :], dta_im[:, :], 0.5, None, ALU.mult))
                then(ts(turns[:, 0, :], ang[:, 0, :], 1.0 / two_pi, 0.25, ALU.mult, ALU.add),
                     ts(turns[:, 4, :], ang[:, 4, :], 1.0 / two_pi, 0.25, ALU.mult, ALU.add),
                     ts(turns[:, 1:4, :], ang[:, 1:4, :], 1.0 / two_pi, None, ALU.mult))
                then(ts(turns[:, :, :], turns[:, :, :], magic, None, ALU.add))
                then(ts(turns[:, :, :], turns[:, :, :], magic, None, ALU.subtract))
                src = ang[:, :, :]
                for c in (c1, c2, c3):
                    then(nc.vector.scalar_tensor_tensor(out=red[:, :, :], in0=turns[:, :, :], scalar=-c, in1=src,
                                                        op0=ALU.mult, op1=ALU.add))
                    src = red[:, :, :]
                for k in (0, 4):
                    made = ts(red[:, k, :], red[:, k, :], np.pi / 2, None, ALU.add)
                then(made)
                limit = float(np.float32(3.1415925))
                ts(red[:, :, :], red[:, :, :], -limit, limit, ALU.max, ALU.min).then_inc(arg_done, 1)
                nc.vector.memset(zb[:, 0, 0, :], 1.0)
                nc.vector.memset(zb[:, 1, 0, :], 0.0)
                nc.vector.memset(za[:, 0, 0, :], 1.0)
                nc.vector.memset(za[:, 1, 0, :], 0.0)
                dve.wait_ge(trig_done, 1)
                then(tt(zb[:, :, 1, :], trig[:, 0:2, :], mag[:, 0:1, :].broadcast_to((P, 2, N)), ALU.mult),
                     tt(za[:, 0, 1, :], trig[:, 4, :], mag[:, 1, :], ALU.mult),
                     tt(za[:, 1, 1, :], trig[:, 3, :], mag[:, 1, :], ALU.mult))
                one = lambda t: (t[:, 0:1, :], t[:, 1:2, :])
                many = lambda t, lo, hi: (t[:, 0, lo:hi, :], t[:, 1, lo:hi, :])
                then(tt(sq[:, 0, :], trig[:, 2, :], trig[:, 2, :], ALU.mult),
                     tt(sq[:, 1, :], mag_m1[:, 0:N], trig[:, 0, :], ALU.mult))
                then(nc.vector.scalar_tensor_tensor(out=num[:, 0, :], in0=sq[:, 0, :], scalar=-2.0, in1=sq[:, 1, :],
                                                    op0=ALU.mult, op1=ALU.add),
                     nc.vector.tensor_copy(num[:, 1, :], zb[:, 1, 1, :]),
                     tt(den[:, 0, :], a_re[:, :], a_re[:, :], ALU.mult),
                     tt(den[:, 1, :], raw[:, 0, :], raw[:, 0, :], ALU.mult))
                then(tt(den[:, 0, :], den[:, 0, :], den[:, 1, :], ALU.add))
                then(nc.vector.reciprocal(den[:, 1, :], den[:, 0, :]))
                cmul(one(cc), one(num), (raw[:, 1:2, :], raw[:, 2:3, :]), 1)
                then(ts(sq[:, 1, :], raw[:, 0, :], -1.0, None, ALU.mult),
                     nc.vector.tensor_copy(sq[:, 0, :], a_re[:, :]))
                cmul(one(num), one(cc), one(sq), 1)
                then(nc.vector.scalar_tensor_tensor(out=cc[:, :, :], in0=num[:, :, :], scalar=2.0,
                                                    in1=den[:, 1:2, :].broadcast_to((P, 2, N)),
                                                    op0=ALU.mult, op1=ALU.mult))
                for table, size in ((zb, NB_POW), (za, NA_POW)):
                    power, m = (table[:, 0, 1:2, :], table[:, 1, 1:2, :]), 2
                    while m < size:
                        cmul(one(sq), power, power, 1)
                        then(nc.vector.tensor_copy(zm[:, :, :], sq[:, :, :]))
                        power = one(zm)
                        wide = (power[0].broadcast_to((P, m, N)), power[1].broadcast_to((P, m, N)))
                        cmul(many(table, m, 2 * m), many(table, 0, m), wide, m)
                        m *= 2
                wide = tuple(part.broadcast_to((P, NA_POW, N)) for part in one(cc))
                cmul(many(coef, 0, NA_POW), many(za, 0, NA_POW), wide, NA_POW, negate_im=True)
                nc.vector.memset(sq[:, 0, 0:1], 0.0).then_inc(coef_done, 1)

                def total(layer, products):
                    then(nc.vector.tensor_reduce(ker[:, layer, :], products[:, :, :], AX_X, ALU.add))
                    tt(ker[:, layer, 0:1], ker[:, layer, 0:1], skip[:, layer:layer + 1], ALU.add).then_inc(ker_done, 1)

                def total_of_pool(n):
                    dve.wait_ge(pool_mul, n + 1)
                    then(*[nc.vector.tensor_reduce(ker[:, own + n, P // 2 * k:P // 2 * (k + 1)], prod2[k], AX_X, ALU.add)
                           for k in range(2)])
                    nc.vector.memset(sq[:, 0, 0:1], 0.0).then_inc(reduced, 1)

                own, done = NL - POOL_LAYERS, 0
                for layer in range(own):
                    then(multiply(nc.vector, lambda a: prod[:, 16 * a:16 * a + 16, :], layer))
                    total(layer, prod)
                    if layer % 2 == 1 and done < POOL_LAYERS - 1:
                        total_of_pool(done)
                        done += 1
                for n in range(POOL_LAYERS):
                    layer = own + n
                    if n >= done:
                        total_of_pool(n)
                    tt(ker[:, layer, 0:1], ker[:, layer, 0:1], skip[:, layer:layer + 1], ALU.add).then_inc(ker_done, 1)
                for g in range(NL // G):
                    dve.wait_ge(tr_done, G * (g + 1))
                    nc.vector.tensor_copy(chunk(ker_t, g), chunk(ps_t, g)).then_inc(trc_done, 1)
                for layer in range(NL):
                    dve.wait_ge(dft_done, layer + 1)
                    nc.vector.tensor_copy(kf[:, :, layer, :], ps_f[:, :, 0:P]).then_inc(kf_done, 1)

            @block.tensor
            def _(pe):
                for layer in range(NL):
                    pe.wait_ge(ker_done, layer + 1)
                    nc.tensor.transpose(ps_t[:, layer, :], ker[:, layer, :], core.ident[:, :]).then_inc(tr_done, 1)
                pe.wait_ge(raw_in, 16 * 7)
                for layer in range(NL):
                    pe.wait_ge(trc_done, layer // G + 1)
                    if layer:
                        pe.wait_ge(kf_done, layer)
                    for m, table in enumerate((COS, SIN, COS_NYQ)):
                        last = nc.tensor.matmul(ps_f[:, m, 0:P], dft[:, table, :], ker_t[:, layer, :],
                                                start=True, stop=True)
                    last.then_inc(dft_done, 1)


class Norm:

    def __init__(self, core, st, name=""):
        self.nc, self.core = core.nc, core
        self.stats = st.sb(name + "stats", [P, 2, G, 6])
        self.mv = st.sb(name + "mv", [P, 2, G, 2])
        self.ve, self.rs = st.sb(name + "ve", [P, 2, G]), st.sb(name + "rs", [P, 2, G])
        self.turn = st.sb(name + "turn", [P, 1])
        self.stats_done, self.var_done, self.rstd_done, self.centred = (
            st.sem(name + n) for n in ("stats_done", "var_done", "rstd_done", "centred"))

    def statistics(self, dve, x, n, k, free=True):
        nc = self.nc
        for g in range(G):
            last = nc.vector.bn_stats(self.stats[:, k, g, :], x[:, g, :])
        last.then_inc(self.stats_done, 1)
        dve.wait_ge(self.stats_done, 2 * n + 1)
        nc.vector.memset(self.turn[:, :], 0.0)
        for g in range(G):
            last = nc.vector.bn_aggr(self.mv[:, k, g, :], self.stats[:, k, g, :])
        last.then_inc(self.stats_done, 1)
        dve.wait_ge(self.stats_done, 2 * n + 2)
        nc.vector.tensor_scalar(self.ve[:, k, :], self.mv[:, k, :, 1], EPS, None, ALU.add).then_inc(self.var_done, 1)

    def rstd(self, pool, n, k):
        pool.wait_ge(self.var_done, n + 1)
        self.nc.gpsimd.tensor_tensor(self.rs[:, k, :], self.ve[:, k, :], self.core.neg_half[:, 0:G],
                                     ALU.pow).then_inc(self.rstd_done, 1)

    def scale(self, dve, out, x, n, k):
        dve.wait_ge(self.rstd_done, n + 1)
        for g in range(G):
            last = self.nc.vector.tensor_scalar(out[:, g, :], x[:, g, :], self.mv[:, k, g, 0:1],
                                                self.rs[:, k, g:g + 1], ALU.subtract, ALU.mult)
        return last

    def scale_affine(self, dve, out, x, gain, bias, n, k):
        dve.wait_ge(self.rstd_done, n + 1)
        for g in range(G):
            last = self.nc.vector.scalar_tensor_tensor(out=out[:, g, :], in0=x[:, g, :],
                                                       scalar=self.mv[:, k, g, 0:1], in1=gain,
                                                       op0=ALU.subtract, op1=ALU.mult)
        last.then_inc(self.centred, 1)
        dve.wait_ge(self.centred, n + 1)
        for g in range(G):
            last = self.nc.vector.scalar_tensor_tensor(out=out[:, g, :], in0=out[:, g, :],
                                                       scalar=self.rs[:, k, g:g + 1], in1=bias,
                                                       op0=ALU.mult, op1=ALU.add)
        return last


def steps(eng, lo, hi, body):
    assert lo % 2 == 0
    pairs = (hi - lo) // 2
    if pairs == 1:
        body(lo, 0)
        body(lo + 1, 1)
    elif pairs > 1:
        with eng.Fori(0, pairs) as pair:
            body(pair * 2 + lo, 0)
            body(pair * 2 + (lo + 1), 1)
    if (hi - lo) % 2:
        body(hi - 1, 0)


def stage_l0_attn(core, kf):
    nc, ins = core.nc, core.ins
    with Stage(core, "l0a") as st:
        u = st.sb("u", [P, B, P])
        dft = st.sb("dft", [P, 6, P])
        out_w = st.sb("out_w", [P, NL, 2 * P])
        out_b = st.sb("out_b", [P, NL, 2 * P])
        norm_rows = st.sb("norm_rows", [P, 2, DEPTH, P])
        norm_cols = st.sb("norm_cols", [P, 2, DEPTH])
        ff_b2 = st.sb("ff_b2", [P, DEPTH, P])
        ff_b1 = st.sb("ff_b1", [P, DEPTH, 8])
        weights_in, halved = st.sem("weights_in"), st.sem("halved")
        with nc.Block() as block:
            @block.sync
            def _(sp):
                sp.dma_start(dft[:, :, :], ins["dft"]).then_inc(weights_in, 16)
                sp.dma_start(out_w[:, :, :], ins["s4_out_wT"]).then_inc(weights_in, 16)
                sp.dma_start(out_b[:, :, :], ins["L0_attn_s4_out_b"].rearrange("i j n -> (i j) n").partition_broadcast(P)).then_inc(weights_in, 16)
                for k, name in enumerate(("L0_attn_ln1_w", "L0_attn_ln1_b")):
                    sp.dma_start(norm_rows[:, k, :, :], ins[name].partition_broadcast(P)).then_inc(weights_in, 16)
                sp.dma_start(ff_b2[:, :, :], ins["L0_attn_ff_b2"].partition_broadcast(P)).then_inc(weights_in, 16)
                with nc.allow_non_contiguous_dma("one value per feature"):
                    for k, name in enumerate(("L0_attn_ln2_w", "L0_attn_ln2_b")):
                        sp.dma_start(norm_cols[:, k, :], ins[name].rearrange("d n -> n d")).then_inc(weights_in, 16)
                    for d in range(DEPTH):
                        sp.dma_start(ff_b1[:, d, :], ins["L0_attn_ff_b1"][d].rearrange("(m n) -> n m", n=P)).then_inc(weights_in, 16)
                sp.wait_ge(weights_in, 16 * (8 + DEPTH))

            @block.vector
            def _(dve):
                dve.wait_ge(weights_in, 16 * (8 + DEPTH))
                nc.vector.tensor_scalar(out_w[:, :, 0:P], out_w[:, :, 0:P], 0.5, None, ALU.mult).then_inc(halved, 1)
                nc.vector.tensor_scalar(out_b[:, :, 0:P], out_b[:, :, 0:P], 0.5, None, ALU.mult).then_inc(halved, 1)
                dve.wait_ge(halved, 2)

        s4 = S4Pair(core, st, u, dft, kf, out_w, out_b, norm_rows)
        ff = FeedForward(core, st, u, norm_cols, ff_b1, ff_b2)
        for d in range(DEPTH):
            s4.run(d)
            ff.run(d)


class S4Pair:
    STEPS = 2 * NCH

    def __init__(self, core, st, u, dft, kf, out_w, out_b, norm_rows):
        self.core, self.u, self.dft, self.kf = core, u, dft, kf
        self.out_w, self.out_b, self.norm_rows = out_w, out_b, norm_rows
        self.st = st
        self.norm = Norm(core, st, "s4")
        self.prods = st.sb("prods", [P, 2, 4, G, P])
        self.spec = st.sb("spec", [P, 2, 2, G, P])
        self.gel = st.sb("gel", [P, 2, G, P])
        self.z = st.sb("z", [P, 2, G, 2 * P])
        self.th = st.sb("th", [P, 2, G, P])
        (self.normed, self.dft_done, self.prod_done, self.spec_done, self.inv_done, self.gelu_done, self.proj_done,
         self.z_done, self.tanh_done, self.glu_done) = (st.sem(n) for n in (
             "normed", "dft_done", "prod_done", "spec_done", "inv_done", "gelu_done", "proj_done",
             "z_done", "tanh_done", "glu_done"))

    def run(self, d):
        nc, core, norm = self.core.nc, self.core, self.norm
        u, dft, kf = self.u, self.dft, self.kf
        N, base, nbase = self.STEPS, self.STEPS * d, NCH * d
        tt = nc.vector.tensor_tensor
        with nc.psum_tensor(f"s4_ri{d}", [P, 2, 2, 512], F32) as ps_ri, \
                nc.psum_tensor(f"s4_y{d}", [P, 2, 512], F32) as ps_y, \
                nc.psum_tensor(f"s4_z{d}", [P, 2, 512], F32) as ps_z, nc.Block() as block:

            @block.tensor
            def _(pe):
                def forward(i, k):
                    if isinstance(i, int) and i < NCH:
                        pe.wait_ge(self.normed, nbase + i + 1)
                    else:
                        pe.wait_ge(self.glu_done, base + i - NCH + 1)
                    if not (isinstance(i, int) and i < 2):
                        pe.wait_ge(self.prod_done, base + i - 1)
                    for m, table in enumerate((COS, SIN_NYQ)):
                        last = nc.tensor.matmul(ps_ri[:, k, m, :], dft[:, table, :], flat(chunk(u, i & (NCH - 1))),
                                                start=True, stop=True)
                    last.then_inc(self.dft_done, 1)

                def inverse(i, k):
                    pe.wait_ge(self.spec_done, base + i + 1)
                    if not (isinstance(i, int) and i < 2):
                        pe.wait_ge(self.gelu_done, base + i - 1)
                    for g in range(G):
                        for m, table in enumerate((INV_COS, INV_SIN)):
                            last = nc.tensor.matmul(ps_y[:, k, P * g:P * g + P], self.spec[:, k, m, g, :],
                                                    dft[:, table, :], start=(m == 0), stop=(m == 1))
                    last.then_inc(self.inv_done, 1)

                def project(i, k):
                    pe.wait_ge(self.gelu_done, base + i + 1)
                    if not (isinstance(i, int) and i < 1):
                        pe.wait_ge(self.z_done, base + i)
                    layer = (i & (N - 1)) // NCH + 2 * d
                    for g in range(G):
                        last = nc.tensor.matmul(ps_z[:, g // 2, 2 * P * (g % 2):2 * P * (g % 2) + 2 * P],
                                                self.gel[:, k, g, :], self.out_w[:, bass.ds(layer, 1), :], start=True, stop=True)
                    last.then_inc(self.proj_done, 1)

                def body(i, k):
                    forward(i, k)
                    inverse(i - 1, 1 - k)
                    project(i - 2, k)

                forward(0, 0)
                forward(1, 1)
                inverse(0, 0)
                for i in range(2, NCH):
                    body(i, i % 2)
                steps(pe, NCH, N, body)
                inverse(N - 1, 1)
                project(N - 2, 0)
                project(N - 1, 1)

            @block.vector
            def _(dve):
                def statistics(i):
                    norm.statistics(dve, chunk(core.x, i), nbase + i, i % 2)

                def scale(i):
                    norm.scale_affine(dve, chunk(u, i), chunk(core.x, i), self.norm_rows[:, 0, d, :],
                                      self.norm_rows[:, 1, d, :], nbase + i, i % 2).then_inc(self.normed, 1)

                def product(i, k):
                    dve.wait_ge(self.dft_done, base + i + 1)
                    if not (isinstance(i, int) and i < 2):
                        dve.wait_ge(self.spec_done, base + i - 1)
                    layer = (i & (N - 1)) // NCH + 2 * d
                    part = lambda m: kf[:, m, bass.ds(layer, 1), :].broadcast_to((P, G, P))
                    four = lambda m: ps_ri[:, k, m, :].rearrange("p (g n) -> p g n", n=P)
                    for n, (m, c) in enumerate(((0, 0), (1, 1), (0, 1), (1, 2))):
                        last = tt(self.prods[:, k, n, :, :], four(m), part(c), ALU.mult)
                    last.then_inc(self.prod_done, 1)

                def add_bias(i, k):
                    dve.wait_ge(self.proj_done, base + i + 1)
                    if not (isinstance(i, int) and i < 2):
                        dve.wait_ge(self.tanh_done, base + i - 1)
                    layer = (i & (N - 1)) // NCH + 2 * d
                    tt(self.z[:, k, :, :], ps_z[:, :, :].rearrange("p a (b n) -> p (a b) n", n=2 * P),
                       self.out_b[:, bass.ds(layer, 1), :].broadcast_to((P, G, 2 * P)), ALU.add).then_inc(self.z_done, 1)

                def gate(i, k):
                    dve.wait_ge(self.tanh_done, base + i + 1)
                    nc.vector.scalar_tensor_tensor(out=chunk(u, i & (NCH - 1)), in0=self.th[:, k, :, :], scalar=1.0,
                                                   in1=self.z[:, k, :, 0:P], op0=ALU.add,
                                                   op1=ALU.mult).then_inc(self.glu_done, 1)

                def body(i, k):
                    product(i, k)
                    gate(i - 3, 1 - k)
                    add_bias(i - 2, k)

                statistics(0)
                scale(0)
                statistics(1)
                for i in range(NCH):
                    if i + 1 < NCH:
                        scale(i + 1)
                    if i + 2 < NCH:
                        statistics(i + 2)
                    product(i, i % 2)
                    if i >= 3:
                        gate(i - 3, (i - 3) % 2)
                    if i >= 2:
                        add_bias(i - 2, i % 2)
                steps(dve, NCH, N, body)
                gate(N - 3, 1)
                add_bias(N - 2, 0)
                gate(N - 2, 0)
                add_bias(N - 1, 1)
                gate(N - 1, 1)
                dve.wait_ge(self.glu_done, base + N)

            @block.gpsimd
            def _(pool):
                def total(i, k):
                    pool.wait_ge(self.prod_done, base + i + 1)
                    if not (isinstance(i, int) and i < 2):
                        pool.wait_ge(self.inv_done, base + i - 1)
                    nc.gpsimd.tensor_tensor(self.spec[:, k, 0, :, :], self.prods[:, k, 0, :, :],
                                            self.prods[:, k, 1, :, :], ALU.subtract)
                    nc.gpsimd.tensor_tensor(self.spec[:, k, 1, :, :], self.prods[:, k, 2, :, :],
                                            self.prods[:, k, 3, :, :], ALU.add).then_inc(self.spec_done, 1)

                norm.rstd(pool, nbase, 0)
                norm.rstd(pool, nbase + 1, 1)
                for i in range(NCH):
                    if i + 2 < NCH:
                        norm.rstd(pool, nbase + i + 2, i % 2)
                    total(i, i % 2)
                steps(pool, NCH, N, total)

            @block.scalar
            def _(act):
                def gelu(i, k):
                    act.wait_ge(self.inv_done, base + i + 1)
                    if not (isinstance(i, int) and i < 2):
                        act.wait_ge(self.proj_done, base + i - 1)
                    nc.scalar.activation(flat(self.gel[:, k, :, :]), ps_y[:, k, :],
                                         ACT.Gelu_apprx_tanh).then_inc(self.gelu_done, 1)

                def tanh(i, k):
                    act.wait_ge(self.z_done, base + i + 1)
                    if not (isinstance(i, int) and i < 2):
                        act.wait_ge(self.glu_done, base + i - 1)
                    nc.scalar.activation(self.th[:, k, :, :], self.z[:, k, :, P:2 * P], ACT.Tanh,
                                         scale=0.5).then_inc(self.tanh_done, 1)

                def body(i, k):
                    gelu(i, k)
                    tanh(i - 1, 1 - k)

                gelu(0, 0)
                gelu(1, 1)
                tanh(0, 0)
                steps(act, 2, N, body)
                tanh(N - 1, 1)


class FeedForward:

    def __init__(self, core, st, u, norm_cols, b1, b2):
        self.core, self.u, self.norm_cols, self.b1, self.b2 = core, u, norm_cols, b1, b2
        self.norm = Norm(core, st, "ff")
        self.w1 = st.sb("w1", [P, 8 * P])
        self.w2 = st.sb("w2", [P, 4, P])
        self.xn = st.sb("xn", [P, 2, G, P])
        self.xt = st.sb("xt", [P, 2, W])
        self.sg = st.sb("sg", [P, 2, W])
        self.mid = st.sb("mid", [P, 2, 4, W])
        (self.w_in, self.xadd_done, self.normed, self.tr_done, self.xt_done, self.up_done, self.silu_done,
         self.mid_done, self.b2_done, self.down_done, self.res_done) = (st.sem("ff_" + n) for n in (
             "w_in", "xadd_done", "normed", "tr_done", "xt_done", "up_done", "silu_done", "mid_done", "b2_done",
             "down_done", "res_done"))

    def run(self, d):
        nc, core, norm = self.core.nc, self.core, self.norm
        N, base = NCH, NCH * d
        with nc.psum_tensor(f"ff_t{d}", [P, 2, 512], F32) as ps_t, \
                nc.psum_tensor(f"ff_u{d}", [P, 2, 2, 512], F32) as ps_u, \
                nc.psum_tensor(f"ff_o{d}", [P, 2, 512], F32) as ps_o, nc.Block() as block:

            @block.sync
            def _(sp):
                sp.dma_start(self.w1[:, :], core.ins["ff_w1T"][d]).then_inc(self.w_in, 16)
                sp.dma_start(self.w2[:, :, :], core.ins["ff_w2T"][d]).then_inc(self.w_in, 16)

            @block.gpsimd
            def _(pool):
                def add_s4(i):
                    nc.gpsimd.tensor_tensor(chunk(core.x, i), chunk(core.x, i), chunk(self.u, i),
                                            ALU.add).then_inc(self.xadd_done, 1)

                def add_b2(i):
                    pool.wait_ge(self.normed, base + i + 1)
                    nc.gpsimd.tensor_tensor(chunk(core.x, i), chunk(core.x, i),
                                            self.b2[:, bass.ds(d, 1), :].broadcast_to((P, G, P)),
                                            ALU.add).then_inc(self.b2_done, 1)

                for i in range(N + 1):
                    if i < N:
                        add_s4(i)
                        norm.rstd(pool, base + i, i % 2)
                    if i >= 1:
                        add_b2(i - 1)

            @block.vector
            def _(dve):
                def statistics(i):
                    dve.wait_ge(self.xadd_done, base + i + 1)
                    norm.statistics(dve, chunk(core.x, i), base + i, i % 2)

                def scale(i):
                    if base + i >= 2:
                        dve.wait_ge(self.tr_done, base + i - 1)
                    norm.scale(dve, self.xn[:, i % 2, :, :], chunk(core.x, i), base + i, i % 2).then_inc(self.normed, 1)

                def gate(i, m):
                    q, t = 4 * (base + i) + m, m % 2
                    dve.wait_ge(self.silu_done, q + 1)
                    if m == 0 and base + i >= 2:
                        dve.wait_ge(self.down_done, base + i - 1)
                    nc.vector.scalar_tensor_tensor(out=self.mid[:, i % 2, m, :], in0=ps_u[:, t, 0, :],
                                                   scalar=self.b1[:, d, m:m + 1], in1=self.sg[:, t, :],
                                                   op0=ALU.add, op1=ALU.mult).then_inc(self.mid_done, 1)

                def residual(i):
                    dve.wait_ge(self.down_done, base + i + 1)
                    dve.wait_ge(self.b2_done, base + i + 1)
                    nc.vector.tensor_tensor(chunk(core.x, i), ps_o[:, i % 2, :].rearrange("p (g n) -> p g n", n=P),
                                            chunk(core.x, i), ALU.add).then_inc(self.res_done, 1)

                statistics(0)
                scale(0)
                statistics(1)
                for i in range(N + 1):
                    if i + 1 < N:
                        scale(i + 1)
                    if i + 2 < N:
                        statistics(i + 2)
                    if i < N:
                        for m in range(4):
                            gate(i, m)
                            if m == 0 and i >= 1:
                                residual(i - 1)
                residual(N - 1)
                dve.wait_ge(self.res_done, base + N)

            @block.scalar
            def _(act):
                def copy_t(i):
                    act.wait_ge(self.tr_done, base + i + 1)
                    if base + i >= 2:
                        act.wait_ge(self.up_done, 4 * (base + i - 1))
                    nc.scalar.activation(self.xt[:, i % 2, :], ps_t[:, i % 2, :], ACT.Identity,
                                         bias=self.norm_cols[:, 1, d:d + 1],
                                         scale=self.norm_cols[:, 0, d:d + 1]).then_inc(self.xt_done, 1)

                def silu(i, m):
                    q, t = 4 * (base + i) + m, m % 2
                    act.wait_ge(self.up_done, q + 1)
                    if q >= 2:
                        act.wait_ge(self.mid_done, q - 1)
                    nc.scalar.activation(self.sg[:, t, :], ps_u[:, t, 1, :], ACT.Silu,
                                         bias=self.b1[:, d, 4 + m:5 + m]).then_inc(self.silu_done, 1)

                copy_t(0)
                for i in range(N):
                    if i + 1 < N:
                        copy_t(i + 1)
                    for m in range(4):
                        silu(i, m)

            @block.tensor
            def _(pe):
                def transpose(i):
                    pe.wait_ge(self.normed, base + i + 1)
                    if base + i >= 2:
                        pe.wait_ge(self.xt_done, base + i - 1)
                    for g in range(G):
                        last = nc.tensor.transpose(ps_t[:, i % 2, P * g:P * g + P], self.xn[:, i % 2, g, :],
                                                   core.ident[:, :])
                    last.then_inc(self.tr_done, 1)

                def up(i, m):
                    q, t = 4 * (base + i) + m, m % 2
                    if m == 0:
                        pe.wait_ge(self.xt_done, base + i + 1)
                    if q >= 2:
                        pe.wait_ge(self.mid_done, q - 1)
                    for part in range(2):
                        col = P * (4 * part + m)
                        last = nc.tensor.matmul(ps_u[:, t, part, :], self.w1[:, col:col + P], self.xt[:, i % 2, :],
                                                start=True, stop=True)
                    last.then_inc(self.up_done, 1)

                def down(i):
                    pe.wait_ge(self.mid_done, 4 * (base + i) + 4)
                    if base + i >= 2:
                        pe.wait_ge(self.res_done, base + i - 1)
                    for g in range(G):
                        for m in range(4):
                            last = nc.tensor.matmul(ps_o[:, i % 2, P * g:P * g + P],
                                                    self.mid[:, i % 2, m, P * g:P * g + P], self.w2[:, m, :],
                                                    start=(m == 0), stop=(m == 3))
                    last.then_inc(self.down_done, 1)

                pe.wait_ge(self.w_in, 32 * (d + 1))
                transpose(0)
                for i in range(N):
                    if i + 1 < N:
                        transpose(i + 1)
                    up(i, 0)
                    up(i, 1)
                    if i >= 1:
                        down(i - 1)
                    up(i, 2)
                    up(i, 3)
                down(N - 1)


UNIT = HEADS // 2


def bank4(ap):
    return ap.rearrange("p (g n) -> p g n", n=P)


class Attention:

    def __init__(self, core, name, src, wq, wk, wv, softmax, scale, wo=None, bq=None, bk=None, bv=None, bo=None,
                 affine=None, wg=None, bg=None, dst=None, sums=None, norm=None):
        self.norm_to, self.norm_rows = norm or (None, ())
        self.dst, self.sums = dst, sums
        self.core, self.name, self.src = core, name, src
        self.w_names = [n for n in (wq, wk, wv, wo, wg) if n]
        self.wq, self.wk, self.wv, self.wo, self.wg = wq, wk, wv, wo, wg
        self.softmax, self.att_scale = softmax, scale
        self.bq, self.bk, self.bv, self.bo, self.bg, self.affine = bq, bk, bv, bo, bg, affine

    def run(self):
        core, nc, ins = self.core, self.core.nc, self.core.ins
        softmax, src = self.softmax, self.src
        NU = 2 * B
        with Stage(core, self.name) as st:
            sem = {n: st.sem(n) for n in (
                "w_in", "x_tr", "xt", "q_mm", "q", "k_mm", "k", "v_mm", "v", "spread", "score", "score_read",
                "max", "exp", "p_tr", "pt", "pv", "rz", "o", "o_tr", "ot", "out_mm", "out", "bo",
                "g_mm", "gate", "ones", "weighted", "summed")}
            w = {n: st.sb("w" + str(i), [P, P]) for i, n in enumerate(self.w_names)}
            head_mask = st.sb("head_mask", [P, HEADS])
            cols = st.sb("cols", [P, 4])
            rows = st.sb("rows", [P, 3, P])
            xt, qt, kt = (st.sb(n, [P, 2, W]) for n in ("xt", "qt", "kt"))
            v = st.sb("v", [P, 2, G, HEADS, HD + 1])
            spread = st.sb("spread", [P, 2, HEADS, P])
            pr = st.sb("pr", [P, 2, UNIT, P])
            o, ot = st.sb("o", [P, 2, G, P]), st.sb("ot", [P, 2, W])
            if softmax:
                mx, rz = st.sb("mx", [P, 2, UNIT]), st.sb("rz", [P, 2, HEADS])
                shifted, pt = st.sb("shifted", [P, 2, UNIT, P]), st.sb("pt", [P, 2, UNIT, P])
            else:
                decay = st.sb("decay", [P, HEADS, P])
                gate = st.sb("gate", [P, 2, G, P])
                gpre = st.sb("gpre", [P, G, P])
            if self.sums:
                weighted = st.sb("weighted", [P, 2, UNIT, P])
            ps_s, ps_o, ps_m = st.ps("ps_s", [P, 2, 512]), st.ps("ps_o", [P, 2, 512]), st.ps("ps_m", [P, 2, 512])
            ps_p = st.ps("ps_p", [P, 2, 512])
            col_names = [n for n in (self.bq, self.bk) if n] + (list(self.affine) if self.affine else [])
            row_names = [n for n in (self.bv, self.bo, self.bg) if n]
            row = {n: rows[:, i:i + 1, :] for i, n in enumerate(row_names)}
            col = {n: cols[:, i:i + 1] for i, n in enumerate(col_names)}
            loads = len(w) + 1 + len(col_names) + len(row_names) + (not softmax)
            values = HD + 1 if softmax else HD
            stationary, moving = (qt, kt) if softmax else (kt, qt)

            if self.norm_to is not None:
                norm, normed = Norm(core, st, "n"), st.sem("normed")
                norm_rows = st.sb("norm_rows", [P, 2, P])
                stream = core.x if self.wo else core.h
                loads += len(self.norm_rows)

            with nc.Block() as block:
                @block.sync
                def _(sp):
                    for i, n in enumerate(self.norm_rows):
                        sp.dma_start(norm_rows[:, i, :], ins[n].partition_broadcast(P)).then_inc(sem["w_in"], 16)
                    for n in self.w_names:
                        sp.dma_start(w[n][:, :], ins[n]).then_inc(sem["w_in"], 16)
                    sp.dma_start(head_mask[:, :], ins["head_mask"]).then_inc(sem["w_in"], 16)
                    with nc.allow_non_contiguous_dma("one value per feature"):
                        for n in col_names:
                            sp.dma_start(col[n], ins[n].unsqueeze(1)).then_inc(sem["w_in"], 16)
                    for n in row_names:
                        sp.dma_start(row[n], ins[n].unsqueeze(0).partition_broadcast(P)).then_inc(sem["w_in"], 16)
                    if not softmax:
                        sp.dma_start(decay[:, :, :], ins["decay"]).then_inc(sem["w_in"], 16)
                    sp.wait_ge(sem["w_in"], 16 * loads)

                @block.tensor
                def _(pe):
                    mm, tr = nc.tensor.matmul, nc.tensor.transpose

                    def transpose_x(c):
                        if c >= 1:
                            pe.wait_ge(sem["k"], c)
                        if self.wo and c >= 3:
                            pe.wait_ge(sem["ot"], c - 2)
                        for g in range(G):
                            last = tr(ps_m[:, 0, P * g:P * g + P], src[:, G * c + g, :], core.ident[:, :])
                        last.then_inc(sem["x_tr"], 1)

                    def project_q(c):
                        pe.wait_ge(sem["xt"], c + 1)
                        if c == 0:
                            pe.wait_ge(sem["w_in"], 16 * loads)
                        if c >= 1:
                            pe.wait_ge(sem["v"], c)
                        if self.wo and c >= 3:
                            pe.wait_ge(sem["out"], c - 2)
                        mm(ps_m[:, 1, :], w[self.wq][:, :], xt[:, c % 2, :], start=True, stop=True).then_inc(sem["q_mm"], 1)

                    def project_k(c):
                        mm(ps_m[:, 0, :], w[self.wk][:, :], xt[:, c % 2, :], start=True, stop=True).then_inc(sem["k_mm"], 1)

                    def project_v(c):
                        pe.wait_ge(sem["q"], c + 1)
                        for g in range(G):
                            last = mm(ps_m[:, 1, P * g:P * g + P], xt[:, c % 2, P * g:P * g + P], w[self.wv][:, :],
                                      start=True, stop=True)
                        last.then_inc(sem["v_mm"], 1)

                    def project_gate(c):
                        if c >= 2:
                            pe.wait_ge(sem["gate"], c - 1)
                        for g in range(G):
                            last = mm(ps_p[:, c % 2, P * g:P * g + P], xt[:, c % 2, P * g:P * g + P],
                                      w[self.wg][:, :], start=True, stop=True)
                        last.then_inc(sem["g_mm"], 1)

                    def scores(n):
                        b, half = n // 2, n % 2
                        pe.wait_ge(sem["spread"], b + 1)
                        if n >= 2:
                            pe.wait_ge(sem["score_read"], n - 1)
                        if half == 0:
                            pe.wait_ge(sem["q" if softmax else "k"], b // G + 1)
                        mm(ps_s[:, half, :], stationary[:, b // G % 2, P * (b % G):P * (b % G) + P],
                           spread[:, b % 2, UNIT * half:UNIT * half + UNIT, :], start=True, stop=True).then_inc(sem["score"], 1)

                    def transpose_p(n):
                        pe.wait_ge(sem["exp"], n + 1)
                        if n >= 2:
                            pe.wait_ge(sem["pt"], n - 1)
                        for j in range(UNIT):
                            last = tr(ps_p[:, n % 2, P * j:P * j + P], pr[:, n % 2, j, :], core.ident[:, :])
                        last.then_inc(sem["p_tr"], 1)

                    def value_product(n):
                        b, half = n // 2, n % 2
                        pe.wait_ge(sem["pt" if softmax else "score_read"], n + 1)
                        pe.wait_ge(sem["v"], b // G + 1)
                        if half == 0 and b >= 2:
                            pe.wait_ge(sem["o"], b - 1)
                        left = pt if softmax else pr
                        for j in range(UNIT):
                            head = UNIT * half + j
                            last = mm(ps_o[:, b % 2, values * head:values * head + values], left[:, n % 2, j, :],
                                      v[:, b // G % 2, b % G, head, 0:values], start=True, stop=True)
                        last.then_inc(sem["pv"], 1)

                    def transpose_o(c):
                        pe.wait_ge(sem["o"], G * (c + 1))
                        pe.wait_ge(sem["k"], min(c + 3, NCH))
                        if c >= 1:
                            pe.wait_ge(sem["ot"], c)
                        for g in range(G):
                            last = tr(ps_m[:, 0, P * g:P * g + P], o[:, c % 2, g, :], core.ident[:, :])
                        last.then_inc(sem["o_tr"], 1)

                    def project_out(c):
                        pe.wait_ge(sem["ot"], c + 1)
                        pe.wait_ge(sem["v"], min(c + 3, NCH))
                        if c >= 1:
                            pe.wait_ge(sem["out"], c)
                        for g in range(G):
                            last = mm(ps_m[:, 1, P * g:P * g + P], ot[:, c % 2, P * g:P * g + P], w[self.wo][:, :],
                                      start=True, stop=True)
                        last.then_inc(sem["out_mm"], 1)

                    def ahead(c, k):
                        if c < NCH:
                            if k == 0:
                                transpose_x(c)
                            elif k == 1:
                                project_q(c)
                            elif k == 2:
                                project_k(c)
                            elif k == 3:
                                project_v(c)
                                if self.wg:
                                    project_gate(c)

                    for k in range(4):
                        ahead(0, k)
                    lag = 3 if softmax else 2
                    for n in range(NU + lag):
                        c, k = n // (2 * G), n % (2 * G)
                        if n < NU:
                            scores(n)
                            ahead(c + 1, k)
                        if softmax and 0 <= n - 2 < NU:
                            transpose_p(n - 2)
                        if 0 <= n - lag < NU:
                            value_product(n - lag)
                        if self.wo and k == 5 and 1 <= c:
                            transpose_o(c - 1)
                        if self.wo and k == 6 and 1 <= c:
                            project_out(c - 1)
                    if self.wo:
                        transpose_o(NCH - 1)
                        project_out(NCH - 1)

                @block.scalar
                def _(act):
                    act.wait_ge(sem["w_in"], 16 * loads)

                    def copy_xt(c):
                        act.wait_ge(sem["x_tr"], c + 1)
                        if c >= 2:
                            act.wait_ge(sem["v_mm"], c - 1)
                            if self.wg:
                                act.wait_ge(sem["g_mm"], c - 1)
                        if self.affine:
                            nc.scalar.activation(xt[:, c % 2, :], ps_m[:, 0, :], ACT.Identity, bias=col[self.affine[1]],
                                                 scale=col[self.affine[0]]).then_inc(sem["xt"], 1)
                        else:
                            nc.scalar.copy(xt[:, c % 2, :], ps_m[:, 0, :]).then_inc(sem["xt"], 1)

                    def copy_q(c, what, bank, bias, to, is_stationary):
                        act.wait_ge(sem[what + "_mm"], c + 1)
                        if c >= 2:
                            if is_stationary:
                                act.wait_ge(sem["score"], 2 * G * (c - 1))
                            else:
                                act.wait_ge(sem["spread"], G * (c - 1))
                        if bias:
                            nc.scalar.activation(to[:, c % 2, :], ps_m[:, bank, :], ACT.Identity,
                                                 bias=col[bias]).then_inc(sem[what], 1)
                        else:
                            nc.scalar.copy(to[:, c % 2, :], ps_m[:, bank, :]).then_inc(sem[what], 1)

                    def exponentials(n):
                        act.wait_ge(sem["score_read"], n + 1)
                        if n >= 2:
                            act.wait_ge(sem["p_tr"], n - 1)
                            if self.sums:
                                act.wait_ge(sem["weighted"], n - 1)
                        nc.scalar.activation(pr[:, n % 2, :, :], shifted[:, n % 2, :, :], ACT.Exp,
                                             scale=self.att_scale).then_inc(sem["exp"], 1)

                    def copy_pt(n):
                        act.wait_ge(sem["p_tr"], n + 1)
                        if n >= 2:
                            act.wait_ge(sem["pv"], n - 1)
                        nc.scalar.copy(flat(pt[:, n % 2, :, :]), ps_p[:, n % 2, :]).then_inc(sem["pt"], 1)

                    def copy_ot(c):
                        act.wait_ge(sem["o_tr"], c + 1)
                        if c >= 2:
                            act.wait_ge(sem["out_mm"], c - 1)
                        nc.scalar.copy(ot[:, c % 2, :], ps_m[:, 0, :]).then_inc(sem["ot"], 1)

                    def ahead(c, k):
                        if c < NCH:
                            if k == 0:
                                copy_xt(c)
                            elif k == 1:
                                copy_q(c, "q", 1, self.bq, qt, softmax)
                            elif k == 2:
                                copy_q(c, "k", 0, self.bk, kt, not softmax)

                    for k in range(3):
                        ahead(0, k)
                    for n in range(NU + 3):
                        c, k = n // (2 * G), n % (2 * G)
                        if n < NU:
                            ahead(c + 1, k)
                        if softmax and 0 <= n - 1 < NU:
                            exponentials(n - 1)
                        if softmax and 0 <= n - 2 < NU:
                            copy_pt(n - 2)
                        if self.wo and k == 5 and 1 <= c:
                            copy_ot(c - 1)
                        if self.wg and k == 4 and n < NU:
                            act.wait_ge(sem["gate"], c + 1)
                            if c >= 2:
                                act.wait_ge(sem["o"], G * (c - 1))
                            nc.scalar.activation(gate[:, c % 2, :, :], gpre[:, :, :], ACT.Silu).then_inc(sem["rz"], 1)
                    if self.wo:
                        copy_ot(NCH - 1)

                @block.gpsimd
                def _(pool):
                    def weigh(n):
                        pool.wait_ge(sem["exp"], n + 1)
                        if n >= 2:
                            pool.wait_ge(sem["summed"], n - 1)
                        nc.gpsimd.tensor_tensor(weighted[:, n % 2, :, :], pr[:, n % 2, :, :], shifted[:, n % 2, :, :],
                                                ALU.mult).then_inc(sem["weighted"], 1)

                    pool.wait_ge(sem["w_in"], 16 * loads)
                    for b in range(B):
                        c = b // G
                        if b % G == 0:
                            pool.wait_ge(sem["k" if softmax else "q"], c + 1)
                            if self.bo:
                                pool.wait_ge(sem["x_tr"], c + 1)
                                nc.gpsimd.tensor_tensor(chunk(core.x, c), chunk(core.x, c),
                                                        row[self.bo].broadcast_to((P, G, P)), ALU.add).then_inc(sem["bo"], 1)
                        if b >= 2:
                            pool.wait_ge(sem["score"], 2 * (b - 1))
                        one = moving[:, c % 2, P * (b % G):P * (b % G) + P].unsqueeze(1).broadcast_to((P, HEADS, P))
                        nc.gpsimd.tensor_tensor(spread[:, b % 2, :, :], one,
                                                head_mask[:, :].unsqueeze(2).broadcast_to((P, HEADS, P)),
                                                ALU.mult).then_inc(sem["spread"], 1)
                        if self.norm_to is not None and b % G == 2 and c >= 2:
                            norm.rstd(pool, c - 2, c % 2)
                        if self.sums and b >= 2:
                            weigh(2 * b - 4)
                            weigh(2 * b - 3)
                    if self.sums:
                        for n in range(2 * B - 4, 2 * B):
                            weigh(n)
                    if self.norm_to is not None:
                        norm.rstd(pool, NCH - 2, 0)
                        norm.rstd(pool, NCH - 1, 1)

                @block.vector
                def _(dve):
                    tt = nc.vector.tensor_tensor
                    if softmax:
                        nc.vector.memset(v[:, :, :, :, HD:HD + 1].rearrange("p a g h e -> p (a g h) e"), 1.0).then_inc(sem["ones"], 1)
                        dve.wait_ge(sem["ones"], 1)
                    dve.wait_ge(sem["w_in"], 16 * loads)

                    def copy_v(c):
                        dve.wait_ge(sem["v_mm"], c + 1)
                        if c >= 2:
                            dve.wait_ge(sem["pv"], 2 * G * (c - 1))
                        to = v[:, c % 2, :, :, 0:HD]
                        if self.bv:
                            for g in range(G):
                                last = tt(to[:, g], ps_m[:, 1, P * g:P * g + P].rearrange("p (h e) -> p h e", e=HD),
                                          row[self.bv].rearrange("p o (h e) -> p (o h) e", e=HD), ALU.add)
                            last.then_inc(sem["v"], 1)
                        else:
                            nc.vector.tensor_copy(to, ps_m[:, 1, :].rearrange("p (g h e) -> p g h e", g=G, e=HD)).then_inc(sem["v"], 1)

                    def bias_gate(c):
                        dve.wait_ge(sem["g_mm"], c + 1)
                        if c >= 1:
                            dve.wait_ge(sem["rz"], c)
                        tt(gpre[:, :, :], bank4(ps_p[:, c % 2, :]), row[self.bg].broadcast_to((P, G, P)),
                           ALU.add).then_inc(sem["gate"], 1)

                    def row_max(n):
                        dve.wait_ge(sem["score"], n + 1)
                        nc.vector.tensor_reduce(mx[:, n % 2, :], bank4(ps_s[:, n % 2, :]), AX_X, ALU.max).then_inc(sem["max"], 1)

                    def shift(n):
                        dve.wait_ge(sem["max"], n + 1)
                        if n >= 2:
                            dve.wait_ge(sem["exp"], n - 1)
                            if self.sums:
                                dve.wait_ge(sem["weighted"], n - 1)
                        tt(shifted[:, n % 2, :, :], bank4(ps_s[:, n % 2, :]),
                           mx[:, n % 2, :].unsqueeze(2).broadcast_to((P, UNIT, P)),
                           ALU.subtract).then_inc(sem["score_read"], 1)

                    def sum_weighted(n):
                        dve.wait_ge(sem["weighted"], n + 1)
                        nc.vector.tensor_reduce(self.sums[1][:, n // 2, UNIT * (n % 2):UNIT * (n % 2) + UNIT],
                                                weighted[:, n % 2, :, :], AX_X, ALU.add).then_inc(sem["summed"], 1)

                    def weigh(n):
                        dve.wait_ge(sem["score"], n + 1)
                        if n >= 2:
                            dve.wait_ge(sem["pv"], n - 1)
                        tt(pr[:, n % 2, :, :], bank4(ps_s[:, n % 2, :]),
                           decay[:, UNIT * (n % 2):UNIT * (n % 2) + UNIT, :], ALU.mult).then_inc(sem["score_read"], 1)

                    def normalise(b):
                        c, g = b // G, b % G
                        dve.wait_ge(sem["pv"], 2 * b + 2)
                        got = ps_o[:, b % 2, 0:HEADS * values].rearrange("p (h e) -> p h e", e=values)
                        to = (o[:, c % 2, g, :] if self.dst is None else self.dst[:, b, :]).rearrange("p (h e) -> p h e", e=HD)
                        if self.wo and c >= 2 and g == 0:
                            dve.wait_ge(sem["o_tr"], c - 1)
                        if self.sums:
                            nc.vector.tensor_copy(self.sums[0][:, b, :], got[:, :, HD])
                        if softmax:
                            nc.vector.reciprocal(rz[:, b % 2, :], got[:, :, HD]).then_inc(sem["rz"], 1)
                            dve.wait_ge(sem["rz"], b + 1)
                            tt(to, got[:, :, 0:HD], rz[:, b % 2, :].unsqueeze(2).broadcast_to((P, HEADS, HD)),
                               ALU.mult).then_inc(sem["o"], 1)
                        else:
                            if g == 0:
                                dve.wait_ge(sem["rz"], c + 1)
                            tt(to, got, gate[:, c % 2, g, :].rearrange("p (h e) -> p h e", e=HD), ALU.mult).then_inc(sem["o"], 1)
                            dve.wait_ge(sem["o"], b + 1)
                            tt(core.h[:, b, :], core.h[:, b, :], o[:, c % 2, g, :], ALU.add).then_inc(sem["out"], 1)

                    def residual(c):
                        dve.wait_ge(sem["out_mm"], c + 1)
                        if self.bo:
                            dve.wait_ge(sem["bo"], c + 1)
                        tt(chunk(core.x, c), bank4(ps_m[:, 1, :]), chunk(core.x, c), ALU.add).then_inc(sem["out"], 1)

                    def statistics(c):
                        dve.wait_ge(sem["out"], c + 1 if self.wo else G * (c + 1))
                        norm.statistics(dve, chunk(stream, c), c, c % 2)

                    def scale(c):
                        to = chunk(self.norm_to, c)
                        if self.norm_rows:
                            last = norm.scale_affine(dve, to, chunk(stream, c), norm_rows[:, 0, :], norm_rows[:, 1, :], c, c % 2)
                        else:
                            last = norm.scale(dve, to, chunk(stream, c), c, c % 2)
                        last.then_inc(normed, 1)

                    copy_v(0)
                    lag = 4 if softmax else 3
                    for n in range(NU + lag):
                        c, k = n // (2 * G), n % (2 * G)
                        if n < NU:
                            if softmax:
                                row_max(n)
                                shift(n)
                            else:
                                weigh(n)
                            if k == 3 and c + 1 < NCH:
                                copy_v(c + 1)
                            if self.wg and k == 3:
                                bias_gate(c)
                        m = n - lag
                        if self.sums and 0 <= n - 3 < NU:
                            sum_weighted(n - 3)
                        if m >= 0 and m % 2 == 1:
                            normalise(m // 2)
                        if self.wo and k == 7 and c >= 1:
                            residual(c - 1)
                        if self.norm_to is not None and n < NU and c >= 2:
                            if k == 0:
                                statistics(c - 2)
                            elif k == 6:
                                scale(c - 2)
                    if self.norm_to is not None:
                        statistics(NCH - 2)
                    if self.wo:
                        residual(NCH - 1)
                    if self.norm_to is not None:
                        statistics(NCH - 1)
                        scale(NCH - 2)
                        scale(NCH - 1)
                        dve.wait_ge(normed, NCH)
                    if self.wo:
                        dve.wait_ge(sem["out"], NCH)
                    elif softmax:
                        dve.wait_ge(sem["o"], B)
                        if self.sums:
                            dve.wait_ge(sem["summed"], NU)
                    else:
                        dve.wait_ge(sem["out"], B)


BS = 256
BT = BS // P
C_L0 = 2 * (B * P * 2 // 64)
assert C_L0 == BS


def blocks_of(experts, k):
    return (B * P * k + experts * (BS - 1)) // BS


SLOTS = max(64, blocks_of(8, 1), blocks_of(8, 2), blocks_of(16, 4)) * BS


def stage_transpose(core, name, src, dst):
    nc = core.nc
    with Stage(core, name) as st:
        ps = st.ps("ps", [P, 2, 512])
        turned, copied = st.sem("turned"), st.sem("copied")
        with nc.Block() as block:
            @block.tensor
            def _(pe):
                for c in range(NCH):
                    if c >= 2:
                        pe.wait_ge(copied, c - 1)
                    for g in range(G):
                        last = nc.tensor.transpose(ps[:, c % 2, P * g:P * g + P], src[:, G * c + g, :], core.ident[:, :])
                    last.then_inc(turned, 1)

            @block.scalar
            def _(act):
                for c in range(NCH):
                    act.wait_ge(turned, c + 1)
                    nc.scalar.copy(dst[:, W * c:W * c + W], ps[:, c % 2, :]).then_inc(copied, 1)
                act.wait_ge(copied, NCH)


class Routing:

    def __init__(self, core, st, experts, k):
        self.experts, self.k = experts, k
        self.gates = st.sb("gates", [P, B, k])
        self.to = st.sb("to", [P, B, k], I32)
        self.back = st.sb("back", [P, B, k], I32)
        self.blocks = blocks_of(experts, k)
        self.block_expert = st.sb("block_expert", [P, self.blocks], I32)


def stage_route(core, name, r, xt, x_rows, gate_w, gate_b=None, over="probs", gate="share", capacity=None,
                scatter=True):
    nc, ins, E, K = core.nc, core.ins, r.experts, r.k
    cols = B * E
    nbank = -(-cols // 512)
    width = min(cols, 512)
    with Stage(core, name) as st:
        w = st.sb("w", [P, E])
        bias = st.sb("bias", [P, 1, E])
        iota = st.sb("iota", [P, 1, P])
        tri, tri_bf = st.sb("tri", [P, P]), st.sb("tri_bf", [P, P], BF16)
        ones_bf = st.sb("ones_bf", [P, P], BF16)
        lg, pr = st.sb("lg", [P, B, E]), st.sb("pr", [P, B, E])
        mx, z, rz = (st.sb(n, [P, B]) for n in ("mx", "z", "rz"))
        top, idx = st.sb("top", [P, B, 8]), st.sb("idx", [P, B, 8], U32)
        idxf = st.sb("idxf", [P, B, K])
        topk, topm = st.sb("topk", [P, B, K]), st.sb("topm", [P, B, K])
        oh = st.sb("oh", [P, K, B, E], BF16)
        cnt, cum = st.sb("cnt", [P, B, E], BF16), st.sb("cum", [P, B + 1, E], BF16)
        pos, picked = st.sb("pos", [P, B, E]), st.sb("picked", [P, B, E])
        posk, slot = st.sb("posk", [P, B, K]), st.sb("slot", [P, B, K])
        drop, spare = st.sb("drop", [P, B, K]), st.sb("spare", [P, B, K])
        nb, end, start = st.sb("nb", [P, E]), st.sb("end", [P, E]), st.sb("start", [P, 1, E])
        past, which = st.sb("past", [P, r.blocks, E]), st.sb("which", [P, r.blocks])
        ps_l, ps_p = st.ps("ps_l", [P, nbank, 512]), st.ps("ps_p", [P, nbank, 512])
        sem = {n: st.sem(n) for n in ("in", "mm", "sub", "exp", "chain", "counted", "pos", "placed", "scattered",
                                      "keyed", "keyed_exp")}
        loads = 3 + (gate_b is not None)
        with nc.Block() as block:
            @block.sync
            def _(sp):
                sp.dma_start(w[:, :], gate_w).then_inc(sem["in"], 16)
                sp.dma_start(iota[:, :, :], ins["iota_row"].unsqueeze(1)).then_inc(sem["in"], 16)
                sp.dma_start(tri[:, :], ins["tri"]).then_inc(sem["in"], 16)
                if gate_b is not None:
                    sp.dma_start(bias[:, :, :], gate_b.unsqueeze(0).partition_broadcast(P)).then_inc(sem["in"], 16)
                sp.wait_ge(sem["in"], 16 * loads)

            @block.tensor
            def _(pe):
                pe.wait_ge(sem["in"], 16 * loads)
                per = width // E
                for b in range(B):
                    last = nc.tensor.matmul(ps_l[:, b // per, E * (b % per):E * (b % per) + E], xt[:, P * b:P * b + P],
                                            w[:, :], start=True, stop=True)
                last.then_inc(sem["mm"], 1)
                pe.wait_ge(sem["counted"], 1)
                cnt_f, cum_f = flat(cnt[:, :, :]), flat(cum[:, :, :])
                for n in range(nbank):
                    s = slice(width * n, width * n + width)
                    nc.tensor.matmul(ps_p[:, n, 0:width], tri_bf[:, :], cnt_f[:, s], start=True, stop=False)
                    nc.tensor.matmul(ps_p[:, n, 0:width], ones_bf[:, :], cum_f[:, s], start=False, stop=True)
                nc.tensor.matmul(ps_l[:, 0, 0:E], ones_bf[:, :], cum[:, B, :], start=True, stop=True).then_inc(sem["pos"], 1)

            @block.scalar
            def _(act):
                if over == "probs":
                    act.wait_ge(sem["sub"], 1)
                    nc.scalar.activation(flat(pr[:, :, :]), flat(lg[:, :, :]), ACT.Exp).then_inc(sem["exp"], 1)
                if gate == "softmax":
                    act.wait_ge(sem["keyed"], 1)
                    nc.scalar.activation(flat(topk[:, :, :]), flat(topm[:, :, :]), ACT.Exp).then_inc(sem["keyed_exp"], 1)

            @block.vector
            def _(dve):
                made = [0]

                def then(*i):
                    i[-1].then_inc(sem["chain"], 1)
                    made[0] += 1
                    dve.wait_ge(sem["chain"], made[0])

                tt, ts = nc.vector.tensor_tensor, nc.vector.tensor_scalar
                per_tile = lambda a: a[:, :].unsqueeze(2).broadcast_to((P, B, E))
                dve.wait_ge(sem["in"], 16 * loads)
                nc.vector.tensor_copy(tri_bf[:, :], tri[:, :])
                nc.vector.memset(ones_bf[:, :], 1.0)
                dve.wait_ge(sem["mm"], 1)
                got = ps_l[:, :, 0:width].rearrange("p n (b e) -> p (n b) e", e=E)
                if gate_b is not None:
                    then(tt(lg[:, :, :], got, bias[:, :, :].broadcast_to((P, B, E)), ALU.add))
                else:
                    then(nc.vector.tensor_copy(lg[:, :, :], got))
                if over == "probs":
                    then(nc.vector.tensor_reduce(mx[:, :], lg[:, :, :], AX_X, ALU.max))
                    tt(lg[:, :, :], lg[:, :, :], per_tile(mx), ALU.subtract).then_inc(sem["sub"], 1)
                    dve.wait_ge(sem["exp"], 1)
                    then(nc.vector.tensor_reduce(z[:, :], pr[:, :, :], AX_X, ALU.add))
                    then(nc.vector.reciprocal(rz[:, :], z[:, :]))
                    then(tt(pr[:, :, :], pr[:, :, :], per_tile(rz), ALU.mult))
                    values = pr
                else:
                    values = lg
                for b in range(B):
                    i = nc.vector.max(top[:, b, :], values[:, b, :])
                then(i)
                for b in range(B):
                    i = nc.vector.max_index(idx[:, b, :], top[:, b, :], values[:, b, :])
                then(i)
                nc.vector.tensor_copy(idxf[:, :, :], idx[:, :, 0:K])
                if gate == "value":
                    then(nc.vector.tensor_copy(r.gates[:, :, :], top[:, :, 0:K]))
                else:
                    if gate == "softmax":
                        tt(topm[:, :, :], top[:, :, 0:K], top[:, :, 0:1].broadcast_to((P, B, K)),
                           ALU.subtract).then_inc(sem["keyed"], 1)
                        dve.wait_ge(sem["keyed_exp"], 1)
                    else:
                        then(nc.vector.tensor_copy(topk[:, :, :], top[:, :, 0:K]))
                    then(nc.vector.tensor_reduce(z[:, :], topk[:, :, :], AX_X, ALU.add))
                    then(nc.vector.reciprocal(rz[:, :], z[:, :]))
                    then(tt(r.gates[:, :, :], topk[:, :, :], rz[:, :].unsqueeze(2).broadcast_to((P, B, K)), ALU.mult))
                for k in range(K):
                    i = tt(oh[:, k, :, :], iota[:, :, 0:E].broadcast_to((P, B, E)),
                           idxf[:, :, k:k + 1].broadcast_to((P, B, E)), ALU.is_equal)
                then(i)
                counts = oh[:, 0, :, :]
                for k in range(1, K):
                    then(tt(cnt[:, :, :], counts, oh[:, k, :, :], ALU.add))
                    counts = cnt[:, :, :]
                if K == 1:
                    then(nc.vector.tensor_copy(cnt[:, :, :], counts))
                then(nc.vector.memset(cum[:, 0, :], 0.0))
                for b in range(B):
                    if b == B - 1:
                        tt(cum[:, b + 1, :], cum[:, b, :], cnt[:, b, :], ALU.add).then_inc(sem["counted"], 1)
                    else:
                        then(tt(cum[:, b + 1, :], cum[:, b, :], cnt[:, b, :], ALU.add))
                dve.wait_ge(sem["pos"], 1)
                before = ps_p[:, :, 0:width].rearrange("p n (b e) -> p (n b) e", e=E)
                if capacity is None:
                    magic = float(1.5 * 2 ** 23)
                    then(ts(nb[:, :], ps_l[:, 0, 0:E], 1.0 / BS, (BS - 1.0) / BS - (BS - 1.0) / (2 * BS), ALU.mult, ALU.add))
                    then(ts(nb[:, :], nb[:, :], magic, None, ALU.add))
                    then(ts(nb[:, :], nb[:, :], magic, None, ALU.subtract))
                    then(nc.vector.tensor_tensor_scan(end[:, :], nb[:, :], nb[:, :], 0.0, ALU.add, ALU.bypass))
                    then(tt(start[:, 0, :], end[:, :], nb[:, :], ALU.subtract))
                    then(ts(start[:, 0, :], start[:, 0, :], float(BS), None, ALU.mult))
                    nblk = r.blocks
                    then(tt(past[:, :, :], end[:, :].unsqueeze(1).broadcast_to((P, nblk, E)),
                            iota[:, 0, 0:nblk].unsqueeze(2).broadcast_to((P, nblk, E)), ALU.is_le))
                    then(nc.vector.tensor_reduce(which[:, :], past[:, :, :], AX_X, ALU.add))
                    then(ts(which[:, :], which[:, :], float(E - 1), None, ALU.min))
                    then(nc.vector.tensor_copy(r.block_expert[:, :], which[:, :]))
                    then(tt(pos[:, :, :], before, start[:, :, :].broadcast_to((P, B, E)), ALU.add))
                else:
                    then(nc.vector.tensor_copy(pos[:, :, :], before))
                for k in range(K):
                    then(tt(picked[:, :, :], pos[:, :, :], oh[:, k, :, :], ALU.mult))
                    then(nc.vector.tensor_reduce(posk[:, :, k], picked[:, :, :], AX_X, ALU.add))
                if capacity is None:
                    nc.vector.tensor_copy(r.to[:, :, :], posk[:, :, :])
                    then(nc.vector.tensor_copy(r.back[:, :, :], posk[:, :, :]))
                else:
                    then(ts(drop[:, :, :], posk[:, :, :], float(capacity), None, ALU.is_ge))
                    then(ts(posk[:, :, :], posk[:, :, :], float(capacity - 1), None, ALU.min))
                    then(nc.vector.scalar_tensor_tensor(out=slot[:, :, :], in0=idxf[:, :, :], scalar=float(capacity),
                                                        in1=posk[:, :, :], op0=ALU.mult, op1=ALU.add))
                    then(nc.vector.tensor_copy(r.back[:, :, :], slot[:, :, :]))
                    then(ts(spare[:, :, :], slot[:, :, :], float(SLOTS), None, ALU.subtract))
                    then(tt(spare[:, :, :], spare[:, :, :], drop[:, :, :], ALU.mult))
                    then(tt(slot[:, :, :], slot[:, :, :], spare[:, :, :], ALU.subtract))
                    then(nc.vector.tensor_copy(r.to[:, :, :], slot[:, :, :]))
                    then(ts(drop[:, :, :], drop[:, :, :], -1.0, 1.0, ALU.mult, ALU.add))
                    then(tt(r.gates[:, :, :], r.gates[:, :, :], drop[:, :, :], ALU.mult))
                nc.vector.memset(mx[:, :], 0.0).then_inc(sem["placed"], 1)

            @block.gpsimd
            def _(pool):
                pool.wait_ge(sem["placed"], 1)
                pool.wait_ge(core.zeroed, 16)
                if scatter:
                    scatter_rows(core, pool, r, x_rows, sem["scattered"])


def scatter_rows(core, pool, r, x_rows, scattered):
    for b in range(B):
        for k in range(r.k):
            core.nc.gpsimd.indirect_dma_start(core.slots_in, bass.IndirectOffsetOnAxis(r.to[:, b, k:k + 1], 0),
                                              x_rows[:, b, :], None, bounds_check=SLOTS - 1,
                                              oob_is_err=False).then_inc(scattered, 16)
    pool.wait_ge(scattered, 16 * B * r.k)


def ring(eng, lo, hi, size, body):
    assert lo % size == 0
    turns = (hi - lo) // size
    if turns:
        with eng.Fori(0, turns) as turn:
            for k in range(size):
                body(turn * size + (lo + k), k)
    for i in range(lo + size * turns, hi):
        body(i, i % size)


RING = 6


def stage_experts(core, name, r, blocks, packed, rows_in, func, grouped, norm=False):
    nc, ins = core.nc, core.ins
    F = 2 * P + 1
    M = packed.shape[2] // F
    with Stage(core, name) as st:
        weights, xin = st.sb("weights", [P, RING, M * F]), st.sb("xin", [P, RING, BT, P])
        w1s = weights[:, :, 0:M * P]
        w2s = weights[:, :, M * P:2 * M * P].rearrange("p k (m d) -> p k m d", d=P)
        b1s = weights[:, :, 2 * M * P:M * F]
        n_rows = 3 if norm else 1
        rows = st.sb("rows", [P, RING, n_rows, P])
        xt, mid = st.sb("xt", [P, 2, BS]), st.sb("mid", [P, 2, M, BS])
        yout = st.sb("yout", [P, RING, BT, P])
        if norm:
            raw = st.sb("raw", [P, 2, BT, P])
            stats, mv = st.sb("stats", [P, 2, BT, 6]), st.sb("mv", [P, 2, BT, 2])
            carrier = st.sb("carrier", [P, 1])
            ve, rs = st.sb("ve", [P, 2, BT]), st.sb("rs", [P, 2, BT])
        ps_t, ps_o = st.ps("ps_t", [P, 2, 512]), st.ps("ps_o", [P, 2, 512])
        ps_u = st.ps("ps_u", [P, 2, 2, 512])
        loaded = [st.sem(f"loaded{k}") for k in range(RING)]
        stored = [st.sem(f"stored{k}") for k in range(RING)]
        x_tr, x_t, up, acted, down, y_done, var_done, rstd_done = (st.sem(n) for n in (
            "x_tr", "x_t", "up", "acted", "down", "y_done", "var_done", "rstd_done"))
        raw_done, stats_done, aggr_done, centred = (st.sem(n) for n in ("raw_done", "stats_done", "aggr_done", "centred"))
        N = blocks
        per = 3
        buf = core.slots_in.rearrange("(n p) d -> p n d", p=P)
        out = core.slots_out.rearrange("(n p) d -> p n d", p=P)

        def late(i, n):
            return not isinstance(i, int) or i >= n

        with nc.Block() as block:
            @block.sync
            def _(sp):
                def load(g, k):
                    if late(g, RING):
                        sp.wait_ge(y_done, g - RING + 1)
                    if grouped:
                        e = sp.value_load(r.block_expert[0:1, bass.ds(g, 1)], min_val=0, max_val=r.experts - 1)
                    else:
                        e = g
                    one = lambda t: t[bass.ds(e, 1)]
                    sp.dma_start(xin[:, k, :, :], buf[:, bass.ds(g * BT, BT), :]).then_inc(loaded[k], 16)
                    sp.dma_start(weights[:, k, :], one(packed).rearrange("e p f -> (e p) f")).then_inc(loaded[k], 16)
                    sp.dma_start(rows[:, k, :, :], one(rows_in).rearrange("e n d -> (e n) d").partition_broadcast(P)
                                 ).then_inc(loaded[k], 16)

                for g in range(RING):
                    load(g, g)
                ring(sp, RING, N, RING, load)

            @block.tensor
            def _(pe):
                def turn(g, k):
                    pe.wait_ge(loaded[k], 16 * per * (g // RING + 1))
                    if late(g, 2):
                        pe.wait_ge(x_t, g - 1)
                    for t in range(BT):
                        last = nc.tensor.transpose(ps_t[:, k % 2, P * t:P * t + P], xin[:, k, t, :], core.ident[:, :])
                    last.then_inc(x_tr, 1)

                def first(g, k):
                    pe.wait_ge(x_t, g + 1)
                    if late(g, 2):
                        pe.wait_ge(acted, g - 1)
                    for m in range(M):
                        last = nc.tensor.matmul(ps_u[:, k % 2, m // 2, BS * (m % 2):BS * (m % 2) + BS],
                                                w1s[:, k, P * m:P * m + P], xt[:, k % 2, :], start=True, stop=True)
                    last.then_inc(up, 1)

                def second(g, k):
                    pe.wait_ge(acted, g + 1)
                    if late(g, 2):
                        pe.wait_ge(y_done if not norm else raw_done, g - 1)
                    for t in range(BT):
                        for m in range(M):
                            last = nc.tensor.matmul(ps_o[:, k % 2, P * t:P * t + P], mid[:, k % 2, m, P * t:P * t + P],
                                                    w2s[:, k, m, :], start=(m == 0), stop=(m == M - 1))
                    last.then_inc(down, 1)

                def body(g, k):
                    turn(g + 1, (k + 1) % RING)
                    first(g, k)
                    second(g - 1, (k - 1) % RING)

                turn(0, 0)
                for g in range(RING):
                    turn(g + 1, (g + 1) % RING)
                    first(g, g)
                    if g:
                        second(g - 1, g - 1)
                ring(pe, RING, N - 1, RING, body)
                first(N - 1, (N - 1) % RING)
                second(N - 2, (N - 2) % RING)
                second(N - 1, (N - 1) % RING)

            @block.scalar
            def _(act):
                def copy_x(g, k):
                    act.wait_ge(x_tr, g + 1)
                    if late(g, 2):
                        act.wait_ge(up, g - 1)
                    nc.scalar.copy(xt[:, k % 2, :], ps_t[:, k % 2, 0:BS]).then_inc(x_t, 1)

                def activate(g, k):
                    act.wait_ge(up, g + 1)
                    if late(g, 2):
                        act.wait_ge(down, g - 1)
                    for m in range(M):
                        last = nc.scalar.activation(mid[:, k % 2, m, :], ps_u[:, k % 2, m // 2, BS * (m % 2):BS * (m % 2) + BS],
                                                    func, bias=b1s[:, k, m:m + 1])
                    last.then_inc(acted, 1)

                def body(g, k):
                    copy_x(g + 1, (k + 1) % RING)
                    activate(g, k)

                copy_x(0, 0)
                for g in range(RING):
                    body(g, g)
                ring(act, RING, N - 1, RING, body)
                activate(N - 1, (N - 1) % RING)

            @block.vector
            def _(dve):
                def output(g, k):
                    dve.wait_ge(down, g + 1)
                    if not norm and late(g, RING):
                        dve.wait_ge(stored[k], 16 * (g // RING))
                    got = ps_o[:, k % 2, 0:BS].rearrange("p (t d) -> p t d", d=P)
                    row = lambda n: rows[:, k, n:n + 1, :].broadcast_to((P, BT, P))
                    if not norm:
                        nc.vector.tensor_tensor(yout[:, k, :, :], got, row(0), ALU.add).then_inc(y_done, 1)
                        return
                    j = k % 2
                    if late(g, 2):
                        dve.wait_ge(y_done, g - 1)
                    nc.vector.tensor_tensor(raw[:, j, :, :], got, row(0), ALU.add).then_inc(raw_done, 1)
                    dve.wait_ge(raw_done, g + 1)
                    for t in range(BT):
                        last = nc.vector.bn_stats(stats[:, j, t, :], raw[:, j, t, :])
                    last.then_inc(stats_done, 1)
                    dve.wait_ge(stats_done, g + 1)
                    nc.vector.memset(carrier[:, :], 0.0)
                    for t in range(BT):
                        last = nc.vector.bn_aggr(mv[:, j, t, :], stats[:, j, t, :])
                    last.then_inc(aggr_done, 1)
                    dve.wait_ge(aggr_done, g + 1)
                    nc.vector.tensor_scalar(ve[:, j, :], mv[:, j, :, 1], EPS, None, ALU.add).then_inc(var_done, 1)

                def normalise(g, k):
                    j = k % 2
                    if late(g, RING):
                        dve.wait_ge(stored[k], 16 * (g // RING))
                    dve.wait_ge(rstd_done, g + 1)
                    for t in range(BT):
                        last = nc.vector.scalar_tensor_tensor(out=raw[:, j, t, :], in0=raw[:, j, t, :],
                                                              scalar=mv[:, j, t, 0:1], in1=rows[:, k, 1, :],
                                                              op0=ALU.subtract, op1=ALU.mult)
                    last.then_inc(centred, 1)
                    dve.wait_ge(centred, g + 1)
                    for t in range(BT):
                        last = nc.vector.scalar_tensor_tensor(out=yout[:, k, t, :], in0=raw[:, j, t, :],
                                                              scalar=rs[:, j, t:t + 1], in1=rows[:, k, 2, :],
                                                              op0=ALU.mult, op1=ALU.add)
                    last.then_inc(y_done, 1)

                def body(g, k):
                    output(g, k)
                    if norm:
                        normalise(g - 1, (k - 1) % RING)

                output(0, 0)
                for g in range(1, RING):
                    body(g, g)
                ring(dve, RING, N, RING, body)
                if norm:
                    normalise(N - 1, (N - 1) % RING)

            @block.gpsimd
            def _(pool):
                def store(g, k):
                    pool.wait_ge(y_done, g + 1)
                    pool.dma_start(out[:, bass.ds(g * BT, BT), :], yout[:, k, :, :]).then_inc(stored[k], 16)

                def rstd(g, k):
                    pool.wait_ge(var_done, g + 1)
                    nc.gpsimd.tensor_tensor(rs[:, k % 2, :], ve[:, k % 2, :], core.neg_half[:, 0:BT],
                                            ALU.pow).then_inc(rstd_done, 1)

                def body(g, k):
                    if not norm:
                        store(g, k)
                    else:
                        rstd(g, k)
                        store(g - 1, (k - 1) % RING)

                if not norm:
                    store(0, 0)
                else:
                    rstd(0, 0)
                for g in range(1, RING):
                    body(g, g)
                ring(pool, RING, N, RING, body)
                if norm:
                    store(N - 1, (N - 1) % RING)
                for k in range(RING):
                    pool.wait_ge(stored[k], 16 * ((N - k + RING - 1) // RING))


def stage_combine(core, name, r, blocks, add=None, out=None):
    nc, K = core.nc, r.k
    per = G * K
    with Stage(core, name) as st:
        R = 8
        y = st.sb("y", [P, R, P])
        got = [st.sem(f"got{k}") for k in range(R)]
        added, used, normed, stored = (st.sem(n) for n in ("added", "used", "normed", "stored"))
        norm = Norm(core, st) if out is None else None
        with nc.Block() as block:
            if out is not None:
                @block.sync
                def _(sp):
                    for c in range(NCH):
                        sp.wait_ge(used, per * (c + 1))
                        sp.dma_start(out[G * c:G * c + G].rearrange("b s d -> s b d"), chunk(core.h, c)).then_inc(stored, 16)
                    sp.wait_ge(stored, 16 * NCH)

            @block.gpsimd
            def _(pool):
                for n in range(B * K):
                    if n >= R:
                        pool.wait_ge(used, n - R + 1)
                    nc.gpsimd.indirect_dma_start(y[:, n % R, :], None, core.slots_out[0:blocks * BS, :],
                                                 bass.IndirectOffsetOnAxis(r.back[:, n // K, n % K:n % K + 1], 0)
                                                 ).then_inc(got[n % R], 16)
                    if norm and n >= per + R and (n - R) % per == 0:
                        norm.rstd(pool, (n - R) // per - 1, ((n - R) // per - 1) % 2)
                if norm:
                    for c in range((B * K - 1 - R) // per, NCH):
                        norm.rstd(pool, c, c % 2)

            @block.vector
            def _(dve):
                if add is not None:
                    for c in range(NCH):
                        nc.vector.tensor_tensor(chunk(core.h, c), chunk(core.h, c), chunk(add, c), ALU.add).then_inc(added, 1)
                    dve.wait_ge(added, NCH)

                def scale(c):
                    norm.scale(dve, chunk(core.x, c), chunk(core.h, c), c, c % 2).then_inc(normed, 1)

                for n in range(B * K):
                    b, k = n // K, n % K
                    dve.wait_ge(got[n % R], 16 * (n // R + 1))
                    if k:
                        dve.wait_ge(used, n)
                    nc.vector.scalar_tensor_tensor(out=core.h[:, b, :], in0=y[:, n % R, :], scalar=r.gates[:, b, k:k + 1],
                                                   in1=core.h[:, b, :], op0=ALU.mult, op1=ALU.add).then_inc(used, 1)
                    if norm and (n + 1) % per == 0:
                        c = n // per
                        dve.wait_ge(used, n + 1)
                        norm.statistics(dve, chunk(core.h, c), c, c % 2)
                        if c:
                            scale(c - 1)
                dve.wait_ge(used, B * K)
                if norm:
                    scale(NCH - 1)
                    dve.wait_ge(normed, NCH)


def stage_twice_normed(core, name, xn):
    nc = core.nc
    with Stage(core, name) as st:
        first, second = Norm(core, st, "first"), Norm(core, st, "second")
        added, normed, twice = st.sem("added"), st.sem("normed"), st.sem("twice")
        with nc.Block() as block:
            @block.gpsimd
            def _(pool):
                def add(c):
                    nc.gpsimd.tensor_tensor(chunk(core.h, c), chunk(core.h, c), chunk(core.x, c), ALU.add).then_inc(added, 1)

                add(0)
                add(1)
                for c in range(NCH + 1):
                    if c < NCH:
                        first.rstd(pool, c, c % 2)
                        if c + 2 < NCH:
                            add(c + 2)
                    if c:
                        second.rstd(pool, c - 1, (c - 1) % 2)

            @block.vector
            def _(dve):
                for c in range(NCH + 3):
                    if c < NCH:
                        dve.wait_ge(added, c + 1)
                        first.statistics(dve, chunk(core.h, c), c, c % 2)
                    if c >= 3:
                        second.scale(dve, chunk(xn, c - 3), chunk(core.x, c - 3), c - 3, (c - 3) % 2).then_inc(twice, 1)
                    if 1 <= c <= NCH:
                        first.scale(dve, chunk(core.x, c - 1), chunk(core.h, c - 1), c - 1, (c - 1) % 2).then_inc(normed, 1)
                    if 2 <= c <= NCH + 1:
                        dve.wait_ge(normed, c - 1)
                        second.statistics(dve, chunk(core.x, c - 2), c - 2, c % 2)
                dve.wait_ge(twice, NCH)


def stage_l0_ffn(core):
    nc, ins = core.nc, core.ins
    with Stage(core, "l0f") as st:
        xn = st.sb("xn", [P, B, P])
        stage_twice_normed(core, "l0f_ln", xn)
        Attention(core, "l0f_att", xn, "L0_ffn_wq", "L0_ffn_wk", "L0_ffn_wv", True, HD ** -0.5, wo="L0_ffn_wo",
                  affine=("L0_ffn_ln1_g", "L0_ffn_ln1_b"), norm=(xn, ("L0_ffn_ln2_g", "L0_ffn_ln2_b"))).run()
        r = Routing(core, st, 64, 2)
        with Stage(core, "l0f_xt") as st2:
            xt = st2.sb("xt", [P, B * P])
            stage_transpose(core, "l0f_tr", xn, xt)
            stage_route(core, "l0f_rt", r, xt, xn, ins["L0_ffn_wr"], capacity=C_L0)
        stage_experts(core, "l0f_ex", r, 64, ins["L0_ffn_packed"], ins["L0_ffn_rows"], ACT.Gelu_apprx_tanh, False)
        stage_combine(core, "l0f_co", r, 64, add=core.x)


def stage_l1_ffn(core):
    nc, ins = core.nc, core.ins
    with Stage(core, "l1f") as st:
        t = st.sb("t", [P, B, P])
        Attention(core, "l1f_att", core.x, "L1_ffn_Wq", "L1_ffn_Wk", "L1_ffn_Wv", True, HD ** -0.5, wo="L1_ffn_Wo",
                  bq="L1_ffn_bq", bk="L1_ffn_bk", bv="L1_ffn_bv", bo="L1_ffn_bo",
                  norm=(t, ("L1_ffn_ln1_g", "L1_ffn_ln1_b"))).run()
        r = Routing(core, st, 8, 1)
        with Stage(core, "l1f_xt") as st2:
            xt = st2.sb("xt", [P, B * P])
            stage_transpose(core, "l1f_tr", t, xt)
            stage_route(core, "l1f_rt", r, xt, t, ins["L1_ffn_gate_W"], ins["L1_ffn_gate_b"], gate="value")
        stage_experts(core, "l1f_ex", r, r.blocks, ins["L1_ffn_packed"], ins["L1_ffn_rows"], ACT.Gelu_apprx_tanh, True)
        stage_combine(core, "l1f_co", r, r.blocks)


def stage_l2_ffn(core):
    nc, ins = core.nc, core.ins
    with Stage(core, "l2f") as st:
        r = Routing(core, st, 8, 2)
        with Stage(core, "l2f_xt") as st2:
            xt = st2.sb("xt", [P, B * P])
            stage_transpose(core, "l2f_tr", core.x, xt)
            stage_route(core, "l2f_rt", r, xt, core.x, ins["L2_ffn_Wg"], over="logits", gate="softmax")
        stage_experts(core, "l2f_ex", r, r.blocks, ins["L2_ffn_packed"], ins["L2_ffn_rows"], ACT.Relu, True, norm=True)
        stage_combine(core, "l2f_co", r, r.blocks)


def stage_shared(core, name, r, xt, w1, b1, w2, b2, experts):
    nc, ins, S = core.nc, core.ins, experts
    M = w1.shape[2] // P
    with Stage(core, name) as st:
        w1s, w2s = st.sb("w1", [P, S, M * P]), st.sb("w2", [P, S, M, P])
        b1s, b2s = st.sb("b1", [P, S, M]), st.sb("b2", [P, S, P])
        mid = st.sb("mid", [P, 2, M, W])
        ps_u, ps_o = st.ps("ps_u", [P, 4, 512]), st.ps("ps_o", [P, 2, 512])
        loaded, up, acted, down, added, scaled = (st.sem(n) for n in ("loaded", "up", "acted", "down", "added", "scaled"))
        scattered = st.sem("scattered")
        N = NCH
        with nc.Block() as block:
            @block.gpsimd
            def _(pool):
                scatter_rows(core, pool, r, core.x, scattered)

            @block.sync
            def _(sp):
                sp.dma_start(w1s[:, :, :], w1.rearrange("s p f -> p s f")).then_inc(loaded, 16)
                sp.dma_start(w2s[:, :, :, :], w2.rearrange("s (m p) d -> p s m d", p=P)).then_inc(loaded, 16)
                sp.dma_start(b1s[:, :, :], b1.rearrange("s p m -> p s m")).then_inc(loaded, 16)
                sp.dma_start(b2s[:, :, :], b2.partition_broadcast(P)).then_inc(loaded, 16)
                sp.wait_ge(loaded, 64)

            @block.tensor
            def _(pe):
                pe.wait_ge(loaded, 64)

                def first(c, s):
                    for m in range(M):
                        q = M * (S * c + s) + m
                        if q >= 4:
                            pe.wait_ge(acted, q - 3)
                        nc.tensor.matmul(ps_u[:, q % 4, :], w1s[:, s, P * m:P * m + P], xt[:, W * c:W * c + W],
                                         start=True, stop=True).then_inc(up, 1)

                def second(n):
                    c, s = n // S, n % S
                    pe.wait_ge(acted, M * (n + 1))
                    if n >= 2:
                        pe.wait_ge(added, n - 1)
                    for g in range(G):
                        for m in range(M):
                            last = nc.tensor.matmul(ps_o[:, n % 2, P * g:P * g + P], mid[:, n % 2, m, P * g:P * g + P],
                                                    w2s[:, s, m, :], start=(m == 0), stop=(m == M - 1))
                    last.then_inc(down, 1)

                for n in range(S * N):
                    first(n // S, n % S)
                    if n:
                        second(n - 1)
                second(S * N - 1)

            @block.scalar
            def _(act):
                act.wait_ge(loaded, 64)
                for n in range(S * N):
                    for m in range(M):
                        q = M * n + m
                        act.wait_ge(up, q + 1)
                        if m == 0 and n >= 2:
                            act.wait_ge(down, n - 1)
                        nc.scalar.activation(mid[:, n % 2, m, :], ps_u[:, q % 4, :], ACT.Gelu,
                                             bias=b1s[:, n % S, m:m + 1]).then_inc(acted, 1)

            @block.vector
            def _(dve):
                dve.wait_ge(loaded, 64)
                tt = nc.vector.tensor_tensor
                tt(b2s[:, 0, :], b2s[:, 0, :], b2s[:, 1, :], ALU.add).then_inc(scaled, 1)
                dve.wait_ge(scaled, 1)
                nc.vector.tensor_scalar(b2s[:, 0, :], b2s[:, 0, :], 1.0 / S, None, ALU.mult).then_inc(scaled, 1)
                dve.wait_ge(scaled, 2)
                for c in range(NCH):
                    last = tt(chunk(core.h, c), chunk(core.h, c), b2s[:, 0:1, :].broadcast_to((P, G, P)), ALU.add)
                last.then_inc(scaled, 1)
                dve.wait_ge(scaled, 3)
                for n in range(S * N):
                    c = n // S
                    dve.wait_ge(down, n + 1)
                    if n:
                        dve.wait_ge(added, n)
                    nc.vector.scalar_tensor_tensor(out=chunk(core.h, c), in0=bank4(ps_o[:, n % 2, :]), scalar=1.0 / S,
                                                   in1=chunk(core.h, c), op0=ALU.mult, op1=ALU.add).then_inc(added, 1)
                dve.wait_ge(added, S * N)


def stage_l3_ffn(core, out):
    nc, ins = core.nc, core.ins
    with Stage(core, "l3f") as st:
        r = Routing(core, st, 16, 4)
        with Stage(core, "l3f_xt") as st2:
            xt = st2.sb("xt", [P, B * P])
            stage_transpose(core, "l3f_tr", core.x, xt)
            stage_route(core, "l3f_rt", r, xt, core.x, ins["L3_ffn_gate_wT"], gate="softmax", scatter=False)
            stage_shared(core, "l3f_sh", r, xt, ins["L3_ffn_se_w1"], ins["L3_ffn_se_b1"], ins["L3_ffn_se_w2"],
                         ins["L3_ffn_se_b2"], 2)
        stage_experts(core, "l3f_ex", r, r.blocks, ins["L3_ffn_packed"], ins["L3_ffn_rows"], ACT.Gelu, True)
        stage_combine(core, "l3f_co", r, r.blocks, out=out)


MAGIC = float(1.5 * 2 ** 23)
TIE_UP = float(2.0 ** -22)


def stage_l1_attn(core):
    nc, ins = core.nc, core.ins
    T = B * P
    with Stage(core, "l1a") as st:
        spikes = st.sb("spikes", [P, 3, T], BF16)
        tie_up = st.sb("tie_up", [P, 1])
        with Stage(core, "l1p") as s1:
            w = s1.sb("w", [P, 3 * P])
            gamma_beta = s1.sb("gamma_beta", [P, 2, 3])
            xs = s1.sb("xs", [P, T])
            qkv = s1.sb("qkv", [P, 3, T])
            half = s1.sb("half", [P, 2, W])
            big = s1.sb("big", [P, 2, W])
            stats, mv = s1.sb("stats", [P, 3, NCH, 6]), s1.sb("mv", [P, 3, 2])
            ve, rs, scale, shift = (s1.sb(n, [P, 3]) for n in ("ve", "rs", "scale", "shift"))
            ps_t, ps_m = s1.ps("ps_t", [P, 2, 512]), s1.ps("ps_m", [P, 2, 3, 512])
            sem = {n: s1.sem(n) for n in ("in", "set", "tr", "half", "big", "xs", "mm", "read", "stats", "aggr", "var",
                                          "rstd", "affine", "nhalf", "nbig", "spike")}
            with nc.Block() as block:
                @block.sync
                def _(sp):
                    sp.dma_start(w[:, :], ins["L1_attn_WqkvT"]).then_inc(sem["in"], 16)
                    with nc.allow_non_contiguous_dma("one value per feature"):
                        for k, n in enumerate(("L1_attn_gamma", "L1_attn_beta")):
                            sp.dma_start(gamma_beta[:, k, :], ins[n].rearrange("(m p) -> p m", p=P)).then_inc(sem["in"], 16)
                    sp.wait_ge(sem["in"], 48)

                @block.tensor
                def _(pe):
                    def turn(c):
                        if c >= 2:
                            pe.wait_ge(sem["half"], c - 1)
                        for g in range(G):
                            last = nc.tensor.transpose(ps_t[:, c % 2, P * g:P * g + P], core.x[:, G * c + g, :], core.ident[:, :])
                        last.then_inc(sem["tr"], 1)

                    turn(0)
                    turn(1)
                    pe.wait_ge(sem["in"], 48)
                    for c in range(NCH):
                        pe.wait_ge(sem["xs"], c + 1)
                        if c >= 2:
                            pe.wait_ge(sem["read"], c - 1)
                            pe.wait_ge(sem["stats"], c - 1)
                        for m in range(3):
                            last = nc.tensor.matmul(ps_m[:, c % 2, m, :], w[:, P * m:P * m + P], xs[:, W * c:W * c + W],
                                                    start=True, stop=True)
                        last.then_inc(sem["mm"], 1)
                        if c + 2 < NCH:
                            turn(c + 2)

                @block.scalar
                def _(act):
                    act.wait_ge(sem["set"], 1)

                    def relu(c):
                        act.wait_ge(sem["tr"], c + 1)
                        if c >= 2:
                            act.wait_ge(sem["big"], c - 1)
                        nc.scalar.activation(half[:, c % 2, :], ps_t[:, c % 2, :], ACT.Relu, bias=tie_up[:, 0:1]).then_inc(sem["half"], 1)

                    relu(0)
                    for c in range(NCH):
                        if c + 1 < NCH:
                            relu(c + 1)
                        act.wait_ge(sem["stats"], c + 1)
                        nc.scalar.copy(qkv[:, :, W * c:W * c + W], ps_m[:, c % 2, :, :]).then_inc(sem["read"], 1)
                    act.wait_ge(sem["read"], NCH)
                    act.wait_ge(sem["affine"], 1)
                    for n in range(3 * NCH):
                        m, c = n // NCH, n % NCH
                        nc.scalar.activation(qkv[:, m, W * c:W * c + W], qkv[:, m, W * c:W * c + W], ACT.Relu,
                                             bias=shift[:, m:m + 1], scale=scale[:, m:m + 1]).then_inc(sem["nhalf"], 1)

                @block.gpsimd
                def _(pool):
                    pool.wait_ge(sem["var"], 1)
                    nc.gpsimd.tensor_tensor(rs[:, :], ve[:, :], core.neg_half[:, 0:3], ALU.pow).then_inc(sem["rstd"], 1)

                @block.vector
                def _(dve):
                    tt, ts = nc.vector.tensor_tensor, nc.vector.tensor_scalar
                    nc.vector.memset(tie_up[:, :], TIE_UP).then_inc(sem["set"], 1)

                    def spike_x(c):
                        dve.wait_ge(sem["half"], c + 1)
                        ts(big[:, c % 2, :], half[:, c % 2, :], 4.0, MAGIC, ALU.min, ALU.add).then_inc(sem["big"], 1)
                        dve.wait_ge(sem["big"], c + 1)
                        ts(xs[:, W * c:W * c + W], big[:, c % 2, :], MAGIC, None, ALU.subtract).then_inc(sem["xs"], 1)

                    spike_x(0)
                    for c in range(NCH):
                        if c + 1 < NCH:
                            spike_x(c + 1)
                        dve.wait_ge(sem["mm"], c + 1)
                        for m in range(3):
                            last = nc.vector.bn_stats(stats[:, m, c, :], ps_m[:, c % 2, m, :])
                        last.then_inc(sem["stats"], 1)
                    dve.wait_ge(sem["stats"], NCH)
                    for m in range(3):
                        last = nc.vector.bn_aggr(mv[:, m, :], stats[:, m, :, :].rearrange("p c s -> p (c s)"))
                    last.then_inc(sem["aggr"], 1)
                    dve.wait_ge(sem["aggr"], 1)
                    ts(ve[:, :], mv[:, :, 1], EPS, None, ALU.add).then_inc(sem["var"], 1)
                    dve.wait_ge(sem["rstd"], 1)
                    dve.wait_ge(sem["in"], 48)
                    tt(scale[:, :], rs[:, :], gamma_beta[:, 0, :], ALU.mult).then_inc(sem["aggr"], 1)
                    dve.wait_ge(sem["aggr"], 2)
                    tt(shift[:, :], mv[:, :, 0], scale[:, :], ALU.mult).then_inc(sem["aggr"], 1)
                    dve.wait_ge(sem["aggr"], 3)
                    tt(shift[:, :], gamma_beta[:, 1, :], shift[:, :], ALU.subtract).then_inc(sem["aggr"], 1)
                    dve.wait_ge(sem["aggr"], 4)
                    ts(shift[:, :], shift[:, :], TIE_UP, None, ALU.add).then_inc(sem["affine"], 1)
                    for n in range(3 * NCH):
                        m, c = n // NCH, n % NCH
                        one = qkv[:, m, W * c:W * c + W]
                        dve.wait_ge(sem["nhalf"], n + 1)
                        ts(one, one, 4.0, MAGIC, ALU.min, ALU.add).then_inc(sem["nbig"], 1)
                        dve.wait_ge(sem["nbig"], n + 1)
                        ts(spikes[:, m, W * c:W * c + W], one, MAGIC, None, ALU.subtract).then_inc(sem["spike"], 1)
                    dve.wait_ge(sem["spike"], 3 * NCH)

        with Stage(core, "l1s") as s2:
            wp = s2.sb("wp", [P, P])
            bias = s2.sb("bias", [P, 1, P])
            head_mask, mask_bf = s2.sb("head_mask", [P, HEADS]), s2.sb("mask_bf", [P, HEADS], BF16)
            ident_bf = s2.sb("ident_bf", [P, P], BF16)
            v = s2.sb("v", [P, 2, G, P], BF16)
            spread = s2.sb("spread", [P, 2, HEADS, P], BF16)
            att = s2.sb("att", [P, 2, UNIT, P], BF16)
            ohalf, obig = s2.sb("ohalf", [P, 2, P]), s2.sb("obig", [P, 2, P])
            o, ot = s2.sb("o", [P, 2, G, P]), s2.sb("ot", [P, 2, W])
            ps_v = s2.ps("ps_v", [P, 1, 1024], BF16)
            ps_s, ps_o, ps_m = s2.ps("ps_s", [P, 2, 512]), s2.ps("ps_o", [P, 2, 512]), s2.ps("ps_m", [P, 2, 512])
            sem = {n: s2.sem(n) for n in ("in", "set", "v_tr", "v", "sp_lo", "sp_hi", "score", "att", "pv", "ohalf",
                                          "obig", "o", "o_tr", "ot", "mm", "hb", "out", "normed")}
            norm = Norm(core, s2, "n")
            NU = 2 * B
            with nc.Block() as block:
                @block.sync
                def _(sp):
                    sp.dma_start(wp[:, :], ins["L1_attn_WprojT"]).then_inc(sem["in"], 16)
                    sp.dma_start(bias[:, :, :], ins["L1_attn_bproj"].unsqueeze(0).partition_broadcast(P)).then_inc(sem["in"], 16)
                    sp.dma_start(head_mask[:, :], ins["head_mask"]).then_inc(sem["in"], 16)
                    sp.wait_ge(sem["in"], 48)

                def spread_half(eng, b, half):
                    hs = slice(UNIT * half, UNIT * half + UNIT)
                    one = spikes[:, 0, P * b:P * b + P].unsqueeze(1).broadcast_to((P, UNIT, P))
                    return eng.tensor_tensor(spread[:, b % 2, hs, :], one,
                                             mask_bf[:, hs].unsqueeze(2).broadcast_to((P, UNIT, P)), ALU.mult)

                @block.gpsimd
                def _(pool):
                    pool.wait_ge(sem["set"], 2)
                    pool.wait_ge(sem["in"], 48)
                    for b in range(B):
                        if b >= 2:
                            pool.wait_ge(sem["score"], 2 * (b - 1))
                        spread_half(nc.gpsimd, b, 1).then_inc(sem["sp_hi"], 1)
                        if b % G == 0:
                            c = b // G
                            nc.gpsimd.tensor_tensor(chunk(core.h, c), chunk(core.h, c),
                                                    bias[:, :, :].broadcast_to((P, G, P)), ALU.add).then_inc(sem["hb"], 1)
                        if b % G == 2 and b >= 2 * G:
                            norm.rstd(pool, b // G - 2, b // G % 2)
                    norm.rstd(pool, NCH - 2, 0)
                    norm.rstd(pool, NCH - 1, 1)

                @block.tensor
                def _(pe):
                    pe.wait_ge(sem["set"], 2)

                    def turn_v(c):
                        if c >= 1:
                            pe.wait_ge(sem["v"], c)
                        for g in range(G):
                            last = nc.tensor.transpose(ps_v[:, 0, P * g:P * g + P], spikes[:, 2, W * c + P * g:W * c + P * g + P],
                                                       ident_bf[:, :])
                        last.then_inc(sem["v_tr"], 1)

                    def scores(n):
                        b, half = n // 2, n % 2
                        pe.wait_ge(sem["sp_hi" if half else "sp_lo"], b + 1)
                        if n >= 2:
                            pe.wait_ge(sem["att"], n - 1)
                        nc.tensor.matmul(ps_s[:, half, :], spikes[:, 1, P * b:P * b + P],
                                         spread[:, b % 2, UNIT * half:UNIT * half + UNIT, :],
                                         start=True, stop=True).then_inc(sem["score"], 1)

                    def value_product(n):
                        b, half = n // 2, n % 2
                        pe.wait_ge(sem["att"], n + 1)
                        pe.wait_ge(sem["v"], b // G + 1)
                        if half == 0 and b >= 2:
                            pe.wait_ge(sem["ohalf"], b - 1)
                        for j in range(UNIT):
                            hd = slice(HD * (UNIT * half + j), HD * (UNIT * half + j + 1))
                            last = nc.tensor.matmul(ps_o[:, b % 2, hd], att[:, n % 2, j, :], v[:, b // G % 2, b % G, hd],
                                                    start=True, stop=True)
                        last.then_inc(sem["pv"], 1)

                    def turn_o(c):
                        pe.wait_ge(sem["o"], G * (c + 1))
                        if c >= 1:
                            pe.wait_ge(sem["ot"], c)
                        for g in range(G):
                            last = nc.tensor.transpose(ps_m[:, 0, P * g:P * g + P], o[:, c % 2, g, :], core.ident[:, :])
                        last.then_inc(sem["o_tr"], 1)

                    def project(c):
                        pe.wait_ge(sem["ot"], c + 1)
                        if c >= 1:
                            pe.wait_ge(sem["out"], c)
                        for g in range(G):
                            last = nc.tensor.matmul(ps_m[:, 1, P * g:P * g + P], ot[:, c % 2, P * g:P * g + P], wp[:, :],
                                                    start=True, stop=True)
                        last.then_inc(sem["mm"], 1)

                    turn_v(0)
                    pe.wait_ge(sem["in"], 48)
                    for n in range(NU + 2):
                        c, k = n // (2 * G), n % (2 * G)
                        if n < NU:
                            scores(n)
                            if k == 1 and c + 1 < NCH:
                                turn_v(c + 1)
                        if n >= 2:
                            value_product(n - 2)
                        if k == 5 and c >= 1:
                            turn_o(c - 1)
                        if k == 6 and c >= 1:
                            project(c - 1)
                    turn_o(NCH - 1)
                    project(NCH - 1)

                @block.scalar
                def _(act):
                    for n in range(NU + 3):
                        c, k = n // (2 * G), n % (2 * G)
                        m = n - 3
                        if m >= 0 and m % 2 == 1:
                            b = m // 2
                            act.wait_ge(sem["pv"], 2 * b + 2)
                            if b >= 2:
                                act.wait_ge(sem["obig"], b - 1)
                            nc.scalar.activation(ohalf[:, b % 2, :], ps_o[:, b % 2, 0:P], ACT.Relu, bias=tie_up[:, 0:1],
                                                 scale=HD ** -0.5).then_inc(sem["ohalf"], 1)
                        if k == 1 and n < NU and c + 1 < NCH or n == 0:
                            nxt = 0 if n == 0 else c + 1
                            act.wait_ge(sem["v_tr"], nxt + 1)
                            if nxt >= 2:
                                act.wait_ge(sem["pv"], 2 * G * (nxt - 1))
                            nc.scalar.copy(flat(v[:, nxt % 2, :, :]), ps_v[:, 0, 0:W]).then_inc(sem["v"], 1)
                        if k == 5 and c >= 1:
                            act.wait_ge(sem["o_tr"], c)
                            if c >= 3:
                                act.wait_ge(sem["mm"], c - 2)
                            nc.scalar.copy(ot[:, (c - 1) % 2, :], ps_m[:, 0, :]).then_inc(sem["ot"], 1)
                    act.wait_ge(sem["o_tr"], NCH)
                    act.wait_ge(sem["mm"], NCH - 2)
                    nc.scalar.copy(ot[:, (NCH - 1) % 2, :], ps_m[:, 0, :]).then_inc(sem["ot"], 1)

                @block.vector
                def _(dve):
                    ts = nc.vector.tensor_scalar
                    dve.wait_ge(sem["in"], 48)
                    nc.vector.tensor_copy(mask_bf[:, :], head_mask[:, :]).then_inc(sem["set"], 1)
                    nc.vector.tensor_copy(ident_bf[:, :], core.ident[:, :]).then_inc(sem["set"], 1)
                    dve.wait_ge(sem["set"], 2)

                    def spread_low(b):
                        if b >= 2:
                            dve.wait_ge(sem["score"], 2 * (b - 1))
                        spread_half(nc.vector, b, 0).then_inc(sem["sp_lo"], 1)

                    def clip(n):
                        dve.wait_ge(sem["score"], n + 1)
                        if n >= 2:
                            dve.wait_ge(sem["pv"], n - 1)
                        ts(att[:, n % 2, :, :], bank4(ps_s[:, n % 2, :]), 4.0, None, ALU.min).then_inc(sem["att"], 1)

                    def spike_o(b):
                        dve.wait_ge(sem["ohalf"], b + 1)
                        c = b // G
                        if c >= 2 and b % G == 0:
                            dve.wait_ge(sem["o_tr"], c - 1)
                        ts(obig[:, b % 2, :], ohalf[:, b % 2, :], 4.0, MAGIC, ALU.min, ALU.add).then_inc(sem["obig"], 1)
                        dve.wait_ge(sem["obig"], b + 1)
                        ts(o[:, c % 2, b % G, :], obig[:, b % 2, :], MAGIC, None, ALU.subtract).then_inc(sem["o"], 1)

                    def residual(c):
                        dve.wait_ge(sem["mm"], c + 1)
                        dve.wait_ge(sem["hb"], c + 1)
                        nc.vector.tensor_tensor(chunk(core.h, c), bank4(ps_m[:, 1, :]), chunk(core.h, c),
                                                ALU.add).then_inc(sem["out"], 1)

                    def statistics(c):
                        dve.wait_ge(sem["out"], c + 1)
                        norm.statistics(dve, chunk(core.h, c), c, c % 2)

                    def scale(c):
                        norm.scale(dve, chunk(core.x, c), chunk(core.h, c), c, c % 2).then_inc(sem["normed"], 1)

                    spread_low(0)
                    for n in range(NU + 4):
                        c, k = n // (2 * G), n % (2 * G)
                        if n < NU:
                            if n % 2 == 0 and n // 2 + 1 < B:
                                spread_low(n // 2 + 1)
                            clip(n)
                        m = n - 4
                        if m >= 0 and m % 2 == 1:
                            spike_o(m // 2)
                        if k == 7 and c >= 1:
                            residual(c - 1)
                        if n < NU and c >= 2:
                            if k == 0:
                                statistics(c - 2)
                            elif k == 6:
                                scale(c - 2)
                    statistics(NCH - 2)
                    residual(NCH - 1)
                    statistics(NCH - 1)
                    scale(NCH - 2)
                    scale(NCH - 1)
                    dve.wait_ge(sem["normed"], NCH)


LEVELS = 5
ENTROPY_LIMIT = 0.8


def stage_l2_attn(core):
    nc, ins = core.nc, core.ins
    with Stage(core, "l2a") as st:
        acc = st.sb("acc", [P, B, P])
        z, ws = st.sb("z", [P, B, HEADS]), st.sb("ws", [P, B, HEADS])
        weight = st.sb("weight", [P, 1])
        go = st.sb("go", [P, 1], I32)
        with Stage(core, "l2i") as s0:
            ready = s0.sem("ready")
            with nc.Block() as block:
                @block.vector
                def _(dve):
                    nc.vector.memset(acc[:, :, :], 0.0)
                    nc.vector.memset(weight[:, :], 1.0).then_inc(ready, 1)
                    dve.wait_ge(ready, 1)
                    nc.vector.tensor_copy(go[:, :], weight[:, :]).then_inc(ready, 1)
                    dve.wait_ge(ready, 2)
        with nc.Fori(0, LEVELS):
            alive = nc.values_load(go[0:1, 0:1], min_val=0, max_val=1)
            with nc.If(alive > 0):
                Attention(core, "l2l", core.x, "L2_attn_wq", "L2_attn_wk", "L2_attn_wv", True, float(P) ** -0.5,
                          bq="L2_attn_bq", bk="L2_attn_bk", bv="L2_attn_bv", dst=core.x, sums=(z, ws)).run()
                l2_level_end(core, acc, z, ws, weight, go)
        l2_out(core, acc)


def l2_level_end(core, acc, z, ws, weight, go):
    nc = core.nc
    with Stage(core, "l2e") as st:
        logz, rz, ent = (st.sb(n, [P, B, HEADS]) for n in ("logz", "rz", "ent"))
        total, under = st.sb("total", [P, 1]), st.sb("under", [P, 1])
        ones = st.sb("ones", [P, P])
        ps = st.ps("ps", [P, 512])
        log_done, chain, total_done, all_done = (st.sem(n) for n in ("log_done", "chain", "total_done", "all_done"))
        with nc.Block() as block:
            @block.scalar
            def _(act):
                nc.scalar.activation(logz[:, :, :], z[:, :, :], ACT.Ln).then_inc(log_done, 1)

            @block.tensor
            def _(pe):
                pe.wait_ge(total_done, 1)
                nc.tensor.matmul(ps[:, 0:1], ones[:, :], total[:, :], start=True, stop=True).then_inc(all_done, 1)

            @block.vector
            def _(dve):
                made = [0]

                def then(*i):
                    i[-1].then_inc(chain, 1)
                    made[0] += 1
                    dve.wait_ge(chain, made[0])

                nc.vector.memset(ones[:, :], 1.0)
                for c in range(NCH):
                    i = nc.vector.scalar_tensor_tensor(out=chunk(acc, c), in0=chunk(core.x, c), scalar=weight[:, 0:1],
                                                       in1=chunk(acc, c), op0=ALU.mult, op1=ALU.add)
                then(i, nc.vector.reciprocal(rz[:, :, :], z[:, :, :]))
                then(nc.vector.tensor_tensor(ent[:, :, :], ws[:, :, :], rz[:, :, :], ALU.mult))
                dve.wait_ge(log_done, 1)
                then(nc.vector.scalar_tensor_tensor(out=ent[:, :, :], in0=ent[:, :, :], scalar=-float(P) ** -0.5,
                                                    in1=logz[:, :, :], op0=ALU.mult, op1=ALU.add))
                nc.vector.tensor_reduce(total[:, :], flat(ent[:, :, :]), AX_X, ALU.add).then_inc(total_done, 1)
                dve.wait_ge(all_done, 1)
                mean = 1.0 / (B * P * HEADS * float(np.log(np.float32(P))))
                then(nc.vector.tensor_scalar(under[:, :], ps[:, 0:1], mean, ENTROPY_LIMIT, ALU.mult, ALU.is_lt))
                then(nc.vector.tensor_tensor(weight[:, :], weight[:, :], under[:, :], ALU.mult))
                then(nc.vector.tensor_copy(go[:, :], weight[:, :]))


def l2_out(core, acc):
    nc, ins = core.nc, core.ins
    with Stage(core, "l2o") as st:
        w, bias = st.sb("w", [P, P]), st.sb("bias", [P, 1, P])
        at = st.sb("at", [P, 2, W])
        ps_t, ps_o = st.ps("ps_t", [P, 2, 512]), st.ps("ps_o", [P, 2, 512])
        loaded, turned, copied, mm, biased, added = (st.sem(n) for n in ("loaded", "turned", "copied", "mm", "biased", "added"))
        norm, normed = Norm(core, st), st.sem("normed")
        with nc.Block() as block:
            @block.sync
            def _(sp):
                sp.dma_start(w[:, :], ins["L2_attn_w_out"]).then_inc(loaded, 16)
                sp.dma_start(bias[:, :, :], ins["L2_attn_b_out"].unsqueeze(0).partition_broadcast(P)).then_inc(loaded, 16)
                sp.wait_ge(loaded, 32)

            @block.tensor
            def _(pe):
                def turn(c):
                    if c >= 2:
                        pe.wait_ge(copied, c - 1)
                    for g in range(G):
                        last = nc.tensor.transpose(ps_t[:, c % 2, P * g:P * g + P], acc[:, G * c + g, :], core.ident[:, :])
                    last.then_inc(turned, 1)

                turn(0)
                pe.wait_ge(loaded, 32)
                for c in range(NCH):
                    if c + 1 < NCH:
                        turn(c + 1)
                    pe.wait_ge(copied, c + 1)
                    if c >= 2:
                        pe.wait_ge(added, c - 1)
                    for g in range(G):
                        last = nc.tensor.matmul(ps_o[:, c % 2, P * g:P * g + P], at[:, c % 2, P * g:P * g + P], w[:, :],
                                                start=True, stop=True)
                    last.then_inc(mm, 1)

            @block.scalar
            def _(act):
                for c in range(NCH):
                    act.wait_ge(turned, c + 1)
                    if c >= 2:
                        act.wait_ge(mm, c - 1)
                    nc.scalar.copy(at[:, c % 2, :], ps_t[:, c % 2, :]).then_inc(copied, 1)

            @block.gpsimd
            def _(pool):
                pool.wait_ge(loaded, 32)
                for c in range(NCH):
                    nc.gpsimd.tensor_tensor(chunk(core.h, c), chunk(core.h, c), bias[:, :, :].broadcast_to((P, G, P)),
                                            ALU.add).then_inc(biased, 1)
                    if c:
                        norm.rstd(pool, c - 1, (c - 1) % 2)
                norm.rstd(pool, NCH - 1, (NCH - 1) % 2)

            @block.vector
            def _(dve):
                def scale(c):
                    norm.scale(dve, chunk(core.x, c), chunk(core.h, c), c, c % 2).then_inc(normed, 1)

                for c in range(NCH):
                    dve.wait_ge(mm, c + 1)
                    dve.wait_ge(biased, c + 1)
                    nc.vector.tensor_tensor(chunk(core.h, c), bank4(ps_o[:, c % 2, :]), chunk(core.h, c), ALU.add).then_inc(added, 1)
                    dve.wait_ge(added, c + 1)
                    norm.statistics(dve, chunk(core.h, c), c, c % 2)
                    if c:
                        scale(c - 1)
                scale(NCH - 1)
                dve.wait_ge(normed, NCH)


def stage_l3_attn(core):
    Attention(core, "l3a", core.x, "L3_attn_wq", "L3_attn_wk", "L3_attn_wv", False, None, bq="L3_attn_bq",
              bk="L3_attn_bk", bv="L3_attn_bv", wg="L3_attn_wg", bg="L3_attn_bg",
              norm=(core.x, ())).run()


def tower(nc, ins, out):
    with ExitStack() as ctx:
        core = Core(nc, ctx, ins)
        with Stage(core, "s4") as st:
            kf, ids = st.sb("kf", [P, 3, NL, P]), st.sb("ids", [P, B], I32)
            stage_setup(core, ids)
            s4_kernels(core, kf, ids)
            stage_norm(core, "n0")
            stage_l0_attn(core, kf)
        stage_l0_ffn(core)
        stage_l1_attn(core)
        stage_l1_ffn(core)
        stage_l2_attn(core)
        stage_l2_ffn(core)
        stage_l3_attn(core)
        stage_l3_ffn(core, out)


def decay_table():
    gamma = 1.0 - 2.0 ** (-5.0 - np.arange(HEADS))
    rel = np.arange(P)[:, None] - np.arange(P)[None, :]
    table = np.where(rel[:, None, :] >= 0, gamma[None, :, None] ** np.maximum(rel, 0)[:, None, :], 0.0)
    return (table / np.sqrt(HD)).astype(np.float32)


PACKED = ("L0_ffn_w1", "L0_ffn_w2", "L0_ffn_b", "L1_ffn_W1", "L1_ffn_W2", "L1_ffn_b1", "L1_ffn_b2", "L2_ffn_W1",
          "L2_ffn_W2", "L2_ffn_b", "L2_ffn_gamma", "L3_ffn_re")


def host_layout(inputs):
    a = {k: np.ascontiguousarray(v) for k, v in inputs.items()}
    out = {}
    put = lambda name, v: out.__setitem__(name, np.ascontiguousarray(v))
    for name in ("x", "L0_tok_w", "L0_attn_s4_log_A_real", "L0_attn_s4_A_imag", "L0_attn_s4_C_re", "L0_attn_s4_C_im",
                 "L0_attn_s4_log_dt", "L0_attn_s4_D"):
        put(name, a[name])
    for name in ("s4_out_b", "ln1_w", "ln1_b", "ln2_w", "ln2_b", "ff_b1", "ff_b2"):
        put("L0_attn_" + name, a["L0_attn_" + name])
    put("s4_out_wT", a["L0_attn_s4_out_w"].reshape(NL, 2 * P, P).transpose(2, 0, 1))
    put("ff_w1T", a["L0_attn_ff_w1"].transpose(0, 2, 1))
    put("ff_w2T", a["L0_attn_ff_w2"].reshape(DEPTH, P, 4, P).transpose(0, 3, 2, 1))
    for name in a:
        if name.startswith(("L0_ffn", "L1", "L2", "L3")) and not name.startswith(PACKED):
            put(name, a[name])
    for name in ("wq", "wk", "wv", "wg"):
        put("L3_attn_" + name, a["L3_attn_" + name].T)
    by_feature = lambda t: t.reshape(t.shape[0], -1, P).transpose(0, 2, 1)
    put("L3_ffn_se_b1", by_feature(a["L3_ffn_se_b1"]))
    for layer, w1, b1, w2, rows in (("L0_ffn", "w1", "b1", "w2", ("b2",)), ("L1_ffn", "W1", "b1", "W2", ("b2",)),
                                    ("L2_ffn", "W1", "b1", "W2", ("b2", "gamma", "beta")),
                                    ("L3_ffn", "re_w1", "re_b1", "re_w2", ("re_b2",))):
        w1, b1, w2 = (a[f"{layer}_{n}"] for n in (w1, b1, w2))
        E = w1.shape[0]
        w2 = w2.reshape(E, -1, P, P).transpose(0, 2, 1, 3).reshape(E, P, -1)
        put(layer + "_packed", np.concatenate([w1, w2, by_feature(b1)], axis=2))
        put(layer + "_rows", np.stack([a[f"{layer}_{n}"] for n in rows], axis=1))
    put("L3_ffn_gate_wT", a["L3_ffn_gate_w"].T)
    put("iota_row", np.broadcast_to(np.arange(P, dtype=np.float32), (P, P)))
    put("tri", np.triu(np.ones((P, P), np.float32), 1))
    put("L1_attn_WqkvT", a["L1_attn_Wqkv"].T)
    put("L1_attn_WprojT", a["L1_attn_Wproj"].T)
    for n, part in enumerate("qkv"):
        put("L2_attn_w" + part, a["L2_attn_w_qkv"][:, n * P:(n + 1) * P])
        put("L2_attn_b" + part, a["L2_attn_b_qkv"][n * P:(n + 1) * P])
    put("head_mask", (np.arange(P)[:, None] // HD == np.arange(HEADS)[None, :]).astype(np.float32))
    put("decay", decay_table())
    put("ident", np.eye(P, dtype=np.float32))
    put("dft", dft_tables())
    return out


def kernel(**inputs):
    import concourse.bacc as _bacc
    from concourse.bass_utils import run_bass_kernel_spmd as _run
    nc = _bacc.Bacc("TRN2", target_bir_lowering=False, num_devices=1)
    arrays, ins = {}, {}
    for name, a in host_layout(inputs).items():
        arrays[f"in_{name}_dram"] = a
        ins[name] = nc.dram_tensor(f"in_{name}_dram", a.shape, mybir.dt.from_np(a.dtype), kind="ExternalInput").ap()
    out = nc.dram_tensor("out_0_dram", (B, P, P), F32, kind="ExternalOutput").ap()
    tower(nc, ins, out)
    r = _run(nc, [arrays], core_ids=[0])
    return r.results[0]["out_0_dram"]
```

```python
from contextlib import ExitStack

import numpy as np
import concourse.bass as bass
from concourse import mybir

F32 = mybir.dt.float32
BF16 = mybir.dt.bfloat16
I32 = mybir.dt.int32
U32 = mybir.dt.uint32
ALU = mybir.AluOpType
ACT = mybir.ActivationFunctionType
AX_X = mybir.AxisListType.X

P = 128
B = 32
G = 4
NCH = B // G
W = G * P
EPS = 1e-5
HEADS = 8
HD = P // HEADS
DEPTH = 4
NL = 2 * DEPTH
NS = 32
POOL_LAYERS = 4
NB_POW, NA_POW = 16, 8


def dft_tables():
    s, f = np.arange(P)[:, None], np.arange(P)[None, :]
    n = 2 * P
    angle = 2.0 * np.pi * ((s * f) % n) / n
    cos, sin = np.cos(angle), -np.sin(angle)
    alternating = np.where(np.arange(P) % 2 == 0, 1.0, -1.0)
    sin_nyq, cos_nyq = sin.copy(), cos.copy()
    sin_nyq[:, 0] = alternating
    cos_nyq[:, 0] = alternating
    inv_cos, inv_sin = 2.0 * cos.T / n, 2.0 * sin.T / n
    inv_cos[0, :] = 1.0 / n
    inv_sin[0, :] = alternating / n
    return np.stack([cos, sin_nyq, sin, cos_nyq, inv_cos, inv_sin], axis=1).astype(np.float32)


COS, SIN_NYQ, SIN, COS_NYQ, INV_COS, INV_SIN = range(6)


class Core:

    def __init__(self, nc, ctx, ins):
        self.nc, self.ins = nc, ins
        sb = lambda name, shape, dt=F32: ctx.enter_context(nc.sbuf_tensor(name, shape, dt))
        self.h = sb("h", [P, B, P])
        self.x = sb("x", [P, B, P])
        self.ident = sb("ident", [P, P])
        self.neg_half = sb("neg_half", [P, B])
        self.slots_in = nc.dram_tensor("slots_in", (SLOTS, P + 1), F32).ap()
        self.returned = nc.dram_tensor("returned", (MAX_K * B * P, P), F32).ap()
        self.zero = sb("zero", [P, P + 1])
        self.zeroed = ctx.enter_context(nc.semaphore("zeroed"))


def start_zeroing(core, sp):
    for rows, width in ((core.slots_in, P + 1), (core.returned, P)):
        n = rows.shape[0] // P
        sp.dma_start(rows.rearrange("(p n) d -> p n d", p=P),
                     core.zero[:, 0:width].unsqueeze(1).broadcast_to((P, n, width))).then_inc(core.zeroed, 16)


class Stage:

    def __init__(self, core, name):
        self.nc, self.name, self.ctx, self.sems = core.nc, name, ExitStack(), []

    def __enter__(self):
        self.ctx.__enter__()
        return self

    def __exit__(self, *a):
        if self.sems and a[0] is None:
            self.nc.clear_and_free_semaphores(self.sems)
            self.nc.all_engine_barrier()
        return self.ctx.__exit__(*a)

    def sb(self, name, shape, dt=F32):
        return self.ctx.enter_context(self.nc.sbuf_tensor(f"{self.name}_{name}", shape, dt))

    def ps(self, name, shape, dt=F32):
        return self.ctx.enter_context(self.nc.psum_tensor(f"{self.name}_{name}", shape, dt))

    def sem(self, name):
        self.sems.append(self.nc.alloc_semaphore(f"{self.name}_{name}"))
        return self.sems[-1]


def chunk(t, c):
    return t[:, bass.ds(c * G, G), :]


def flat(ap):
    return ap.rearrange("p a b -> p (a b)")


def stage_setup(core, ids):
    nc, ins = core.nc, core.ins
    with Stage(core, "set") as st:
        ids_in, const_in, const_set = (st.sem(n) for n in ("ids_in", "const_in", "const_set"))
        with nc.Block() as block:
            @block.sync
            def _(sp):
                with nc.allow_non_contiguous_dma("token ids, one column per sequence"):
                    sp.dma_start(ids[:, :], ins["x"].rearrange("b s -> s b")).then_inc(ids_in, 16)
                sp.dma_start(core.ident[:, :], ins["ident"]).then_inc(const_in, 16)
                sp.wait_ge(const_in, 16)
                sp.wait_ge(ids_in, 16)

            @block.gpsimd
            def _(pool):
                nc.gpsimd.memset(core.zero[:, :], 0.0)
                nc.gpsimd.memset(core.neg_half[:, :], -0.5).then_inc(const_set, 1)
                pool.wait_ge(const_set, 1)


def stage_norm(core, name, src=None, dst=None, rows=None):
    src, dst = src or core.h, dst or core.x
    nc = core.nc
    with Stage(core, name) as st:
        stats, mv = st.sb("stats", [P, B, 6]), st.sb("mv", [P, B, 2])
        ve, rs = st.sb("ve", [P, B]), st.sb("rs", [P, B])
        gain_bias = st.sb("gain_bias", [P, 2, P])
        stats_done, var_done, rstd_done, rows_in, centred = (st.sem(n) for n in (
            "stats_done", "var_done", "rstd_done", "rows_in", "centred"))
        with nc.Block() as block:
            if rows:
                @block.sync
                def _(sp):
                    for k, row in enumerate(rows):
                        sp.dma_start(gain_bias[:, k, :], core.ins[row].partition_broadcast(P)).then_inc(rows_in, 16)

            @block.vector
            def _(dve):
                for c in range(NCH):
                    for b in range(G * c, G * c + G):
                        last = nc.vector.bn_stats(stats[:, b, :], src[:, b, :])
                    last.then_inc(stats_done, 1)
                for c in range(NCH):
                    dve.wait_ge(stats_done, c + 1)
                    for b in range(G * c, G * c + G):
                        last = nc.vector.bn_aggr(mv[:, b, :], stats[:, b, :])
                last.then_inc(stats_done, 1)
                dve.wait_ge(stats_done, NCH + 1)
                nc.vector.tensor_scalar(ve[:, :], mv[:, :, 1], EPS, None, ALU.add).then_inc(var_done, 1)
                if rows:
                    dve.wait_ge(rows_in, 32)
                    for b in range(B):
                        last = nc.vector.scalar_tensor_tensor(out=dst[:, b, :], in0=src[:, b, :], scalar=mv[:, b, 0:1],
                                                              in1=gain_bias[:, 0, :], op0=ALU.subtract, op1=ALU.mult)
                    last.then_inc(centred, 1)
                    dve.wait_ge(rstd_done, 1)
                    dve.wait_ge(centred, 1)
                    for b in range(B):
                        nc.vector.scalar_tensor_tensor(out=dst[:, b, :], in0=dst[:, b, :], scalar=rs[:, b:b + 1],
                                                       in1=gain_bias[:, 1, :], op0=ALU.mult, op1=ALU.add)
                    return
                dve.wait_ge(rstd_done, 1)
                for b in range(B):
                    nc.vector.tensor_scalar(dst[:, b, :], src[:, b, :], mv[:, b, 0:1], rs[:, b:b + 1],
                                            ALU.subtract, ALU.mult)

            @block.gpsimd
            def _(pool):
                pool.wait_ge(var_done, 1)
                nc.gpsimd.tensor_tensor(rs[:, :], ve[:, :], core.neg_half[:, :], ALU.pow).then_inc(rstd_done, 1)


def s4_kernels(core, kf, ids, free):
    nc, ins = core.nc, core.ins
    N = NL * NS
    with Stage(core, "s4k") as st:
        raw = st.sb("raw", [P, 3, N])
        skip = st.sb("skip", [P, NL])
        logs, exps = st.sb("logs", [P, N + NL]), st.sb("exps", [P, N + NL])
        small = st.sb("small", [P, 2 * N])
        whole, power_bits = st.sb("whole", [P, N + NL]), st.sb("power_bits", [P, N + NL], I32)
        expa, dt = exps[:, 0:N], exps[:, N:N + NL]
        dft = st.sb("dft", [P, 6, P])
        a_re, dta_re, dta_im = st.sb("a_re", [P, N]), st.sb("dta_re", [P, 2 * N]), st.sb("dta_im", [P, N])
        angles = flat(free[:, :, :])
        ang, red, turns = (angles[:, 5 * N * k:5 * N * (k + 1)].rearrange("p (k n) -> p k n", n=N) for k in range(3))
        trig, mag = st.sb("trig", [P, 5, N]), st.sb("mag", [P, 2, N])
        mag_m1 = st.sb("mag_m1", [P, 2 * N])
        zb = st.sb("zb", [P, 2, NB_POW, N])
        za = st.sb("za", [P, 2, NA_POW, N])
        zm = st.sb("zm", [P, 2, N])
        sq = st.sb("sq", [P, 2, N])
        tmp = st.sb("tmp", [P, 4, 8 * N])
        num = st.sb("num", [P, 2, N])
        cc = st.sb("cc", [P, 2, N])
        den = st.sb("den", [P, 2, N])
        coef = st.sb("coef", [P, 2, NA_POW, N])
        prod = tmp[:, :, :].rearrange("p k n -> p (k n)").rearrange("p (l n) -> p l n", n=2 * NS)
        ker = st.sb("ker", [P, NL, P])
        ker_t = st.sb("ker_t", [P, NL, P])
        ps_t = st.ps("ps_t", [P, NL, P])
        ps_f = st.ps("ps_f", [P, NL // G, 3, 512])
        raw_in, arg_done, trig_done, chain = (st.sem(n) for n in (
            "raw_in", "arg_done", "trig_done", "chain"))
        mul_done, ker_done, tr_done, trc_done, dft_done, kf_done = (st.sem(n) for n in (
            "mul_done", "ker_done", "tr_done", "trc_done", "dft_done", "kf_done"))
        rows_in, coef_done, pool_mul, reduced = (st.sem(n) for n in ("rows_in", "coef_done", "pool_mul", "reduced"))
        prod2 = [ap.rearrange("p (l n) -> p l n", n=2 * NS) for ap in (flat(core.x[:, :, :]), angles)]

        pool_rows = lambda a: prod2[a // 4][:, 16 * (a % 4):16 * (a % 4) + 16, :]

        def multiply(eng, to, layer):
            s = slice(layer * NS, (layer + 1) * NS)
            for a in range(NA_POW):
                for c in range(2):
                    made = eng.tensor_tensor(to(a)[:, :, c * NS:(c + 1) * NS],
                                             coef[:, c, a:a + 1, s].broadcast_to((P, NB_POW, NS)), zb[:, c, :, s], ALU.mult)
            return made

        with nc.Block() as block:
            @block.gpsimd
            def _(pool):
                for b in range(B):
                    nc.gpsimd.indirect_dma_start(core.h[:, b, :], None, ins["L0_tok_w"],
                                                 bass.IndirectOffsetOnAxis(ids[:, b:b + 1], 0)).then_inc(rows_in, 16)
                pool.wait_ge(rows_in, 16 * B)
                pool.wait_ge(coef_done, 1)
                for n, layer in enumerate(range(NL - POOL_LAYERS, NL)):
                    if n:
                        pool.wait_ge(reduced, n)
                    multiply(nc.gpsimd, pool_rows, layer).then_inc(pool_mul, 1)

            @block.sync
            def _(sp):
                for k, name in enumerate(("s4_log_A_real", "s4_A_imag", "s4_C_re", "s4_C_im")):
                    sp.dma_start((raw[:, k - 1, :] if k else logs[:, 0:N]).rearrange("p (l n) -> p l n", n=NS),
                                 ins["L0_attn_" + name].rearrange("i j h n -> h (i j) n")).then_inc(raw_in, 16)
                sp.dma_start(dft[:, :, :], ins["dft"]).then_inc(raw_in, 16)
                with nc.allow_non_contiguous_dma("one value per channel and layer"):
                    sp.dma_start(logs[:, N:N + NL], ins["L0_attn_s4_log_dt"].rearrange("i j h -> h (i j)")).then_inc(raw_in, 16)
                    sp.dma_start(skip[:, :], ins["L0_attn_s4_D"].rearrange("i j h -> h (i j)")).then_inc(raw_in, 16)
                sp.wait_ge(raw_in, 16 * 7)
                start_zeroing(core, sp)

            @block.scalar
            def _(act):
                act.wait_ge(arg_done, 1)
                nc.scalar.activation(flat(trig[:, :, :]), flat(red[:, :, :]), ACT.Sin).then_inc(trig_done, 1)
                for g in range(NL // G):
                    act.wait_ge(tr_done, G * (g + 1))
                    nc.scalar.copy(chunk(ker_t, g), chunk(ps_t, g)).then_inc(trc_done, 1)
                    act.wait_ge(dft_done, g + 1)
                    for m in range(3):
                        nc.scalar.copy(chunk(kf[:, m], g), ps_f[:, g, m, :].rearrange("p (l n) -> p l n", n=P)).then_inc(kf_done, 1)
                act.wait_ge(kf_done, 3 * NL // G)

            @block.vector
            def _(dve):
                steps = [0]

                def then(*made):
                    made[-1].then_inc(chain, 1)
                    steps[0] += 1
                    dve.wait_ge(chain, steps[0])

                tt, ts = nc.vector.tensor_tensor, nc.vector.tensor_scalar

                def cmul(out, a, b, count, negate_im=False):
                    t = [tmp[:, k, 0:count * N].rearrange("p (k n) -> p k n", n=N) for k in range(4)]
                    then(tt(t[0], a[0], b[0], ALU.mult), tt(t[1], a[1], b[1], ALU.mult),
                         tt(t[2], a[0], b[1], ALU.mult), tt(t[3], a[1], b[0], ALU.mult))
                    if negate_im:
                        then(tt(out[0], t[0], t[1], ALU.subtract), nc.vector.scalar_tensor_tensor(
                            out=out[1], in0=t[2], scalar=-1.0, in1=t[3], op0=ALU.mult, op1=ALU.subtract))
                    else:
                        then(tt(out[0], t[0], t[1], ALU.subtract), tt(out[1], t[2], t[3], ALU.add))

                def expm1(out, x):
                    y = small[:, 0:x.shape[1]]
                    then(ts(y, x, -87.0, 87.0, ALU.max, ALU.min))
                    then(ts(y, y, 1.0 / 64.0, None, ALU.mult))
                    terms = 9
                    inverse = [1.0]
                    for k in range(1, terms + 1):
                        inverse.append(inverse[-1] / k)
                    then(ts(out, y, inverse[terms], None, ALU.mult))
                    for k in range(terms - 1, 0, -1):
                        then(nc.vector.scalar_tensor_tensor(out=out, in0=out, scalar=inverse[k], in1=y,
                                                            op0=ALU.add, op1=ALU.mult))
                    for _ in range(6):
                        then(nc.vector.scalar_tensor_tensor(out=out, in0=out, scalar=2.0, in1=out,
                                                            op0=ALU.add, op1=ALU.mult))

                def exp(out, x):
                    n = x.shape[1]
                    y, k, scale = small[:, 0:n], whole[:, 0:n], power_bits[:, 0:n]
                    ln2_hi = 0.693359375
                    ln2_lo = float(np.log(2.0) - ln2_hi)
                    then(ts(y, x, -87.0, 87.0, ALU.max, ALU.min))
                    then(ts(k, y, float(1.0 / np.log(2.0)), magic, ALU.mult, ALU.add))
                    then(ts(k, k, magic, None, ALU.subtract))
                    then(ts(scale, k, 127.0, None, ALU.add))
                    then(ts(scale, scale, 23, None, ALU.logical_shift_left))
                    for part in (ln2_hi, ln2_lo):
                        then(nc.vector.scalar_tensor_tensor(out=y, in0=k, scalar=-part, in1=y,
                                                            op0=ALU.mult, op1=ALU.add))
                    terms = 9
                    inverse = [1.0]
                    for j in range(1, terms + 1):
                        inverse.append(inverse[-1] / j)
                    then(ts(out, y, inverse[terms], None, ALU.mult))
                    for j in range(terms - 1, 0, -1):
                        then(nc.vector.scalar_tensor_tensor(out=out, in0=out, scalar=inverse[j], in1=y,
                                                            op0=ALU.add, op1=ALU.mult))
                    then(nc.vector.scalar_tensor_tensor(out=out, in0=out, scalar=1.0, in1=scale.bitcast(F32),
                                                        op0=ALU.add, op1=ALU.mult))

                magic = float(1.5 * 2 ** 23)
                dve.wait_ge(raw_in, 16 * 7)
                exp(exps[:, :], logs[:, :])
                dtb = dt.unsqueeze(2).broadcast_to((P, NL, NS))
                by_layer = lambda ap: ap.rearrange("p (l n) -> p l n", n=NS)
                then(ts(a_re[:, :], expa, -1.0, None, ALU.mult),
                     tt(by_layer(dta_im[:, :]), by_layer(raw[:, 0, :]), dtb, ALU.mult))
                then(tt(by_layer(dta_re[:, 0:N]), by_layer(a_re[:, :]), dtb, ALU.mult))
                then(ts(dta_re[:, N:2 * N], dta_re[:, 0:N], float(NB_POW), None, ALU.mult))
                expm1(mag_m1[:, :], dta_re[:, :])
                ts(flat(mag[:, :, :]), mag_m1[:, :], 1.0, None, ALU.add)
                two_pi = 2.0 * np.pi
                c1 = 6.28125
                c2 = float(np.float32(np.round((two_pi - c1) * 2 ** 22) / 2 ** 22))
                c3 = float(np.float32(two_pi - c1 - c2))
                nc.vector.tensor_copy(ang[:, 0:2, :], dta_im[:, :].unsqueeze(1).broadcast_to((P, 2, N)))
                ts(ang[:, 3:5, :], dta_im[:, :].unsqueeze(1).broadcast_to((P, 2, N)), float(NB_POW), None, ALU.mult)
                then(ts(ang[:, 2, :], dta_im[:, :], 0.5, None, ALU.mult))
                then(ts(turns[:, 0, :], ang[:, 0, :], 1.0 / two_pi, 0.25, ALU.mult, ALU.add),
                     ts(turns[:, 4, :], ang[:, 4, :], 1.0 / two_pi, 0.25, ALU.mult, ALU.add),
                     ts(turns[:, 1:4, :], ang[:, 1:4, :], 1.0 / two_pi, None, ALU.mult))
                then(ts(turns[:, :, :], turns[:, :, :], magic, None, ALU.add))
                then(ts(turns[:, :, :], turns[:, :, :], magic, None, ALU.subtract))
                src = ang[:, :, :]
                for c in (c1, c2, c3):
                    then(nc.vector.scalar_tensor_tensor(out=red[:, :, :], in0=turns[:, :, :], scalar=-c, in1=src,
                                                        op0=ALU.mult, op1=ALU.add))
                    src = red[:, :, :]
                for k in (0, 4):
                    made = ts(red[:, k, :], red[:, k, :], np.pi / 2, None, ALU.add)
                then(made)
                limit = float(np.float32(3.1415925))
                ts(red[:, :, :], red[:, :, :], -limit, limit, ALU.max, ALU.min).then_inc(arg_done, 1)
                nc.vector.memset(zb[:, 0, 0, :], 1.0)
                nc.vector.memset(zb[:, 1, 0, :], 0.0)
                nc.vector.memset(za[:, 0, 0, :], 1.0)
                nc.vector.memset(za[:, 1, 0, :], 0.0)
                dve.wait_ge(trig_done, 1)
                then(tt(zb[:, :, 1, :], trig[:, 0:2, :], mag[:, 0:1, :].broadcast_to((P, 2, N)), ALU.mult),
                     tt(za[:, 0, 1, :], trig[:, 4, :], mag[:, 1, :], ALU.mult),
                     tt(za[:, 1, 1, :], trig[:, 3, :], mag[:, 1, :], ALU.mult))
                one = lambda t: (t[:, 0:1, :], t[:, 1:2, :])
                many = lambda t, lo, hi: (t[:, 0, lo:hi, :], t[:, 1, lo:hi, :])
                then(tt(sq[:, 0, :], trig[:, 2, :], trig[:, 2, :], ALU.mult),
                     tt(sq[:, 1, :], mag_m1[:, 0:N], trig[:, 0, :], ALU.mult))
                then(nc.vector.scalar_tensor_tensor(out=num[:, 0, :], in0=sq[:, 0, :], scalar=-2.0, in1=sq[:, 1, :],
                                                    op0=ALU.mult, op1=ALU.add),
                     nc.vector.tensor_copy(num[:, 1, :], zb[:, 1, 1, :]),
                     tt(den[:, 0, :], a_re[:, :], a_re[:, :], ALU.mult),
                     tt(den[:, 1, :], raw[:, 0, :], raw[:, 0, :], ALU.mult))
                then(tt(den[:, 0, :], den[:, 0, :], den[:, 1, :], ALU.add))
                then(nc.vector.reciprocal(den[:, 1, :], den[:, 0, :]))
                cmul(one(cc), one(num), (raw[:, 1:2, :], raw[:, 2:3, :]), 1)
                then(ts(sq[:, 1, :], raw[:, 0, :], -1.0, None, ALU.mult),
                     nc.vector.tensor_copy(sq[:, 0, :], a_re[:, :]))
                cmul(one(num), one(cc), one(sq), 1)
                then(nc.vector.scalar_tensor_tensor(out=cc[:, :, :], in0=num[:, :, :], scalar=2.0,
                                                    in1=den[:, 1:2, :].broadcast_to((P, 2, N)),
                                                    op0=ALU.mult, op1=ALU.mult))
                for table, size in ((zb, NB_POW), (za, NA_POW)):
                    power, m = (table[:, 0, 1:2, :], table[:, 1, 1:2, :]), 2
                    while m < size:
                        cmul(one(sq), power, power, 1)
                        then(nc.vector.tensor_copy(zm[:, :, :], sq[:, :, :]))
                        power = one(zm)
                        wide = (power[0].broadcast_to((P, m, N)), power[1].broadcast_to((P, m, N)))
                        cmul(many(table, m, 2 * m), many(table, 0, m), wide, m)
                        m *= 2
                wide = tuple(part.broadcast_to((P, NA_POW, N)) for part in one(cc))
                cmul(many(coef, 0, NA_POW), many(za, 0, NA_POW), wide, NA_POW, negate_im=True)
                nc.vector.memset(sq[:, 0, 0:1], 0.0).then_inc(coef_done, 1)

                def total(layer, products):
                    then(nc.vector.tensor_reduce(ker[:, layer, :], products[:, :, :], AX_X, ALU.add))
                    tt(ker[:, layer, 0:1], ker[:, layer, 0:1], skip[:, layer:layer + 1], ALU.add).then_inc(ker_done, 1)

                def total_of_pool(n):
                    dve.wait_ge(pool_mul, n + 1)
                    then(*[nc.vector.tensor_reduce(ker[:, own + n, P // 2 * k:P // 2 * (k + 1)], prod2[k], AX_X, ALU.add)
                           for k in range(2)])
                    nc.vector.memset(sq[:, 0, 0:1], 0.0).then_inc(reduced, 1)

                own, done = NL - POOL_LAYERS, 0
                for layer in range(own):
                    then(multiply(nc.vector, lambda a: prod[:, 16 * a:16 * a + 16, :], layer))
                    total(layer, prod)
                    if done < POOL_LAYERS - 1:
                        total_of_pool(done)
                        done += 1
                for n in range(POOL_LAYERS):
                    layer = own + n
                    if n >= done:
                        total_of_pool(n)
                    tt(ker[:, layer, 0:1], ker[:, layer, 0:1], skip[:, layer:layer + 1], ALU.add).then_inc(ker_done, 1)
                dve.wait_ge(reduced, POOL_LAYERS)

            @block.tensor
            def _(pe):
                pe.wait_ge(raw_in, 16 * 7)
                for g in range(NL // G):
                    for layer in range(G * g, G * g + G):
                        pe.wait_ge(ker_done, layer + 1)
                        nc.tensor.transpose(ps_t[:, layer, :], ker[:, layer, :], core.ident[:, :]).then_inc(tr_done, 1)
                    pe.wait_ge(trc_done, g + 1)
                    for m, table in enumerate((COS, SIN, COS_NYQ)):
                        last = nc.tensor.matmul(ps_f[:, g, m, :], dft[:, table, :], flat(chunk(ker_t, g)),
                                                start=True, stop=True)
                    last.then_inc(dft_done, 1)


class Norm:

    def __init__(self, core, st, name=""):
        self.nc, self.core = core.nc, core
        self.stats = st.sb(name + "stats", [P, 2, G, 6])
        self.mv = st.sb(name + "mv", [P, 2, G, 2])
        self.ve, self.rs = st.sb(name + "ve", [P, 2, G]), st.sb(name + "rs", [P, 2, G])
        self.turn = st.sb(name + "turn", [P, 1])
        self.stats_done, self.var_done, self.rstd_done, self.centred = (
            st.sem(name + n) for n in ("stats_done", "var_done", "rstd_done", "centred"))

    def statistics(self, dve, x, n, k, free=True):
        nc = self.nc
        for g in range(G):
            last = nc.vector.bn_stats(self.stats[:, k, g, :], x[:, g, :])
        last.then_inc(self.stats_done, 1)
        dve.wait_ge(self.stats_done, 2 * n + 1)
        nc.vector.memset(self.turn[:, :], 0.0)
        for g in range(G):
            last = nc.vector.bn_aggr(self.mv[:, k, g, :], self.stats[:, k, g, :])
        last.then_inc(self.stats_done, 1)
        dve.wait_ge(self.stats_done, 2 * n + 2)
        nc.vector.tensor_scalar(self.ve[:, k, :], self.mv[:, k, :, 1], EPS, None, ALU.add).then_inc(self.var_done, 1)

    def rstd(self, pool, n, k):
        pool.wait_ge(self.var_done, n + 1)
        self.nc.gpsimd.tensor_tensor(self.rs[:, k, :], self.ve[:, k, :], self.core.neg_half[:, 0:G],
                                     ALU.pow).then_inc(self.rstd_done, 1)

    def scale(self, dve, out, x, n, k):
        dve.wait_ge(self.rstd_done, n + 1)
        for g in range(G):
            last = self.nc.vector.tensor_scalar(out[:, g, :], x[:, g, :], self.mv[:, k, g, 0:1],
                                                self.rs[:, k, g:g + 1], ALU.subtract, ALU.mult)
        return last

    def scale_affine(self, dve, out, x, gain, bias, n, k):
        dve.wait_ge(self.rstd_done, n + 1)
        for g in range(G):
            last = self.nc.vector.scalar_tensor_tensor(out=out[:, g, :], in0=x[:, g, :],
                                                       scalar=self.mv[:, k, g, 0:1], in1=gain,
                                                       op0=ALU.subtract, op1=ALU.mult)
        last.then_inc(self.centred, 1)
        dve.wait_ge(self.centred, n + 1)
        for g in range(G):
            last = self.nc.vector.scalar_tensor_tensor(out=out[:, g, :], in0=out[:, g, :],
                                                       scalar=self.rs[:, k, g:g + 1], in1=bias,
                                                       op0=ALU.mult, op1=ALU.add)
        return last


def steps(eng, lo, hi, body):
    assert lo % 2 == 0
    pairs = (hi - lo) // 2
    if pairs == 1:
        body(lo, 0)
        body(lo + 1, 1)
    elif pairs > 1:
        with eng.Fori(0, pairs) as pair:
            body(pair * 2 + lo, 0)
            body(pair * 2 + (lo + 1), 1)
    if (hi - lo) % 2:
        body(hi - 1, 0)


def stage_l0_attn(core, kf, u):
    nc, ins = core.nc, core.ins
    with Stage(core, "l0a") as st:
        dft = st.sb("dft", [P, 6, P])
        out_w = st.sb("out_w", [P, NL, 2 * P])
        out_b = st.sb("out_b", [P, NL, 2 * P])
        norm_rows = st.sb("norm_rows", [P, 2, DEPTH, P])
        norm_cols = st.sb("norm_cols", [P, 2, DEPTH])
        ff_b2 = st.sb("ff_b2", [P, DEPTH, P])
        ff_b1 = st.sb("ff_b1", [P, DEPTH, 8])
        weights_in, halved = st.sem("weights_in"), st.sem("halved")
        with nc.Block() as block:
            @block.sync
            def _(sp):
                sp.dma_start(dft[:, :, :], ins["dft"]).then_inc(weights_in, 16)
                sp.dma_start(out_w[:, :, :], ins["s4_out_wT"]).then_inc(weights_in, 16)
                sp.dma_start(out_b[:, :, :], ins["L0_attn_s4_out_b"].rearrange("i j n -> (i j) n").partition_broadcast(P)).then_inc(weights_in, 16)
                for k, name in enumerate(("L0_attn_ln1_w", "L0_attn_ln1_b")):
                    sp.dma_start(norm_rows[:, k, :, :], ins[name].partition_broadcast(P)).then_inc(weights_in, 16)
                sp.dma_start(ff_b2[:, :, :], ins["L0_attn_ff_b2"].partition_broadcast(P)).then_inc(weights_in, 16)
                with nc.allow_non_contiguous_dma("one value per feature"):
                    for k, name in enumerate(("L0_attn_ln2_w", "L0_attn_ln2_b")):
                        sp.dma_start(norm_cols[:, k, :], ins[name].rearrange("d n -> n d")).then_inc(weights_in, 16)
                    for d in range(DEPTH):
                        sp.dma_start(ff_b1[:, d, :], ins["L0_attn_ff_b1"][d].rearrange("(m n) -> n m", n=P)).then_inc(weights_in, 16)

        stage_norm(core, "n0")
        with nc.Block() as block:
            @block.vector
            def _(dve):
                dve.wait_ge(weights_in, 16 * (8 + DEPTH))
                nc.vector.tensor_scalar(out_w[:, :, 0:P], out_w[:, :, 0:P], 0.5, None, ALU.mult).then_inc(halved, 1)
                nc.vector.tensor_scalar(out_b[:, :, 0:P], out_b[:, :, 0:P], 0.5, None, ALU.mult).then_inc(halved, 1)
                dve.wait_ge(halved, 2)

        ps_a, ps_t, ps_o = st.ps("ps_a", [P, 2, 2, 512]), st.ps("ps_t", [P, 2, 512]), st.ps("ps_o", [P, 2, 512])
        s4 = S4Pair(core, st, u, dft, kf, out_w, out_b, norm_rows, ps_a, ps_t, ps_o)
        ff = FeedForward(core, st, u, norm_cols, ff_b1, ff_b2, ps_a, ps_t, ps_o)
        s4.ff, ff.s4 = ff, s4
        with nc.Block() as block:
            @block.sync
            def _(sp):
                for d in range(DEPTH):
                    ff.load(sp, d)

            @block.tensor
            def _(pe):
                for d in range(DEPTH):
                    s4.tensor(pe, d)
                    ff.tensor(pe, d)

            @block.scalar
            def _(act):
                for d in range(DEPTH):
                    s4.scalar(act, d)
                    ff.scalar(act, d)

            @block.gpsimd
            def _(pool):
                for d in range(DEPTH):
                    s4.gpsimd(pool, d)
                    ff.gpsimd(pool, d)

            @block.vector
            def _(dve):
                for d in range(DEPTH):
                    s4.vector(dve, d)
                    ff.vector(dve, d)
                dve.wait_ge(ff.res_done, NCH * DEPTH)


S4_STEPS = 2 * NCH


def late(i, n, before=0):
    return not isinstance(i, int) or before + i >= n


class S4Pair:

    def __init__(self, core, st, u, dft, kf, out_w, out_b, norm_rows, ps_ri, ps_y, ps_z):
        self.nc, self.core, self.u, self.dft, self.kf = core.nc, core, u, dft, kf
        self.out_w, self.out_b, self.norm_rows = out_w, out_b, norm_rows
        self.ps_ri, self.ps_y, self.ps_z = ps_ri, ps_y, ps_z
        self.norm = Norm(core, st, "s4")
        self.prods = st.sb("prods", [P, 2, 4, G, P])
        self.spec = st.sb("spec", [P, 2, 2, G, P])
        self.gel = st.sb("gel", [P, 2, G, P])
        self.z = st.sb("z", [P, 2, G, 2 * P])
        self.th = st.sb("th", [P, 2, G, P])
        (self.normed, self.dft_done, self.prod_done, self.spec_done, self.inv_done, self.gelu_done, self.proj_done,
         self.z_done, self.tanh_done, self.glu_done) = (st.sem(n) for n in (
             "normed", "dft_done", "prod_done", "spec_done", "inv_done", "gelu_done", "proj_done",
             "z_done", "tanh_done", "glu_done"))


    def forward(self, pe, d, i, k):
        nc, base = self.nc, S4_STEPS * d
        if isinstance(i, int) and i < NCH:
            pe.wait_ge(self.normed, NCH * d + i + 1)
        else:
            pe.wait_ge(self.glu_done, base + i - NCH + 1)
        if late(i, 2, base):
            pe.wait_ge(self.prod_done, base + i - 1)
        if d and not late(i, 2):
            pe.wait_ge(self.ff.mid_done, 4 * NCH * d - 1 + i)
        for m, table in enumerate((COS, SIN_NYQ)):
            last = nc.tensor.matmul(self.ps_ri[:, k, m, :], self.dft[:, table, :], flat(chunk(self.u, i & (NCH - 1))),
                                    start=True, stop=True)
        last.then_inc(self.dft_done, 1)

    def inverse(self, pe, d, i, k):
        nc, base = self.nc, S4_STEPS * d
        pe.wait_ge(self.spec_done, base + i + 1)
        if late(i, 2, base):
            pe.wait_ge(self.gelu_done, base + i - 1)
        if d and not late(i, 2):
            pe.wait_ge(self.ff.xt_done, NCH * d - 1 + i)
        for g in range(G):
            for m, table in enumerate((INV_COS, INV_SIN)):
                last = nc.tensor.matmul(self.ps_y[:, k, P * g:P * g + P], self.spec[:, k, m, g, :],
                                        self.dft[:, table, :], start=(m == 0), stop=(m == 1))
        last.then_inc(self.inv_done, 1)

    def project(self, pe, d, i, k):
        nc, base = self.nc, S4_STEPS * d
        pe.wait_ge(self.gelu_done, base + i + 1)
        if late(i, 1, base):
            pe.wait_ge(self.z_done, base + i)
        if d and not late(i, 1):
            pe.wait_ge(self.ff.res_done, NCH * d)
        layer = (i & (S4_STEPS - 1)) // NCH + 2 * d
        for g in range(G):
            last = nc.tensor.matmul(self.ps_z[:, g // 2, 2 * P * (g % 2):2 * P * (g % 2) + 2 * P],
                                    self.gel[:, k, g, :], self.out_w[:, bass.ds(layer, 1), :], start=True, stop=True)
        last.then_inc(self.proj_done, 1)

    def tensor(self, pe, d):
        def body(i, k):
            self.forward(pe, d, i, k)
            self.inverse(pe, d, i - 1, 1 - k)
            self.project(pe, d, i - 2, k)

        if d == 0:
            self.forward(pe, d, 0, 0)
            self.forward(pe, d, 1, 1)
        self.inverse(pe, d, 0, 0)
        for i in range(2, NCH):
            body(i, i % 2)
        steps(pe, NCH, S4_STEPS, body)
        self.inverse(pe, d, S4_STEPS - 1, 1)
        self.project(pe, d, S4_STEPS - 2, 0)
        self.ff.transpose(pe, d, 0)
        self.project(pe, d, S4_STEPS - 1, 1)


    def statistics(self, dve, d, i):
        if d:
            dve.wait_ge(self.ff.res_done, NCH * (d - 1) + i + 1)
        self.norm.statistics(dve, chunk(self.core.x, i), NCH * d + i, i % 2)

    def scale(self, dve, d, i):
        self.norm.scale_affine(dve, chunk(self.u, i), chunk(self.core.x, i), self.norm_rows[:, 0, d, :],
                               self.norm_rows[:, 1, d, :], NCH * d + i, i % 2).then_inc(self.normed, 1)

    def begin(self, dve, d):
        self.scale(dve, d, 1)
        self.statistics(dve, d, 2)
        self.product(dve, d, 0, 0)

    def product(self, dve, d, i, k):
        base = S4_STEPS * d
        dve.wait_ge(self.dft_done, base + i + 1)
        if late(i, 2, base):
            dve.wait_ge(self.spec_done, base + i - 1)
        layer = (i & (S4_STEPS - 1)) // NCH + 2 * d
        part = lambda m: self.kf[:, m, bass.ds(layer, 1), :].broadcast_to((P, G, P))
        for n, (m, c) in enumerate(((0, 0), (1, 1), (0, 1), (1, 2))):
            last = self.nc.vector.tensor_tensor(self.prods[:, k, n, :, :],
                                                self.ps_ri[:, k, m, :].rearrange("p (g n) -> p g n", n=P), part(c), ALU.mult)
        last.then_inc(self.prod_done, 1)

    def add_bias(self, dve, d, i, k):
        base = S4_STEPS * d
        dve.wait_ge(self.proj_done, base + i + 1)
        if late(i, 2, base):
            dve.wait_ge(self.tanh_done, base + i - 1)
        layer = (i & (S4_STEPS - 1)) // NCH + 2 * d
        self.nc.vector.tensor_tensor(self.z[:, k, :, :], self.ps_z[:, :, :].rearrange("p a (b n) -> p (a b) n", n=2 * P),
                                     self.out_b[:, bass.ds(layer, 1), :].broadcast_to((P, G, 2 * P)),
                                     ALU.add).then_inc(self.z_done, 1)

    def gate(self, dve, d, i, k):
        dve.wait_ge(self.tanh_done, S4_STEPS * d + i + 1)
        self.nc.vector.scalar_tensor_tensor(out=chunk(self.u, i & (NCH - 1)), in0=self.th[:, k, :, :], scalar=1.0,
                                            in1=self.z[:, k, :, 0:P], op0=ALU.add,
                                            op1=ALU.mult).then_inc(self.glu_done, 1)

    def vector(self, dve, d):
        N = S4_STEPS

        def body(i, k):
            self.product(dve, d, i, k)
            self.gate(dve, d, i - 3, 1 - k)
            self.add_bias(dve, d, i - 2, k)

        if d == 0:
            self.statistics(dve, d, 0)
            self.scale(dve, d, 0)
            self.statistics(dve, d, 1)
            self.begin(dve, d)
        for i in range(1, NCH):
            if i + 1 < NCH:
                self.scale(dve, d, i + 1)
            if i + 2 < NCH:
                self.statistics(dve, d, i + 2)
            self.product(dve, d, i, i % 2)
            if i >= 3:
                self.gate(dve, d, i - 3, (i - 3) % 2)
            if i >= 2:
                self.add_bias(dve, d, i - 2, i % 2)
        steps(dve, NCH, N - 2, body)
        body(N - 2, 0)
        self.product(dve, d, N - 1, 1)
        self.ff.statistics(dve, d, 0)
        self.gate(dve, d, N - 4, 0)
        self.add_bias(dve, d, N - 3, 1)
        self.ff.scale(dve, d, 0)
        self.gate(dve, d, N - 3, 1)
        self.add_bias(dve, d, N - 2, 0)
        self.ff.statistics(dve, d, 1)
        self.gate(dve, d, N - 2, 0)
        self.add_bias(dve, d, N - 1, 1)
        self.gate(dve, d, N - 1, 1)


    def gpsimd(self, pool, d):
        nc, base, norm = self.nc, S4_STEPS * d, self.norm

        def total(i, k):
            pool.wait_ge(self.prod_done, base + i + 1)
            if late(i, 2, base):
                pool.wait_ge(self.inv_done, base + i - 1)
            nc.gpsimd.tensor_tensor(self.spec[:, k, 0, :, :], self.prods[:, k, 0, :, :],
                                    self.prods[:, k, 1, :, :], ALU.subtract)
            nc.gpsimd.tensor_tensor(self.spec[:, k, 1, :, :], self.prods[:, k, 2, :, :],
                                    self.prods[:, k, 3, :, :], ALU.add).then_inc(self.spec_done, 1)

        norm.rstd(pool, NCH * d, 0)
        norm.rstd(pool, NCH * d + 1, 1)
        for i in range(NCH):
            if i + 2 < NCH:
                norm.rstd(pool, NCH * d + i + 2, i % 2)
            total(i, i % 2)
        steps(pool, NCH, S4_STEPS - 2, total)
        total(S4_STEPS - 2, 0)
        self.ff.add_s4(pool, d, 0)
        total(S4_STEPS - 1, 1)


    def scalar(self, act, d):
        nc, base = self.nc, S4_STEPS * d

        def gelu(i, k):
            act.wait_ge(self.inv_done, base + i + 1)
            if late(i, 2, base):
                act.wait_ge(self.proj_done, base + i - 1)
            nc.scalar.activation(flat(self.gel[:, k, :, :]), self.ps_y[:, k, :],
                                 ACT.Gelu_apprx_tanh).then_inc(self.gelu_done, 1)

        def tanh(i, k):
            act.wait_ge(self.z_done, base + i + 1)
            if late(i, 2, base):
                act.wait_ge(self.glu_done, base + i - 1)
            nc.scalar.activation(self.th[:, k, :, :], self.z[:, k, :, P:2 * P], ACT.Tanh,
                                 scale=0.5).then_inc(self.tanh_done, 1)

        def body(i, k):
            gelu(i, k)
            tanh(i - 1, 1 - k)

        gelu(0, 0)
        gelu(1, 1)
        tanh(0, 0)
        steps(act, 2, S4_STEPS, body)
        self.ff.copy_t(act, d, 0)
        tanh(S4_STEPS - 1, 1)


class FeedForward:

    def __init__(self, core, st, u, norm_cols, b1, b2, ps_u, ps_t, ps_o):
        self.nc, self.core, self.u, self.norm_cols, self.b1, self.b2 = core.nc, core, u, norm_cols, b1, b2
        self.ps_u, self.ps_t, self.ps_o = ps_u, ps_t, ps_o
        self.norm = Norm(core, st, "ff")
        self.first, self.second = Norm(core, st, "first"), Norm(core, st, "second")
        self.h_done, self.x_done, self.u_done = (st.sem("ff_" + n) for n in ("h_done", "x_done", "u_done"))
        self.w1 = st.sb("w1", [P, 8 * P])
        self.w2 = st.sb("w2", [P, 4, P])
        self.xn = st.sb("xn", [P, 2, G, P])
        self.xt = st.sb("xt", [P, 2, W])
        self.sg = st.sb("sg", [P, 2, W])
        self.mid = st.sb("mid", [P, 2, 4, W])
        (self.w_in, self.xadd_done, self.normed, self.tr_done, self.xt_done, self.up_done, self.silu_done,
         self.mid_done, self.b2_done, self.down_done, self.res_done) = (st.sem("ff_" + n) for n in (
             "w_in", "xadd_done", "normed", "tr_done", "xt_done", "up_done", "silu_done", "mid_done", "b2_done",
             "down_done", "res_done"))

    def load(self, sp, d):
        if d:
            sp.wait_ge(self.down_done, NCH * d)
        sp.dma_start(self.w1[:, :], self.core.ins["ff_w1T"][d]).then_inc(self.w_in, 16)
        sp.dma_start(self.w2[:, :, :], self.core.ins["ff_w2T"][d]).then_inc(self.w_in, 16)


    def add_s4(self, pool, d, i):
        pool.wait_ge(self.s4.glu_done, S4_STEPS * d + NCH + i + 1)
        self.nc.gpsimd.tensor_tensor(chunk(self.core.x, i), chunk(self.core.x, i), chunk(self.u, i),
                                     ALU.add).then_inc(self.xadd_done, 1)

    def gpsimd(self, pool, d):
        nc, core, base = self.nc, self.core, NCH * d

        def add_b2(i):
            pool.wait_ge(self.normed, base + i + 1)
            nc.gpsimd.tensor_tensor(chunk(core.x, i), chunk(core.x, i),
                                    self.b2[:, d:d + 1, :].broadcast_to((P, G, P)),
                                    ALU.add).then_inc(self.b2_done, 1)

        for i in range(NCH + 5 if d == DEPTH - 1 else NCH + 1):
            if i < NCH:
                if i:
                    self.add_s4(pool, d, i)
                self.norm.rstd(pool, base + i, i % 2)
            if 1 <= i <= NCH:
                add_b2(i - 1)
            if d == DEPTH - 1:
                if 0 <= i - 3 < NCH:
                    pool.wait_ge(self.res_done, base + i - 2)
                    nc.gpsimd.tensor_tensor(chunk(core.h, i - 3), chunk(core.h, i - 3), chunk(core.x, i - 3),
                                            ALU.add).then_inc(self.h_done, 1)
                if 0 <= i - 4 < NCH:
                    self.first.rstd(pool, i - 4, i % 2)
                if 0 <= i - 5 < NCH:
                    self.second.rstd(pool, i - 5, (i - 5) % 2)


    def statistics(self, dve, d, i):
        dve.wait_ge(self.xadd_done, NCH * d + i + 1)
        self.norm.statistics(dve, chunk(self.core.x, i), NCH * d + i, i % 2)

    def scale(self, dve, d, i):
        base = NCH * d
        if base + i >= 2:
            dve.wait_ge(self.tr_done, base + i - 1)
        self.norm.scale(dve, self.xn[:, i % 2, :, :], chunk(self.core.x, i), base + i, i % 2).then_inc(self.normed, 1)

    def vector(self, dve, d):
        nc, core, base = self.nc, self.core, NCH * d

        def gate(i, m):
            q, t = 4 * (base + i) + m, m % 2
            dve.wait_ge(self.silu_done, q + 1)
            if m == 0 and base + i >= 2:
                dve.wait_ge(self.down_done, base + i - 1)
            nc.vector.scalar_tensor_tensor(out=self.mid[:, i % 2, m, :], in0=self.ps_u[:, t, 0, :],
                                           scalar=self.b1[:, d, m:m + 1], in1=self.sg[:, t, :],
                                           op0=ALU.add, op1=ALU.mult).then_inc(self.mid_done, 1)

        def residual(i):
            dve.wait_ge(self.down_done, base + i + 1)
            dve.wait_ge(self.b2_done, base + i + 1)
            nc.vector.tensor_tensor(chunk(core.x, i), self.ps_o[:, i % 2, :].rearrange("p (g n) -> p g n", n=P),
                                    chunk(core.x, i), ALU.add).then_inc(self.res_done, 1)

        def follow(i, part):
            first, second = self.first, self.second
            if d < DEPTH - 1:
                return
            if part == 0 and 0 <= i - 2 < NCH:
                dve.wait_ge(self.h_done, i - 1)
                first.statistics(dve, chunk(core.h, i - 2), i - 2, i % 2)
            if part == 1 and 0 <= i - 3 < NCH:
                first.scale(dve, chunk(core.x, i - 3), chunk(core.h, i - 3), i - 3, (i - 3) % 2).then_inc(self.x_done, 1)
                dve.wait_ge(self.x_done, i - 2)
                second.statistics(dve, chunk(core.x, i - 3), i - 3, (i - 3) % 2)
            if part == 2 and 0 <= i - 4 < NCH:
                second.scale(dve, chunk(self.u, i - 4), chunk(core.x, i - 4), i - 4, i % 2).then_inc(self.u_done, 1)

        for i in range(NCH):
            gate(i, 0)
            if i + 1 < NCH:
                self.scale(dve, d, i + 1)
            gate(i, 1)
            if i + 2 < NCH:
                self.statistics(dve, d, i + 2)
            if i >= 1:
                residual(i - 1)
            follow(i, 0)
            gate(i, 2)
            follow(i, 1)
            if d + 1 < DEPTH and i == NCH - 1:
                self.s4.scale(dve, d + 1, 0)
            gate(i, 3)
            follow(i, 2)
            if d + 1 < DEPTH and i >= NCH - 2:
                self.s4.statistics(dve, d + 1, i - (NCH - 2))
        if d + 1 < DEPTH:
            self.s4.begin(dve, d + 1)
        residual(NCH - 1)
        if d == DEPTH - 1:
            for i in range(NCH, NCH + 4):
                for part in range(3):
                    follow(i, part)
            dve.wait_ge(self.u_done, NCH)


    def copy_t(self, act, d, i):
        base = NCH * d
        act.wait_ge(self.tr_done, base + i + 1)
        if base + i >= 2:
            act.wait_ge(self.up_done, 4 * (base + i - 1))
        self.nc.scalar.activation(self.xt[:, i % 2, :], self.ps_t[:, i % 2, :], ACT.Identity,
                                  bias=self.norm_cols[:, 1, d:d + 1],
                                  scale=self.norm_cols[:, 0, d:d + 1]).then_inc(self.xt_done, 1)

    def scalar(self, act, d):
        nc, base = self.nc, NCH * d

        def silu(i, m):
            q, t = 4 * (base + i) + m, m % 2
            act.wait_ge(self.up_done, q + 1)
            if q >= 2:
                act.wait_ge(self.mid_done, q - 1)
            nc.scalar.activation(self.sg[:, t, :], self.ps_u[:, t, 1, :], ACT.Silu,
                                 bias=self.b1[:, d, 4 + m:5 + m]).then_inc(self.silu_done, 1)

        for i in range(NCH):
            silu(i, 0)
            silu(i, 1)
            if i + 1 < NCH:
                self.copy_t(act, d, i + 1)
            silu(i, 2)
            silu(i, 3)


    def transpose(self, pe, d, i):
        base = NCH * d
        pe.wait_ge(self.normed, base + i + 1)
        if base + i >= 2:
            pe.wait_ge(self.xt_done, base + i - 1)
        if i < 2:
            pe.wait_ge(self.s4.gelu_done, S4_STEPS * (d + 1) - 1 + i)
        for g in range(G):
            last = self.nc.tensor.transpose(self.ps_t[:, i % 2, P * g:P * g + P], self.xn[:, i % 2, g, :],
                                            self.core.ident[:, :])
        last.then_inc(self.tr_done, 1)

    def tensor(self, pe, d):
        nc, base = self.nc, NCH * d

        def up(i, m):
            q, t = 4 * (base + i) + m, m % 2
            if m == 0:
                pe.wait_ge(self.xt_done, base + i + 1)
            if q >= 2:
                pe.wait_ge(self.mid_done, q - 1)
            if i == 0 and m < 2:
                pe.wait_ge(self.s4.prod_done, S4_STEPS * (d + 1) - 1 + m)
            for part in range(2):
                col = P * (4 * part + m)
                last = nc.tensor.matmul(self.ps_u[:, t, part, :], self.w1[:, col:col + P], self.xt[:, i % 2, :],
                                        start=True, stop=True)
            last.then_inc(self.up_done, 1)

        def down(i):
            pe.wait_ge(self.mid_done, 4 * (base + i) + 4)
            if base + i >= 2:
                pe.wait_ge(self.res_done, base + i - 1)
            if i == 0:
                pe.wait_ge(self.s4.z_done, S4_STEPS * (d + 1))
            for g in range(G):
                for m in range(4):
                    last = nc.tensor.matmul(self.ps_o[:, i % 2, P * g:P * g + P],
                                            self.mid[:, i % 2, m, P * g:P * g + P], self.w2[:, m, :],
                                            start=(m == 0), stop=(m == 3))
            last.then_inc(self.down_done, 1)

        pe.wait_ge(self.w_in, 32 * (d + 1))
        for i in range(NCH):
            up(i, 0)
            up(i, 1)
            if i + 1 < NCH:
                self.transpose(pe, d, i + 1)
            if i >= 1:
                down(i - 1)
            up(i, 2)
            up(i, 3)
        if d + 1 < DEPTH:
            self.s4.forward(pe, d + 1, 0, 0)
            self.s4.forward(pe, d + 1, 1, 1)
        down(NCH - 1)


UNIT = HEADS // 2


def bank4(ap):
    return ap.rearrange("p (g n) -> p g n", n=P)


class Attention:

    def __init__(self, core, name, src, wq, wk, wv, softmax, scale, wo=None, bq=None, bk=None, bv=None, bo=None,
                 affine=None, wg=None, bg=None, dst=None, sums=None, norm=None, source=None):
        self.norm_to, self.norm_rows = norm or (None, ())
        self.source = source
        self.dst, self.sums = dst, sums
        self.core, self.name, self.src = core, name, src
        self.w_names = [n for n in (wq, wk, wv, wo, wg) if n]
        self.wq, self.wk, self.wv, self.wo, self.wg = wq, wk, wv, wo, wg
        self.softmax, self.att_scale = softmax, scale
        self.bq, self.bk, self.bv, self.bo, self.bg, self.affine = bq, bk, bv, bo, bg, affine

    def run(self):
        core, nc, ins = self.core, self.core.nc, self.core.ins
        softmax, src = self.softmax, self.src
        NU = 2 * B
        with Stage(core, self.name) as st:
            sem = {n: st.sem(n) for n in (
                "w_in", "x_tr", "xt", "q_mm", "q", "k_mm", "k", "v_mm", "v", "spread", "score", "score_read",
                "max", "exp", "p_tr", "pt", "pv", "rz", "o", "o_tr", "ot", "out_mm", "out", "bo",
                "g_mm", "gate", "ones", "weighted", "summed")}
            w = {n: st.sb("w" + str(i), [P, P]) for i, n in enumerate(self.w_names)}
            head_mask = st.sb("head_mask", [P, HEADS])
            cols = st.sb("cols", [P, 4])
            rows = st.sb("rows", [P, 3, P])
            xt, qt, kt = (st.sb(n, [P, 2, W]) for n in ("xt", "qt", "kt"))
            v = st.sb("v", [P, 2, G, HEADS, HD + 1])
            spread = st.sb("spread", [P, 2, HEADS, P])
            pr = st.sb("pr", [P, 2, UNIT, P])
            o, ot = st.sb("o", [P, 2, G, P]), st.sb("ot", [P, 2, W])
            if softmax:
                mx, rz = st.sb("mx", [P, 2, UNIT]), st.sb("rz", [P, 2, HEADS])
                shifted, pt = st.sb("shifted", [P, 2, UNIT, P]), st.sb("pt", [P, 2, UNIT, P])
            else:
                decay = st.sb("decay", [P, HEADS, P])
                gate = st.sb("gate", [P, 2, G, P])
                gpre = st.sb("gpre", [P, G, P])
            if self.sums:
                weighted = st.sb("weighted", [P, 2, UNIT, P])
            ps_s, ps_o, ps_m = st.ps("ps_s", [P, 2, 512]), st.ps("ps_o", [P, 2, 512]), st.ps("ps_m", [P, 2, 512])
            ps_p = st.ps("ps_p", [P, 2, 512])
            col_names = [n for n in (self.bq, self.bk) if n] + (list(self.affine) if self.affine else [])
            row_names = [n for n in (self.bv, self.bo, self.bg) if n]
            row = {n: rows[:, i:i + 1, :] for i, n in enumerate(row_names)}
            col = {n: cols[:, i:i + 1] for i, n in enumerate(col_names)}
            loads = len(w) + 1 + len(col_names) + len(row_names) + (not softmax)
            values = HD + 1 if softmax else HD
            stationary, moving = (qt, kt) if softmax else (kt, qt)

            if self.norm_to is not None:
                norm, normed = Norm(core, st, "n"), st.sem("normed")
                norm_rows = st.sb("norm_rows", [P, 2, P])
                stream = core.x if self.wo else core.h
                loads += len(self.norm_rows)

            source = Combine(core, st, self.source) if self.source else None

            with nc.Block() as block:
                @block.sync
                def _(sp):
                    for i, n in enumerate(self.norm_rows):
                        sp.dma_start(norm_rows[:, i, :], ins[n].partition_broadcast(P)).then_inc(sem["w_in"], 16)
                    for n in self.w_names:
                        sp.dma_start(w[n][:, :], ins[n]).then_inc(sem["w_in"], 16)
                    sp.dma_start(head_mask[:, :], ins["head_mask"]).then_inc(sem["w_in"], 16)
                    with nc.allow_non_contiguous_dma("one value per feature"):
                        for n in col_names:
                            sp.dma_start(col[n], ins[n].unsqueeze(1)).then_inc(sem["w_in"], 16)
                    for n in row_names:
                        sp.dma_start(row[n], ins[n].unsqueeze(0).partition_broadcast(P)).then_inc(sem["w_in"], 16)
                    if not softmax:
                        sp.dma_start(decay[:, :, :], ins["decay"]).then_inc(sem["w_in"], 16)
                    if source:
                        source.sync(sp)
                    sp.wait_ge(sem["w_in"], 16 * loads)

                @block.tensor
                def _(pe):
                    mm, tr = nc.tensor.matmul, nc.tensor.transpose

                    def transpose_x(c):
                        if source:
                            pe.wait_ge(source.ready, c + 1)
                        if c >= 1:
                            pe.wait_ge(sem["k"], c)
                        if self.wo and c >= 3:
                            pe.wait_ge(sem["ot"], c - 2)
                        for g in range(G):
                            last = tr(ps_m[:, 0, P * g:P * g + P], src[:, G * c + g, :], core.ident[:, :])
                        last.then_inc(sem["x_tr"], 1)

                    def project_q(c):
                        pe.wait_ge(sem["xt"], c + 1)
                        if c == 0:
                            pe.wait_ge(sem["w_in"], 16 * loads)
                        if c >= 1:
                            pe.wait_ge(sem["v"], c)
                        if self.wo and c >= 3:
                            pe.wait_ge(sem["out"], c - 2)
                        mm(ps_m[:, 1, :], w[self.wq][:, :], xt[:, c % 2, :], start=True, stop=True).then_inc(sem["q_mm"], 1)

                    def project_k(c):
                        mm(ps_m[:, 0, :], w[self.wk][:, :], xt[:, c % 2, :], start=True, stop=True).then_inc(sem["k_mm"], 1)

                    def project_v(c):
                        pe.wait_ge(sem["q"], c + 1)
                        for g in range(G):
                            last = mm(ps_m[:, 1, P * g:P * g + P], xt[:, c % 2, P * g:P * g + P], w[self.wv][:, :],
                                      start=True, stop=True)
                        last.then_inc(sem["v_mm"], 1)

                    def project_gate(c):
                        if c >= 2:
                            pe.wait_ge(sem["gate"], c - 1)
                        for g in range(G):
                            last = mm(ps_p[:, c % 2, P * g:P * g + P], xt[:, c % 2, P * g:P * g + P],
                                      w[self.wg][:, :], start=True, stop=True)
                        last.then_inc(sem["g_mm"], 1)

                    def scores(n):
                        b, half = n // 2, n % 2
                        pe.wait_ge(sem["spread"], b + 1)
                        if n >= 2:
                            pe.wait_ge(sem["score_read"], n - 1)
                        if half == 0:
                            pe.wait_ge(sem["q" if softmax else "k"], b // G + 1)
                        mm(ps_s[:, half, :], stationary[:, b // G % 2, P * (b % G):P * (b % G) + P],
                           spread[:, b % 2, UNIT * half:UNIT * half + UNIT, :], start=True, stop=True).then_inc(sem["score"], 1)

                    def transpose_p(n):
                        pe.wait_ge(sem["exp"], n + 1)
                        if n >= 2:
                            pe.wait_ge(sem["pt"], n - 1)
                        for j in range(UNIT):
                            last = tr(ps_p[:, n % 2, P * j:P * j + P], pr[:, n % 2, j, :], core.ident[:, :])
                        last.then_inc(sem["p_tr"], 1)

                    def value_product(n):
                        b, half = n // 2, n % 2
                        pe.wait_ge(sem["pt" if softmax else "score_read"], n + 1)
                        pe.wait_ge(sem["v"], b // G + 1)
                        if half == 0 and b >= 2:
                            pe.wait_ge(sem["o"], b - 1)
                        left = pt if softmax else pr
                        for j in range(UNIT):
                            head = UNIT * half + j
                            last = mm(ps_o[:, b % 2, values * head:values * head + values], left[:, n % 2, j, :],
                                      v[:, b // G % 2, b % G, head, 0:values], start=True, stop=True)
                        last.then_inc(sem["pv"], 1)

                    def transpose_o(c):
                        pe.wait_ge(sem["o"], G * (c + 1))
                        pe.wait_ge(sem["k"], min(c + 3, NCH))
                        if c >= 1:
                            pe.wait_ge(sem["ot"], c)
                        for g in range(G):
                            last = tr(ps_m[:, 0, P * g:P * g + P], o[:, c % 2, g, :], core.ident[:, :])
                        last.then_inc(sem["o_tr"], 1)

                    def project_out(c):
                        pe.wait_ge(sem["ot"], c + 1)
                        pe.wait_ge(sem["v"], min(c + 3, NCH))
                        if c >= 1:
                            pe.wait_ge(sem["out"], c)
                        for g in range(G):
                            last = mm(ps_m[:, 1, P * g:P * g + P], ot[:, c % 2, P * g:P * g + P], w[self.wo][:, :],
                                      start=True, stop=True)
                        last.then_inc(sem["out_mm"], 1)

                    def ahead(c, k):
                        if c < NCH:
                            if k == 0:
                                transpose_x(c)
                            elif k == 1:
                                project_q(c)
                            elif k == 2:
                                project_k(c)
                            elif k == 3:
                                project_v(c)
                                if self.wg:
                                    project_gate(c)

                    for k in range(4):
                        ahead(0, k)
                    lag = 3 if softmax else 2
                    for n in range(NU + lag):
                        c, k = n // (2 * G), n % (2 * G)
                        if n < NU:
                            scores(n)
                            ahead(c + 1, k)
                        if softmax and 0 <= n - 2 < NU:
                            transpose_p(n - 2)
                        if 0 <= n - lag < NU:
                            value_product(n - lag)
                        if self.wo and k == 5 and 1 <= c:
                            transpose_o(c - 1)
                        if self.wo and k == 6 and 1 <= c:
                            project_out(c - 1)
                    if self.wo:
                        transpose_o(NCH - 1)
                        project_out(NCH - 1)

                @block.scalar
                def _(act):
                    act.wait_ge(sem["w_in"], 16 * loads)

                    def copy_xt(c):
                        act.wait_ge(sem["x_tr"], c + 1)
                        if c >= 2:
                            act.wait_ge(sem["v_mm"], c - 1)
                            if self.wg:
                                act.wait_ge(sem["g_mm"], c - 1)
                        if self.affine:
                            nc.scalar.activation(xt[:, c % 2, :], ps_m[:, 0, :], ACT.Identity, bias=col[self.affine[1]],
                                                 scale=col[self.affine[0]]).then_inc(sem["xt"], 1)
                        else:
                            nc.scalar.copy(xt[:, c % 2, :], ps_m[:, 0, :]).then_inc(sem["xt"], 1)

                    def copy_q(c, what, bank, bias, to, is_stationary):
                        act.wait_ge(sem[what + "_mm"], c + 1)
                        if c >= 2:
                            if is_stationary:
                                act.wait_ge(sem["score"], 2 * G * (c - 1))
                            else:
                                act.wait_ge(sem["spread"], G * (c - 1))
                        if bias:
                            nc.scalar.activation(to[:, c % 2, :], ps_m[:, bank, :], ACT.Identity,
                                                 bias=col[bias]).then_inc(sem[what], 1)
                        else:
                            nc.scalar.copy(to[:, c % 2, :], ps_m[:, bank, :]).then_inc(sem[what], 1)

                    def exponentials(n):
                        act.wait_ge(sem["score_read"], n + 1)
                        if n >= 2:
                            act.wait_ge(sem["p_tr"], n - 1)
                            if self.sums:
                                act.wait_ge(sem["weighted"], n - 1)
                        nc.scalar.activation(pr[:, n % 2, :, :], shifted[:, n % 2, :, :], ACT.Exp,
                                             scale=self.att_scale).then_inc(sem["exp"], 1)

                    def copy_pt(n):
                        act.wait_ge(sem["p_tr"], n + 1)
                        if n >= 2:
                            act.wait_ge(sem["pv"], n - 1)
                        nc.scalar.copy(flat(pt[:, n % 2, :, :]), ps_p[:, n % 2, :]).then_inc(sem["pt"], 1)

                    def copy_ot(c):
                        act.wait_ge(sem["o_tr"], c + 1)
                        if c >= 2:
                            act.wait_ge(sem["out_mm"], c - 1)
                        nc.scalar.copy(ot[:, c % 2, :], ps_m[:, 0, :]).then_inc(sem["ot"], 1)

                    def ahead(c, k):
                        if c < NCH:
                            if k == 0:
                                copy_xt(c)
                            elif k == 1:
                                copy_q(c, "q", 1, self.bq, qt, softmax)
                            elif k == 2:
                                copy_q(c, "k", 0, self.bk, kt, not softmax)

                    for k in range(3):
                        ahead(0, k)
                    for n in range(NU + 3):
                        c, k = n // (2 * G), n % (2 * G)
                        if n < NU:
                            ahead(c + 1, k)
                        if softmax and 0 <= n - 1 < NU:
                            exponentials(n - 1)
                        if softmax and 0 <= n - 2 < NU:
                            copy_pt(n - 2)
                        if self.wo and k == 5 and 1 <= c:
                            copy_ot(c - 1)
                        if self.wg and k == 4 and n < NU:
                            act.wait_ge(sem["gate"], c + 1)
                            if c >= 2:
                                act.wait_ge(sem["o"], G * (c - 1))
                            nc.scalar.activation(gate[:, c % 2, :, :], gpre[:, :, :], ACT.Silu).then_inc(sem["rz"], 1)
                    if self.wo:
                        copy_ot(NCH - 1)

                @block.gpsimd
                def _(pool):
                    def weigh(n):
                        pool.wait_ge(sem["exp"], n + 1)
                        if n >= 2:
                            pool.wait_ge(sem["summed"], n - 1)
                        nc.gpsimd.tensor_tensor(weighted[:, n % 2, :, :], pr[:, n % 2, :, :], shifted[:, n % 2, :, :],
                                                ALU.mult).then_inc(sem["weighted"], 1)

                    if source:
                        source.gpsimd(pool, 0)
                        source.gpsimd(pool, 1)
                    pool.wait_ge(sem["w_in"], 16 * loads)
                    for b in range(B):
                        c = b // G
                        if b % G == 0:
                            pool.wait_ge(sem["k" if softmax else "q"], c + 1)
                            if self.bo:
                                pool.wait_ge(sem["x_tr"], c + 1)
                                nc.gpsimd.tensor_tensor(chunk(core.x, c), chunk(core.x, c),
                                                        row[self.bo].broadcast_to((P, G, P)), ALU.add).then_inc(sem["bo"], 1)
                        if b >= 2:
                            pool.wait_ge(sem["score"], 2 * (b - 1))
                        one = moving[:, c % 2, P * (b % G):P * (b % G) + P].unsqueeze(1).broadcast_to((P, HEADS, P))
                        nc.gpsimd.tensor_tensor(spread[:, b % 2, :, :], one,
                                                head_mask[:, :].unsqueeze(2).broadcast_to((P, HEADS, P)),
                                                ALU.mult).then_inc(sem["spread"], 1)
                        if source and b % G == 2 and c + 2 < NCH:
                            source.gpsimd(pool, c + 2)
                        if self.norm_to is not None and b % G == 2 and c >= 2:
                            norm.rstd(pool, c - 2, c % 2)
                        if self.sums and b >= 2:
                            weigh(2 * b - 4)
                            weigh(2 * b - 3)
                    if self.sums:
                        for n in range(2 * B - 4, 2 * B):
                            weigh(n)
                    if self.norm_to is not None:
                        norm.rstd(pool, NCH - 2, 0)
                        norm.rstd(pool, NCH - 1, 1)

                @block.vector
                def _(dve):
                    tt = nc.vector.tensor_tensor
                    if softmax:
                        nc.vector.memset(v[:, :, :, :, HD:HD + 1].rearrange("p a g h e -> p (a g h) e"), 1.0).then_inc(sem["ones"], 1)
                        dve.wait_ge(sem["ones"], 1)
                    if source:
                        source.rows(dve, 0, range(source.r.k))
                        source.statistics(dve, 0)
                        source.rows(dve, 1, range(source.r.k))
                        source.scale(dve, 0)
                        source.statistics(dve, 1)
                        source.scale(dve, 1)
                    dve.wait_ge(sem["w_in"], 16 * loads)

                    def copy_v(c):
                        dve.wait_ge(sem["v_mm"], c + 1)
                        if c >= 2:
                            dve.wait_ge(sem["pv"], 2 * G * (c - 1))
                        to = v[:, c % 2, :, :, 0:HD]
                        if self.bv:
                            for g in range(G):
                                last = tt(to[:, g], ps_m[:, 1, P * g:P * g + P].rearrange("p (h e) -> p h e", e=HD),
                                          row[self.bv].rearrange("p o (h e) -> p (o h) e", e=HD), ALU.add)
                            last.then_inc(sem["v"], 1)
                        else:
                            nc.vector.tensor_copy(to, ps_m[:, 1, :].rearrange("p (g h e) -> p g h e", g=G, e=HD)).then_inc(sem["v"], 1)

                    def bias_gate(c):
                        dve.wait_ge(sem["g_mm"], c + 1)
                        if c >= 1:
                            dve.wait_ge(sem["rz"], c)
                        tt(gpre[:, :, :], bank4(ps_p[:, c % 2, :]), row[self.bg].broadcast_to((P, G, P)),
                           ALU.add).then_inc(sem["gate"], 1)

                    def row_max(n):
                        dve.wait_ge(sem["score"], n + 1)
                        nc.vector.tensor_reduce(mx[:, n % 2, :], bank4(ps_s[:, n % 2, :]), AX_X, ALU.max).then_inc(sem["max"], 1)

                    def shift(n):
                        dve.wait_ge(sem["max"], n + 1)
                        if n >= 2:
                            dve.wait_ge(sem["exp"], n - 1)
                            if self.sums:
                                dve.wait_ge(sem["weighted"], n - 1)
                        tt(shifted[:, n % 2, :, :], bank4(ps_s[:, n % 2, :]),
                           mx[:, n % 2, :].unsqueeze(2).broadcast_to((P, UNIT, P)),
                           ALU.subtract).then_inc(sem["score_read"], 1)

                    def sum_weighted(n):
                        dve.wait_ge(sem["weighted"], n + 1)
                        nc.vector.tensor_reduce(self.sums[1][:, n // 2, UNIT * (n % 2):UNIT * (n % 2) + UNIT],
                                                weighted[:, n % 2, :, :], AX_X, ALU.add).then_inc(sem["summed"], 1)

                    def weigh(n):
                        dve.wait_ge(sem["score"], n + 1)
                        if n >= 2:
                            dve.wait_ge(sem["pv"], n - 1)
                        tt(pr[:, n % 2, :, :], bank4(ps_s[:, n % 2, :]),
                           decay[:, UNIT * (n % 2):UNIT * (n % 2) + UNIT, :], ALU.mult).then_inc(sem["score_read"], 1)

                    def normalise(b):
                        c, g = b // G, b % G
                        dve.wait_ge(sem["pv"], 2 * b + 2)
                        got = ps_o[:, b % 2, 0:HEADS * values].rearrange("p (h e) -> p h e", e=values)
                        to = (o[:, c % 2, g, :] if self.dst is None else self.dst[:, b, :]).rearrange("p (h e) -> p h e", e=HD)
                        if self.wo and c >= 2 and g == 0:
                            dve.wait_ge(sem["o_tr"], c - 1)
                        if self.sums:
                            nc.vector.tensor_copy(self.sums[0][:, b, :], got[:, :, HD])
                        if softmax:
                            nc.vector.reciprocal(rz[:, b % 2, :], got[:, :, HD]).then_inc(sem["rz"], 1)
                            dve.wait_ge(sem["rz"], b + 1)
                            tt(to, got[:, :, 0:HD], rz[:, b % 2, :].unsqueeze(2).broadcast_to((P, HEADS, HD)),
                               ALU.mult).then_inc(sem["o"], 1)
                        else:
                            if g == 0:
                                dve.wait_ge(sem["rz"], c + 1)
                            tt(to, got, gate[:, c % 2, g, :].rearrange("p (h e) -> p h e", e=HD), ALU.mult).then_inc(sem["o"], 1)
                            dve.wait_ge(sem["o"], b + 1)
                            tt(core.h[:, b, :], core.h[:, b, :], o[:, c % 2, g, :], ALU.add).then_inc(sem["out"], 1)

                    def residual(c):
                        dve.wait_ge(sem["out_mm"], c + 1)
                        if self.bo:
                            dve.wait_ge(sem["bo"], c + 1)
                        tt(chunk(core.x, c), bank4(ps_m[:, 1, :]), chunk(core.x, c), ALU.add).then_inc(sem["out"], 1)

                    def statistics(c):
                        dve.wait_ge(sem["out"], c + 1 if self.wo else G * (c + 1))
                        norm.statistics(dve, chunk(stream, c), c, c % 2)

                    def scale(c):
                        to = chunk(self.norm_to, c)
                        if self.norm_rows:
                            last = norm.scale_affine(dve, to, chunk(stream, c), norm_rows[:, 0, :], norm_rows[:, 1, :], c, c % 2)
                        else:
                            last = norm.scale(dve, to, chunk(stream, c), c, c % 2)
                        last.then_inc(normed, 1)

                    copy_v(0)
                    lag = 4 if softmax else 3
                    for n in range(NU + lag):
                        c, k = n // (2 * G), n % (2 * G)
                        if n < NU:
                            if softmax:
                                row_max(n)
                                shift(n)
                            else:
                                weigh(n)
                            if k == 3 and c + 1 < NCH:
                                copy_v(c + 1)
                            if source and c + 2 < NCH:
                                if k < source.r.k:
                                    source.rows(dve, c + 2, (k,))
                                elif k == source.r.k:
                                    source.statistics(dve, c + 2)
                                elif k == 5:
                                    source.scale(dve, c + 2)
                            if self.wg and k == 3:
                                bias_gate(c)
                        m = n - lag
                        if self.sums and 0 <= n - 3 < NU:
                            sum_weighted(n - 3)
                        if m >= 0 and m % 2 == 1:
                            normalise(m // 2)
                        if self.wo and k == 7 and c >= 1:
                            residual(c - 1)
                        if self.norm_to is not None and n < NU and c >= 2:
                            if k == 0:
                                statistics(c - 2)
                            elif k == 6:
                                scale(c - 2)
                    if self.norm_to is not None:
                        statistics(NCH - 2)
                    if self.wo:
                        residual(NCH - 1)
                    if self.norm_to is not None:
                        statistics(NCH - 1)
                        scale(NCH - 2)
                        scale(NCH - 1)
                        dve.wait_ge(normed, NCH)
                    if self.wo:
                        dve.wait_ge(sem["out"], NCH)
                    elif softmax:
                        dve.wait_ge(sem["o"], B)
                        if self.sums:
                            dve.wait_ge(sem["summed"], NU)
                    else:
                        dve.wait_ge(sem["out"], B)


BS = 256
BT = BS // P
C_L0 = 2 * (B * P * 2 // 64)
assert C_L0 == BS


def blocks_of(experts, k):
    return (B * P * k + experts * (BS - 1)) // BS


MAX_K = 4
TAG = 2 * MAX_K * B * P
SLOTS = max(64, blocks_of(8, 1), blocks_of(8, 2), blocks_of(16, 4)) * BS


class Routing:

    def __init__(self, core, st, experts, k, layer):
        self.experts, self.k, self.tag = experts, k, TAG * (layer + 1)
        self.gates = st.sb("gates", [P, B, k])
        self.to = st.sb("to", [P, B, k], I32)
        self.tags = st.sb("tags", [P, B, k])
        self.blocks = blocks_of(experts, k)
        self.block_expert = st.sb("block_expert", [P, self.blocks], I32)


def stage_route(core, name, r, xt, x_rows, gate_w, gate_b=None, over="probs", gate="share", capacity=None,
                scatter=True):
    nc, ins, E, K = core.nc, core.ins, r.experts, r.k
    cols = B * E
    nbank = -(-cols // 512)
    width = min(cols, 512)
    with Stage(core, name) as st:
        w = st.sb("w", [P, E])
        bias = st.sb("bias", [P, 1, E])
        iota = st.sb("iota", [P, 1, P])
        token = st.sb("token", [P, B])
        tri, after_bf = st.sb("tri", [P, P]), st.sb("after_bf", [P, P], BF16)
        ones_bf = st.sb("ones_bf", [P, P], BF16)
        lg, pr = st.sb("lg", [P, B, E]), st.sb("pr", [P, B, E])
        mx, z, rz = (st.sb(n, [P, B]) for n in ("mx", "z", "rz"))
        top, idx = st.sb("top", [P, B, 8]), st.sb("idx", [P, B, 8], U32)
        idxf = st.sb("idxf", [P, B, K])
        topk, topm = st.sb("topk", [P, B, K]), st.sb("topm", [P, B, K])
        oh = st.sb("oh", [P, K, B, E], BF16)
        cnt, cum = st.sb("cnt", [P, E, B], BF16), st.sb("cum", [P, E, B], BF16)
        run, base = st.sb("run", [P, E, B]), st.sb("base", [P, E])
        pos, picked = st.sb("pos", [P, B, E]), st.sb("picked", [P, B, E])
        posk, slot = st.sb("posk", [P, B, K]), st.sb("slot", [P, B, K])
        drop, spare = st.sb("drop", [P, B, K]), st.sb("spare", [P, B, K])
        nb, end, start = st.sb("nb", [P, E]), st.sb("end", [P, E]), st.sb("start", [P, 1, E])
        past, which = st.sb("past", [P, r.blocks, E]), st.sb("which", [P, r.blocks])
        ps_l, ps_p = st.ps("ps_l", [P, nbank, 512]), st.ps("ps_p", [P, max(nbank, 2), 512])
        sem = {n: st.sem(n) for n in ("in", "mm", "sub", "exp", "chain", "counted", "pos", "placed", "keyed",
                                      "keyed_exp", "x_turned", "x_copied")}
        loads = 4 + (gate_b is not None)
        sc = Scatter(core, st, r, x_rows) if scatter else None
        with nc.Block() as block:
            @block.sync
            def _(sp):
                sp.dma_start(w[:, :], gate_w).then_inc(sem["in"], 16)
                sp.dma_start(iota[:, :, :], ins["iota_row"].unsqueeze(1)).then_inc(sem["in"], 16)
                sp.dma_start(tri[:, :], ins["tri"]).then_inc(sem["in"], 16)
                sp.dma_start(token[:, :], ins["token"]).then_inc(sem["in"], 16)
                if gate_b is not None:
                    sp.dma_start(bias[:, :, :], gate_b.unsqueeze(0).partition_broadcast(P)).then_inc(sem["in"], 16)
                sp.wait_ge(sem["in"], 16 * loads)

            @block.tensor
            def _(pe):
                per = width // E

                def turn(c):
                    for g in range(G):
                        last = nc.tensor.transpose(ps_p[:, c % 2, P * g:P * g + P], x_rows[:, G * c + g, :], core.ident[:, :])
                    last.then_inc(sem["x_turned"], 1)

                turn(0)
                turn(1)
                pe.wait_ge(sem["in"], 16 * loads)
                for c in range(NCH):
                    pe.wait_ge(sem["x_copied"], c + 1)
                    for b in range(G * c, G * c + G):
                        last = nc.tensor.matmul(ps_l[:, b // per, E * (b % per):E * (b % per) + E], xt[:, P * b:P * b + P],
                                                w[:, :], start=True, stop=True)
                    if c + 2 < NCH:
                        turn(c + 2)
                last.then_inc(sem["mm"], 1)
                pe.wait_ge(sem["counted"], 1)
                cnt_f, cum_f = flat(cnt[:, :, :]), flat(cum[:, :, :])
                for n in range(nbank):
                    s = slice(width * n, width * n + width)
                    nc.tensor.matmul(ps_p[:, n, 0:width], after_bf[:, :], cnt_f[:, s], start=True, stop=False)
                    nc.tensor.matmul(ps_p[:, n, 0:width], ones_bf[:, :], cum_f[:, s], start=False, stop=True)
                nc.tensor.matmul(ps_l[:, 0, 0:E], ones_bf[:, :], cum[:, :, B - 1], start=True, stop=True).then_inc(sem["pos"], 1)

            @block.scalar
            def _(act):
                for c in range(NCH):
                    act.wait_ge(sem["x_turned"], c + 1)
                    nc.scalar.copy(xt[:, W * c:W * c + W], ps_p[:, c % 2, :]).then_inc(sem["x_copied"], 1)
                if over == "probs":
                    act.wait_ge(sem["sub"], 1)
                    nc.scalar.activation(flat(pr[:, :, :]), flat(lg[:, :, :]), ACT.Exp).then_inc(sem["exp"], 1)
                if gate == "softmax":
                    act.wait_ge(sem["keyed"], 1)
                    nc.scalar.activation(flat(topk[:, :, :]), flat(topm[:, :, :]), ACT.Exp).then_inc(sem["keyed_exp"], 1)
                if sc:
                    for b in range(B):
                        sc.scalar(act, b)

            @block.vector
            def _(dve):
                made = [0]

                def then(*i):
                    i[-1].then_inc(sem["chain"], 1)
                    made[0] += 1
                    dve.wait_ge(sem["chain"], made[0])

                tt, ts = nc.vector.tensor_tensor, nc.vector.tensor_scalar
                per_tile = lambda a: a[:, :].unsqueeze(2).broadcast_to((P, B, E))
                dve.wait_ge(sem["in"], 16 * loads)
                ts(after_bf[:, :], tri[:, :], 1.0, None, ALU.subtract)
                nc.vector.memset(ones_bf[:, :], 1.0)
                for k in range(K):
                    ts(r.tags[:, :, k], token[:, :], float(k * B * P - r.tag), None, ALU.add)
                dve.wait_ge(sem["mm"], 1)
                got = ps_l[:, :, 0:width].rearrange("p n (b e) -> p (n b) e", e=E)
                if gate_b is not None:
                    then(tt(lg[:, :, :], got, bias[:, :, :].broadcast_to((P, B, E)), ALU.add))
                else:
                    then(nc.vector.tensor_copy(lg[:, :, :], got))
                if over == "probs":
                    then(nc.vector.tensor_reduce(mx[:, :], lg[:, :, :], AX_X, ALU.max))
                    tt(lg[:, :, :], lg[:, :, :], per_tile(mx), ALU.subtract).then_inc(sem["sub"], 1)
                    dve.wait_ge(sem["exp"], 1)
                    then(nc.vector.tensor_reduce(z[:, :], pr[:, :, :], AX_X, ALU.add))
                    then(nc.vector.reciprocal(rz[:, :], z[:, :]))
                    then(tt(pr[:, :, :], pr[:, :, :], per_tile(rz), ALU.mult))
                    values = pr
                else:
                    values = lg
                for b in range(B):
                    i = nc.vector.max(top[:, b, :], values[:, b, :])
                then(i)
                for b in range(B):
                    i = nc.vector.max_index(idx[:, b, :], top[:, b, :], values[:, b, :])
                then(i)
                then(nc.vector.tensor_copy(idxf[:, :, :], idx[:, :, 0:K]))
                for k in range(K):
                    i = tt(oh[:, k, :, :], iota[:, :, 0:E].broadcast_to((P, B, E)),
                           idxf[:, :, k:k + 1].broadcast_to((P, B, E)), ALU.is_equal)
                then(i)
                by_tile = lambda t: t[:, :, :].rearrange("p e b -> p b e")
                counts = oh[:, 0, :, :]
                for k in range(1, K):
                    then(tt(by_tile(cnt), counts, oh[:, k, :, :], ALU.add))
                    counts = by_tile(cnt)
                if K == 1:
                    then(nc.vector.tensor_copy(by_tile(cnt), counts))
                then(nc.vector.tensor_tensor_scan(flat(run[:, :, :]), flat(cnt[:, :, :]), flat(cnt[:, :, :]), 0.0,
                                                  ALU.add, ALU.bypass))
                then(nc.vector.memset(base[:, 0:1], 0.0),
                     nc.vector.tensor_copy(base[:, 1:E], run[:, 0:E - 1, B - 1]))
                tt(cum[:, :, :], run[:, :, :], base[:, :].unsqueeze(2).broadcast_to((P, E, B)),
                   ALU.subtract).then_inc(sem["counted"], 1)
                if gate == "value":
                    then(nc.vector.tensor_copy(r.gates[:, :, :], top[:, :, 0:K]))
                else:
                    if gate == "softmax":
                        tt(topm[:, :, :], top[:, :, 0:K], top[:, :, 0:1].broadcast_to((P, B, K)),
                           ALU.subtract).then_inc(sem["keyed"], 1)
                        dve.wait_ge(sem["keyed_exp"], 1)
                    else:
                        then(nc.vector.tensor_copy(topk[:, :, :], top[:, :, 0:K]))
                    then(nc.vector.tensor_reduce(z[:, :], topk[:, :, :], AX_X, ALU.add))
                    then(nc.vector.reciprocal(rz[:, :], z[:, :]))
                    then(tt(r.gates[:, :, :], topk[:, :, :], rz[:, :].unsqueeze(2).broadcast_to((P, B, K)), ALU.mult))
                dve.wait_ge(sem["pos"], 1)
                before = flat(ps_p[:, 0:nbank, 0:width]).rearrange("p (e b) -> p b e", b=B) if nbank > 1 else \
                    ps_p[:, 0, 0:width].rearrange("p (e b) -> p b e", b=B)
                if capacity is None:
                    magic = float(1.5 * 2 ** 23)
                    then(ts(nb[:, :], ps_l[:, 0, 0:E], 1.0 / BS, (BS - 1.0) / BS - (BS - 1.0) / (2 * BS), ALU.mult, ALU.add))
                    then(ts(nb[:, :], nb[:, :], magic, None, ALU.add))
                    then(ts(nb[:, :], nb[:, :], magic, None, ALU.subtract))
                    then(nc.vector.tensor_tensor_scan(end[:, :], nb[:, :], nb[:, :], 0.0, ALU.add, ALU.bypass))
                    then(tt(start[:, 0, :], end[:, :], nb[:, :], ALU.subtract))
                    then(ts(start[:, 0, :], start[:, 0, :], float(BS), None, ALU.mult))
                    nblk = r.blocks
                    then(tt(past[:, :, :], end[:, :].unsqueeze(1).broadcast_to((P, nblk, E)),
                            iota[:, 0, 0:nblk].unsqueeze(2).broadcast_to((P, nblk, E)), ALU.is_le))
                    then(nc.vector.tensor_reduce(which[:, :], past[:, :, :], AX_X, ALU.add))
                    then(ts(which[:, :], which[:, :], float(E - 1), None, ALU.min))
                    then(nc.vector.tensor_copy(r.block_expert[:, :], which[:, :]))
                    then(tt(pos[:, :, :], before, start[:, :, :].broadcast_to((P, B, E)), ALU.add))
                else:
                    then(nc.vector.tensor_copy(pos[:, :, :], before))
                for k in range(K):
                    then(tt(picked[:, :, :], pos[:, :, :], oh[:, k, :, :], ALU.mult))
                    then(nc.vector.tensor_reduce(posk[:, :, k], picked[:, :, :], AX_X, ALU.add))
                if capacity is None:
                    then(nc.vector.tensor_copy(r.to[:, :, :], posk[:, :, :]))
                else:
                    then(ts(drop[:, :, :], posk[:, :, :], float(capacity), None, ALU.is_ge))
                    then(ts(posk[:, :, :], posk[:, :, :], float(capacity - 1), None, ALU.min))
                    then(nc.vector.scalar_tensor_tensor(out=slot[:, :, :], in0=idxf[:, :, :], scalar=float(capacity),
                                                        in1=posk[:, :, :], op0=ALU.mult, op1=ALU.add))
                    then(ts(spare[:, :, :], slot[:, :, :], float(SLOTS), None, ALU.subtract))
                    then(tt(spare[:, :, :], spare[:, :, :], drop[:, :, :], ALU.mult))
                    then(tt(slot[:, :, :], slot[:, :, :], spare[:, :, :], ALU.subtract))
                    then(nc.vector.tensor_copy(r.to[:, :, :], slot[:, :, :]))
                    then(ts(drop[:, :, :], drop[:, :, :], -1.0, 1.0, ALU.mult, ALU.add))
                    then(tt(r.gates[:, :, :], r.gates[:, :, :], drop[:, :, :], ALU.mult))
                nc.vector.memset(mx[:, :], 0.0).then_inc(sem["placed"], 1)
                if sc:
                    for b in range(B):
                        sc.vector(dve, b)

            @block.gpsimd
            def _(pool):
                pool.wait_ge(sem["placed"], 1)
                if sc:
                    sc.gpsimd(pool)


class Scatter:
    STAGED = 4

    def __init__(self, core, st, r, x_rows):
        self.core, self.nc, self.r, self.x_rows = core, core.nc, r, x_rows
        self.staged = st.sb("staged", [P, self.STAGED, r.k, P + 1])
        self.copied, self.tagged = st.sem("copied"), st.sem("tagged")
        self.wrote = [st.sem(f"wrote{k}") for k in range(self.STAGED)]

    def free(self, eng, b):
        if b >= self.STAGED:
            eng.wait_ge(self.wrote[b % self.STAGED], 16 * self.r.k * (b // self.STAGED))

    def scalar(self, act, b):
        K = self.r.k
        self.free(act, b)
        self.nc.scalar.copy(self.staged[:, b % self.STAGED, :, 0:P],
                            self.x_rows[:, b:b + 1, :].broadcast_to((P, K, P))).then_inc(self.copied, 1)

    def vector(self, dve, b):
        self.free(dve, b)
        self.nc.vector.tensor_copy(self.staged[:, b % self.STAGED, :, P], self.r.tags[:, b, :]).then_inc(self.tagged, 1)

    def gpsimd(self, pool):
        K = self.r.k
        pool.wait_ge(self.core.zeroed, 32)
        for b in range(B):
            pool.wait_ge(self.copied, b + 1)
            pool.wait_ge(self.tagged, b + 1)
            for k in range(K):
                self.nc.gpsimd.indirect_dma_start(self.core.slots_in, bass.IndirectOffsetOnAxis(self.r.to[:, b, k:k + 1], 0),
                                                  self.staged[:, b % self.STAGED, k, :], None, bounds_check=SLOTS - 1,
                                                  oob_is_err=False).then_inc(self.wrote[b % self.STAGED], 16)
        for wrote in self.wrote:
            pool.wait_ge(wrote, 16 * K * B // self.STAGED)


def ring(eng, lo, hi, size, body):
    assert lo % size == 0
    turns = (hi - lo) // size
    if turns:
        with eng.Fori(0, turns) as turn:
            for k in range(size):
                body(turn * size + (lo + k), k)
    for i in range(lo + size * turns, hi):
        body(i, i % size)


RING = 6


def stage_experts(core, name, r, blocks, packed, rows_in, func, grouped, norm=False):
    nc, ins = core.nc, core.ins
    F = 2 * P + 1
    M = packed.shape[2] // F
    with Stage(core, name) as st:
        weights, xin = st.sb("weights", [P, RING, M * F]), st.sb("xin", [P, RING, BT, P + 1])
        pool_carrier = st.sb("pool_carrier", [P, 1])
        back = st.sb("back", [P, RING, BT], I32)
        w1s = weights[:, :, 0:M * P]
        w2s = weights[:, :, M * P:2 * M * P].rearrange("p k (m d) -> p k m d", d=P)
        b1s = weights[:, :, 2 * M * P:M * F]
        n_rows = 3 if norm else 1
        rows = st.sb("rows", [P, RING, n_rows, P])
        xt, mid = st.sb("xt", [P, 2, BS]), st.sb("mid", [P, 2, M, BS])
        yout = st.sb("yout", [P, RING, BT, P])
        if norm:
            raw = st.sb("raw", [P, 2, BT, P])
            stats, mv = st.sb("stats", [P, 2, BT, 6]), st.sb("mv", [P, 2, BT, 2])
            carrier = st.sb("carrier", [P, 1])
            ve, rs = st.sb("ve", [P, 2, BT]), st.sb("rs", [P, 2, BT])
        ps_t, ps_o = st.ps("ps_t", [P, 2, 512]), st.ps("ps_o", [P, 2, 512])
        ps_u = st.ps("ps_u", [P, 2, 2, 512])
        loaded = [st.sem(f"loaded{k}") for k in range(RING)]
        stored = [st.sem(f"stored{k}") for k in range(RING)]
        x_tr, x_t, up, acted, down, y_done, var_done, rstd_done = (st.sem(n) for n in (
            "x_tr", "x_t", "up", "acted", "down", "y_done", "var_done", "rstd_done"))
        raw_done, stats_done, aggr_done, centred, carried = (st.sem(n) for n in (
            "raw_done", "stats_done", "aggr_done", "centred", "carried"))
        N = blocks
        per = 3
        last_row = r.k * B * P - 1
        buf = core.slots_in.rearrange("(n p) d -> p n d", p=P)

        def late(i, n):
            return not isinstance(i, int) or i >= n

        with nc.Block() as block:
            @block.sync
            def _(sp):
                def load(g, k):
                    if late(g, RING):
                        sp.wait_ge(y_done, g - RING + 1)
                    if grouped:
                        e = sp.value_load(r.block_expert[0:1, bass.ds(g, 1)], min_val=0, max_val=r.experts - 1)
                    else:
                        e = g
                    one = lambda t: t[bass.ds(e, 1)]
                    sp.dma_start(xin[:, k, :, :], buf[:, bass.ds(g * BT, BT), :]).then_inc(loaded[k], 16)
                    sp.dma_start(weights[:, k, :], one(packed).rearrange("e p f -> (e p) f")).then_inc(loaded[k], 16)
                    sp.dma_start(rows[:, k, :, :], one(rows_in).rearrange("e n d -> (e n) d").partition_broadcast(P)
                                 ).then_inc(loaded[k], 16)

                for g in range(RING):
                    load(g, g)
                ring(sp, RING, N, RING, load)

            @block.tensor
            def _(pe):
                def turn(g, k):
                    pe.wait_ge(loaded[k], 16 * per * (g // RING + 1))
                    if late(g, 2):
                        pe.wait_ge(x_t, g - 1)
                    for t in range(BT):
                        last = nc.tensor.transpose(ps_t[:, k % 2, P * t:P * t + P], xin[:, k, t, 0:P], core.ident[:, :])
                    last.then_inc(x_tr, 1)

                def first(g, k):
                    pe.wait_ge(x_t, g + 1)
                    if late(g, 2):
                        pe.wait_ge(acted, g - 1)
                    for m in range(M):
                        last = nc.tensor.matmul(ps_u[:, k % 2, m // 2, BS * (m % 2):BS * (m % 2) + BS],
                                                w1s[:, k, P * m:P * m + P], xt[:, k % 2, :], start=True, stop=True)
                    last.then_inc(up, 1)

                def second(g, k):
                    pe.wait_ge(acted, g + 1)
                    if late(g, 2):
                        pe.wait_ge(y_done if not norm else raw_done, g - 1)
                    for t in range(BT):
                        for m in range(M):
                            last = nc.tensor.matmul(ps_o[:, k % 2, P * t:P * t + P], mid[:, k % 2, m, P * t:P * t + P],
                                                    w2s[:, k, m, :], start=(m == 0), stop=(m == M - 1))
                    last.then_inc(down, 1)

                def body(g, k):
                    turn(g + 1, (k + 1) % RING)
                    first(g, k)
                    second(g - 1, (k - 1) % RING)

                turn(0, 0)
                for g in range(RING):
                    turn(g + 1, (g + 1) % RING)
                    first(g, g)
                    if g:
                        second(g - 1, g - 1)
                ring(pe, RING, N - 1, RING, body)
                first(N - 1, (N - 1) % RING)
                second(N - 2, (N - 2) % RING)
                second(N - 1, (N - 1) % RING)

            @block.scalar
            def _(act):
                def copy_x(g, k):
                    act.wait_ge(x_tr, g + 1)
                    if late(g, 2):
                        act.wait_ge(up, g - 1)
                    nc.scalar.copy(xt[:, k % 2, :], ps_t[:, k % 2, 0:BS]).then_inc(x_t, 1)

                def activate(g, k):
                    act.wait_ge(up, g + 1)
                    if late(g, 2):
                        act.wait_ge(down, g - 1)
                    for m in range(M):
                        last = nc.scalar.activation(mid[:, k % 2, m, :], ps_u[:, k % 2, m // 2, BS * (m % 2):BS * (m % 2) + BS],
                                                    func, bias=b1s[:, k, m:m + 1])
                    last.then_inc(acted, 1)

                def body(g, k):
                    copy_x(g + 1, (k + 1) % RING)
                    activate(g, k)

                copy_x(0, 0)
                for g in range(RING):
                    body(g, g)
                ring(act, RING, N - 1, RING, body)
                activate(N - 1, (N - 1) % RING)

            @block.vector
            def _(dve):
                def find_rows(g, k):
                    nc.vector.tensor_scalar(back[:, k, :], xin[:, k, :, P], float(r.tag), None, ALU.add)

                def output(g, k):
                    dve.wait_ge(down, g + 1)
                    if not norm and late(g, RING):
                        dve.wait_ge(stored[k], 16 * BT * (g // RING))
                    if not norm:
                        find_rows(g, k)
                    got = ps_o[:, k % 2, 0:BS].rearrange("p (t d) -> p t d", d=P)
                    row = lambda n: rows[:, k, n:n + 1, :].broadcast_to((P, BT, P))
                    if not norm:
                        nc.vector.tensor_tensor(yout[:, k, :, :], got, row(0), ALU.add).then_inc(y_done, 1)
                        return
                    j = k % 2
                    if late(g, 2):
                        dve.wait_ge(y_done, g - 1)
                    nc.vector.tensor_tensor(raw[:, j, :, :], got, row(0), ALU.add).then_inc(raw_done, 1)
                    dve.wait_ge(raw_done, g + 1)
                    for t in range(BT):
                        last = nc.vector.bn_stats(stats[:, j, t, :], raw[:, j, t, :])
                    last.then_inc(stats_done, 1)
                    dve.wait_ge(stats_done, g + 1)
                    nc.vector.memset(carrier[:, :], 0.0)
                    for t in range(BT):
                        last = nc.vector.bn_aggr(mv[:, j, t, :], stats[:, j, t, :])
                    last.then_inc(aggr_done, 1)
                    dve.wait_ge(aggr_done, g + 1)
                    nc.vector.tensor_scalar(ve[:, j, :], mv[:, j, :, 1], EPS, None, ALU.add).then_inc(var_done, 1)

                def normalise(g, k):
                    j = k % 2
                    if late(g, RING):
                        dve.wait_ge(stored[k], 16 * BT * (g // RING))
                    find_rows(g, k)
                    dve.wait_ge(rstd_done, g + 1)
                    for t in range(BT):
                        last = nc.vector.scalar_tensor_tensor(out=raw[:, j, t, :], in0=raw[:, j, t, :],
                                                              scalar=mv[:, j, t, 0:1], in1=rows[:, k, 1, :],
                                                              op0=ALU.subtract, op1=ALU.mult)
                    last.then_inc(centred, 1)
                    dve.wait_ge(centred, g + 1)
                    for t in range(BT):
                        last = nc.vector.scalar_tensor_tensor(out=yout[:, k, t, :], in0=raw[:, j, t, :],
                                                              scalar=rs[:, j, t:t + 1], in1=rows[:, k, 2, :],
                                                              op0=ALU.mult, op1=ALU.add)
                    last.then_inc(y_done, 1)

                def body(g, k):
                    output(g, k)
                    if norm:
                        normalise(g - 1, (k - 1) % RING)

                output(0, 0)
                for g in range(1, RING):
                    body(g, g)
                ring(dve, RING, N, RING, body)
                if norm:
                    normalise(N - 1, (N - 1) % RING)

            @block.gpsimd
            def _(pool):
                def store(g, k):
                    if late(g, 1):
                        pool.wait_ge(carried, g)
                    pool.wait_ge(y_done, g + 1)
                    nc.gpsimd.tensor_tensor(pool_carrier[:, :], core.neg_half[:, 0:1], core.neg_half[:, 0:1],
                                            ALU.mult).then_inc(carried, 1)
                    for t in range(BT):
                        nc.gpsimd.indirect_dma_start(core.returned[0:last_row + 1, :],
                                                     bass.IndirectOffsetOnAxis(back[:, k, t:t + 1], 0),
                                                     yout[:, k, t, :], None, bounds_check=last_row,
                                                     oob_is_err=False).then_inc(stored[k], 16)

                def rstd(g, k):
                    pool.wait_ge(var_done, g + 1)
                    nc.gpsimd.tensor_tensor(rs[:, k % 2, :], ve[:, k % 2, :], core.neg_half[:, 0:BT],
                                            ALU.pow).then_inc(rstd_done, 1)

                def body(g, k):
                    if not norm:
                        store(g, k)
                    else:
                        rstd(g, k)
                        store(g - 1, (k - 1) % RING)

                if not norm:
                    store(0, 0)
                else:
                    rstd(0, 0)
                for g in range(1, RING):
                    body(g, g)
                ring(pool, RING, N, RING, body)
                if norm:
                    store(N - 1, (N - 1) % RING)
                for k in range(RING):
                    pool.wait_ge(stored[k], 16 * BT * ((N - k + RING - 1) // RING))


class Combine:
    AHEAD = 4

    def __init__(self, core, st, r, add=None):
        self.core, self.nc, self.r, self.add = core, core.nc, r, add
        self.per = G * r.k
        self.y = st.sb("y", [P, self.AHEAD, r.k, G, P])
        self.got = [st.sem(f"got{k}") for k in range(self.AHEAD)]
        self.added, self.used, self.ready = (st.sem(n) for n in ("added", "used", "ready"))
        self.norm = Norm(core, st, "c")

    def sync(self, sp):
        K, R = self.r.k, self.AHEAD
        for c in range(NCH):
            if c >= R:
                sp.wait_ge(self.used, self.per * (c - R + 1))
            for k in range(K):
                rows = self.core.returned[(k * NCH + c) * W:(k * NCH + c) * W + W, :]
                sp.dma_start(self.y[:, c % R, k, :, :], rows.rearrange("(g p) d -> p g d", p=P)).then_inc(self.got[c % R], 16)

    def gpsimd_add(self, c):
        h = chunk(self.core.h, c)
        self.nc.gpsimd.tensor_tensor(h, h, chunk(self.add, c), ALU.add).then_inc(self.added, 1)

    def gpsimd(self, pool, c):
        self.norm.rstd(pool, c, c % 2)

    def rows(self, dve, c, ks):
        core, R = self.core, self.AHEAD
        if 0 in ks:
            if self.add is not None:
                dve.wait_ge(self.added, c + 1)
            dve.wait_ge(self.got[c % R], 16 * self.r.k * (c // R + 1))
        for k in ks:
            if k:
                dve.wait_ge(self.used, self.per * c + G * k)
            for g in range(G):
                b = G * c + g
                self.nc.vector.scalar_tensor_tensor(out=core.h[:, b, :], in0=self.y[:, c % R, k, g, :],
                                                    scalar=self.r.gates[:, b, k:k + 1], in1=core.h[:, b, :],
                                                    op0=ALU.mult, op1=ALU.add).then_inc(self.used, 1)

    def statistics(self, dve, c):
        dve.wait_ge(self.used, self.per * (c + 1))
        self.norm.statistics(dve, chunk(self.core.h, c), c, c % 2)

    def scale(self, dve, c):
        self.norm.scale(dve, chunk(self.core.x, c), chunk(self.core.h, c), c, c % 2).then_inc(self.ready, 1)


def stage_combine(core, name, r, out=None):
    with Stage(core, name) as st:
        co = Combine(core, st, r)
        stored = st.sem("stored")
        with core.nc.Block() as block:
            @block.sync
            def _(sp):
                co.sync(sp)

            if out is not None:
                @block.scalar
                def _(act):
                    for c in range(NCH):
                        act.wait_ge(co.used, co.per * (c + 1))
                        act.dma_start(out[G * c:G * c + G].rearrange("b s d -> s b d"), chunk(core.h, c)).then_inc(stored, 16)
                    act.wait_ge(stored, 16 * NCH)

            @block.gpsimd
            def _(pool):
                if out is None:
                    for c in range(NCH):
                        co.gpsimd(pool, c)

            @block.vector
            def _(dve):
                for c in range(NCH):
                    co.rows(dve, c, range(r.k))
                    if out is None:
                        if c:
                            co.scale(dve, c - 1)
                        co.statistics(dve, c)
                if out is None:
                    co.scale(dve, NCH - 1)
                    dve.wait_ge(co.ready, NCH)


def stage_l0_ffn_l1_attn(core, xn):
    nc, ins = core.nc, core.ins
    with Stage(core, "l0f") as st:
        Attention(core, "l0f_att", xn, "L0_ffn_wq", "L0_ffn_wk", "L0_ffn_wv", True, HD ** -0.5, wo="L0_ffn_wo",
                  affine=("L0_ffn_ln1_g", "L0_ffn_ln1_b"), norm=(xn, ("L0_ffn_ln2_g", "L0_ffn_ln2_b"))).run()
        r = Routing(core, st, 64, 2, 0)
        with Stage(core, "l0f_xt") as st2:
            xt = st2.sb("xt", [P, B * P])
            stage_route(core, "l0f_rt", r, xt, xn, ins["L0_ffn_wr"], capacity=C_L0)
        stage_experts(core, "l0f_ex", r, 64, ins["L0_ffn_packed"], ins["L0_ffn_rows"], ACT.Gelu_apprx_tanh, False)
        stage_l1_attn(core, r)


def stage_l1_ffn(core):
    nc, ins = core.nc, core.ins
    with Stage(core, "l1f") as st:
        t = st.sb("t", [P, B, P])
        Attention(core, "l1f_att", core.x, "L1_ffn_Wq", "L1_ffn_Wk", "L1_ffn_Wv", True, HD ** -0.5, wo="L1_ffn_Wo",
                  bq="L1_ffn_bq", bk="L1_ffn_bk", bv="L1_ffn_bv", bo="L1_ffn_bo",
                  norm=(t, ("L1_ffn_ln1_g", "L1_ffn_ln1_b"))).run()
        r = Routing(core, st, 8, 1, 1)
        with Stage(core, "l1f_xt") as st2:
            xt = st2.sb("xt", [P, B * P])
            stage_route(core, "l1f_rt", r, xt, t, ins["L1_ffn_gate_W"], ins["L1_ffn_gate_b"], gate="value")
        stage_experts(core, "l1f_ex", r, r.blocks, ins["L1_ffn_packed"], ins["L1_ffn_rows"], ACT.Gelu_apprx_tanh, True)
        stage_combine(core, "l1f_co", r)


def stage_l2_ffn_l3_attn(core):
    nc, ins = core.nc, core.ins
    with Stage(core, "l2f") as st:
        r = Routing(core, st, 8, 2, 2)
        with Stage(core, "l2f_xt") as st2:
            xt = st2.sb("xt", [P, B * P])
            stage_route(core, "l2f_rt", r, xt, core.x, ins["L2_ffn_Wg"], over="logits", gate="softmax")
        stage_experts(core, "l2f_ex", r, r.blocks, ins["L2_ffn_packed"], ins["L2_ffn_rows"], ACT.Relu, True, norm=True)
        Attention(core, "l3a", core.x, "L3_attn_wq", "L3_attn_wk", "L3_attn_wv", False, None, bq="L3_attn_bq",
                  bk="L3_attn_bk", bv="L3_attn_bv", wg="L3_attn_wg", bg="L3_attn_bg", norm=(core.x, ()), source=r).run()


def stage_shared(core, name, r, xt, w1, b1, w2, b2, experts):
    nc, ins, S = core.nc, core.ins, experts
    M = w1.shape[2] // P
    with Stage(core, name) as st:
        w1s, w2s = st.sb("w1", [P, S, M * P]), st.sb("w2", [P, S, M, P])
        b1s, b2s = st.sb("b1", [P, S, M]), st.sb("b2", [P, S, P])
        mid = st.sb("mid", [P, 2, M, W])
        ps_u, ps_o = st.ps("ps_u", [P, 4, 512]), st.ps("ps_o", [P, 2, 512])
        loaded, up, acted, down, added, scaled = (st.sem(n) for n in ("loaded", "up", "acted", "down", "added", "scaled"))
        sc = Scatter(core, st, r, core.x)
        N = NCH
        with nc.Block() as block:
            @block.gpsimd
            def _(pool):
                sc.gpsimd(pool)

            @block.sync
            def _(sp):
                sp.dma_start(w1s[:, :, :], w1.rearrange("s p f -> p s f")).then_inc(loaded, 16)
                sp.dma_start(w2s[:, :, :, :], w2.rearrange("s (m p) d -> p s m d", p=P)).then_inc(loaded, 16)
                sp.dma_start(b1s[:, :, :], b1.rearrange("s p m -> p s m")).then_inc(loaded, 16)
                sp.dma_start(b2s[:, :, :], b2.partition_broadcast(P)).then_inc(loaded, 16)
                sp.wait_ge(loaded, 64)

            @block.tensor
            def _(pe):
                pe.wait_ge(loaded, 64)

                def first(c, s):
                    for m in range(M):
                        q = M * (S * c + s) + m
                        if q >= 4:
                            pe.wait_ge(acted, q - 3)
                        nc.tensor.matmul(ps_u[:, q % 4, :], w1s[:, s, P * m:P * m + P], xt[:, W * c:W * c + W],
                                         start=True, stop=True).then_inc(up, 1)

                def second(n):
                    c, s = n // S, n % S
                    pe.wait_ge(acted, M * (n + 1))
                    if n >= 2:
                        pe.wait_ge(added, n - 1)
                    for g in range(G):
                        for m in range(M):
                            last = nc.tensor.matmul(ps_o[:, n % 2, P * g:P * g + P], mid[:, n % 2, m, P * g:P * g + P],
                                                    w2s[:, s, m, :], start=(m == 0), stop=(m == M - 1))
                    last.then_inc(down, 1)

                for n in range(S * N):
                    first(n // S, n % S)
                    if n:
                        second(n - 1)
                second(S * N - 1)

            @block.scalar
            def _(act):
                act.wait_ge(loaded, 64)
                for n in range(S * N):
                    for b in range(B * n // (S * N), B * (n + 1) // (S * N)):
                        sc.scalar(act, b)
                    for m in range(M):
                        q = M * n + m
                        act.wait_ge(up, q + 1)
                        if m == 0 and n >= 2:
                            act.wait_ge(down, n - 1)
                        nc.scalar.activation(mid[:, n % 2, m, :], ps_u[:, q % 4, :], ACT.Gelu,
                                             bias=b1s[:, n % S, m:m + 1]).then_inc(acted, 1)

            @block.vector
            def _(dve):
                dve.wait_ge(loaded, 64)
                tt = nc.vector.tensor_tensor
                tt(b2s[:, 0, :], b2s[:, 0, :], b2s[:, 1, :], ALU.add).then_inc(scaled, 1)
                dve.wait_ge(scaled, 1)
                nc.vector.tensor_scalar(b2s[:, 0, :], b2s[:, 0, :], 1.0 / S, None, ALU.mult).then_inc(scaled, 1)
                dve.wait_ge(scaled, 2)
                for c in range(NCH):
                    last = tt(chunk(core.h, c), chunk(core.h, c), b2s[:, 0:1, :].broadcast_to((P, G, P)), ALU.add)
                last.then_inc(scaled, 1)
                dve.wait_ge(scaled, 3)
                for n in range(S * N):
                    for b in range(B * n // (S * N), B * (n + 1) // (S * N)):
                        sc.vector(dve, b)
                    c = n // S
                    dve.wait_ge(down, n + 1)
                    if n:
                        dve.wait_ge(added, n)
                    nc.vector.scalar_tensor_tensor(out=chunk(core.h, c), in0=bank4(ps_o[:, n % 2, :]), scalar=1.0 / S,
                                                   in1=chunk(core.h, c), op0=ALU.mult, op1=ALU.add).then_inc(added, 1)
                dve.wait_ge(added, S * N)


def stage_l3_ffn(core, out):
    nc, ins = core.nc, core.ins
    with Stage(core, "l3f") as st:
        r = Routing(core, st, 16, 4, 3)
        with Stage(core, "l3f_xt") as st2:
            xt = st2.sb("xt", [P, B * P])
            stage_route(core, "l3f_rt", r, xt, core.x, ins["L3_ffn_gate_wT"], gate="softmax", scatter=False)
            stage_shared(core, "l3f_sh", r, xt, ins["L3_ffn_se_w1"], ins["L3_ffn_se_b1"], ins["L3_ffn_se_w2"],
                         ins["L3_ffn_se_b2"], 2)
        stage_experts(core, "l3f_ex", r, r.blocks, ins["L3_ffn_packed"], ins["L3_ffn_rows"], ACT.Gelu, True)
        stage_combine(core, "l3f_co", r, out=out)


MAGIC = float(1.5 * 2 ** 23)
TIE_UP = float(2.0 ** -22)


def stage_l1_attn(core, r):
    nc, ins = core.nc, core.ins
    T = B * P
    with Stage(core, "l1a") as st:
        spikes = st.sb("spikes", [P, 3, T], BF16)
        tie_up = st.sb("tie_up", [P, 1])
        with Stage(core, "l1p") as s1:
            w = s1.sb("w", [P, 3 * P])
            gamma_beta = s1.sb("gamma_beta", [P, 2, 3])
            xs = s1.sb("xs", [P, T])
            qkv = s1.sb("qkv", [P, 3, T])
            half = s1.sb("half", [P, 2, W])
            big = s1.sb("big", [P, 2, W])
            stats, mv = s1.sb("stats", [P, 3, NCH, 6]), s1.sb("mv", [P, 3, 2])
            ve, rs, scale, shift = (s1.sb(n, [P, 3]) for n in ("ve", "rs", "scale", "shift"))
            ps_t, ps_m = s1.ps("ps_t", [P, 2, 512]), s1.ps("ps_m", [P, 2, 3, 512])
            sem = {n: s1.sem(n) for n in ("in", "set", "tr", "half", "big", "xs", "mm", "read", "stats", "aggr", "var",
                                          "rstd", "affine", "nhalf", "nbig", "spike")}
            source = Combine(core, s1, r, add=core.x)
            with nc.Block() as block:
                @block.sync
                def _(sp):
                    sp.dma_start(w[:, :], ins["L1_attn_WqkvT"]).then_inc(sem["in"], 16)
                    with nc.allow_non_contiguous_dma("one value per feature"):
                        for k, n in enumerate(("L1_attn_gamma", "L1_attn_beta")):
                            sp.dma_start(gamma_beta[:, k, :], ins[n].rearrange("(m p) -> p m", p=P)).then_inc(sem["in"], 16)
                    source.sync(sp)
                    sp.wait_ge(sem["in"], 48)

                @block.tensor
                def _(pe):
                    def turn(c):
                        if c >= 2:
                            pe.wait_ge(sem["half"], c - 1)
                        pe.wait_ge(source.ready, c + 1)
                        for g in range(G):
                            last = nc.tensor.transpose(ps_t[:, c % 2, P * g:P * g + P], core.x[:, G * c + g, :], core.ident[:, :])
                        last.then_inc(sem["tr"], 1)

                    turn(0)
                    turn(1)
                    pe.wait_ge(sem["in"], 48)
                    for c in range(NCH):
                        pe.wait_ge(sem["xs"], c + 1)
                        if c >= 2:
                            pe.wait_ge(sem["read"], c - 1)
                            pe.wait_ge(sem["stats"], c - 1)
                        for m in range(3):
                            last = nc.tensor.matmul(ps_m[:, c % 2, m, :], w[:, P * m:P * m + P], xs[:, W * c:W * c + W],
                                                    start=True, stop=True)
                        last.then_inc(sem["mm"], 1)
                        if c + 2 < NCH:
                            turn(c + 2)

                @block.scalar
                def _(act):
                    act.wait_ge(sem["set"], 1)

                    def relu(c):
                        act.wait_ge(sem["tr"], c + 1)
                        if c >= 2:
                            act.wait_ge(sem["big"], c - 1)
                        nc.scalar.activation(half[:, c % 2, :], ps_t[:, c % 2, :], ACT.Relu, bias=tie_up[:, 0:1]).then_inc(sem["half"], 1)

                    relu(0)
                    for c in range(NCH):
                        if c + 1 < NCH:
                            relu(c + 1)
                        act.wait_ge(sem["stats"], c + 1)
                        nc.scalar.copy(qkv[:, :, W * c:W * c + W], ps_m[:, c % 2, :, :]).then_inc(sem["read"], 1)
                    act.wait_ge(sem["read"], NCH)
                    act.wait_ge(sem["affine"], 1)
                    for n in range(3 * NCH):
                        m, c = n // NCH, n % NCH
                        nc.scalar.activation(qkv[:, m, W * c:W * c + W], qkv[:, m, W * c:W * c + W], ACT.Relu,
                                             bias=shift[:, m:m + 1], scale=scale[:, m:m + 1]).then_inc(sem["nhalf"], 1)

                @block.gpsimd
                def _(pool):
                    source.gpsimd_add(0)
                    for c in range(NCH):
                        if c + 1 < NCH:
                            source.gpsimd_add(c + 1)
                        source.gpsimd(pool, c)
                    pool.wait_ge(sem["var"], 1)
                    nc.gpsimd.tensor_tensor(rs[:, :], ve[:, :], core.neg_half[:, 0:3], ALU.pow).then_inc(sem["rstd"], 1)

                @block.vector
                def _(dve):
                    tt, ts = nc.vector.tensor_tensor, nc.vector.tensor_scalar
                    nc.vector.memset(tie_up[:, :], TIE_UP).then_inc(sem["set"], 1)

                    def spike_x(c):
                        dve.wait_ge(sem["half"], c + 1)
                        ts(big[:, c % 2, :], half[:, c % 2, :], 4.0, MAGIC, ALU.min, ALU.add).then_inc(sem["big"], 1)
                        dve.wait_ge(sem["big"], c + 1)
                        ts(xs[:, W * c:W * c + W], big[:, c % 2, :], MAGIC, None, ALU.subtract).then_inc(sem["xs"], 1)

                    source.rows(dve, 0, range(r.k))
                    source.statistics(dve, 0)
                    source.rows(dve, 1, range(r.k))
                    source.scale(dve, 0)
                    source.statistics(dve, 1)
                    source.scale(dve, 1)
                    spike_x(0)
                    for c in range(NCH):
                        if c + 2 < NCH:
                            source.rows(dve, c + 2, range(r.k))
                            source.statistics(dve, c + 2)
                        if c + 1 < NCH:
                            spike_x(c + 1)
                        if c + 2 < NCH:
                            source.scale(dve, c + 2)
                        dve.wait_ge(sem["mm"], c + 1)
                        for m in range(3):
                            last = nc.vector.bn_stats(stats[:, m, c, :], ps_m[:, c % 2, m, :])
                        last.then_inc(sem["stats"], 1)
                    dve.wait_ge(sem["stats"], NCH)
                    for m in range(3):
                        last = nc.vector.bn_aggr(mv[:, m, :], stats[:, m, :, :].rearrange("p c s -> p (c s)"))
                    last.then_inc(sem["aggr"], 1)
                    dve.wait_ge(sem["aggr"], 1)
                    ts(ve[:, :], mv[:, :, 1], EPS, None, ALU.add).then_inc(sem["var"], 1)
                    dve.wait_ge(sem["rstd"], 1)
                    dve.wait_ge(sem["in"], 48)
                    tt(scale[:, :], rs[:, :], gamma_beta[:, 0, :], ALU.mult).then_inc(sem["aggr"], 1)
                    dve.wait_ge(sem["aggr"], 2)
                    tt(shift[:, :], mv[:, :, 0], scale[:, :], ALU.mult).then_inc(sem["aggr"], 1)
                    dve.wait_ge(sem["aggr"], 3)
                    tt(shift[:, :], gamma_beta[:, 1, :], shift[:, :], ALU.subtract).then_inc(sem["aggr"], 1)
                    dve.wait_ge(sem["aggr"], 4)
                    ts(shift[:, :], shift[:, :], TIE_UP, None, ALU.add).then_inc(sem["affine"], 1)
                    for n in range(3 * NCH):
                        m, c = n // NCH, n % NCH
                        one = qkv[:, m, W * c:W * c + W]
                        dve.wait_ge(sem["nhalf"], n + 1)
                        ts(one, one, 4.0, MAGIC, ALU.min, ALU.add).then_inc(sem["nbig"], 1)
                        dve.wait_ge(sem["nbig"], n + 1)
                        ts(spikes[:, m, W * c:W * c + W], one, MAGIC, None, ALU.subtract).then_inc(sem["spike"], 1)
                    dve.wait_ge(sem["spike"], 3 * NCH)

        with Stage(core, "l1s") as s2:
            wp = s2.sb("wp", [P, P])
            bias = s2.sb("bias", [P, 1, P])
            head_mask, mask_bf = s2.sb("head_mask", [P, HEADS]), s2.sb("mask_bf", [P, HEADS], BF16)
            ident_bf = s2.sb("ident_bf", [P, P], BF16)
            v = s2.sb("v", [P, 2, G, P], BF16)
            spread = s2.sb("spread", [P, 2, HEADS, P], BF16)
            att = s2.sb("att", [P, 2, UNIT, P], BF16)
            ohalf, obig = s2.sb("ohalf", [P, 2, P]), s2.sb("obig", [P, 2, P])
            o, ot = s2.sb("o", [P, 2, G, P]), s2.sb("ot", [P, 2, W])
            ps_v = s2.ps("ps_v", [P, 1, 1024], BF16)
            ps_s, ps_o, ps_m = s2.ps("ps_s", [P, 2, 512]), s2.ps("ps_o", [P, 2, 512]), s2.ps("ps_m", [P, 2, 512])
            sem = {n: s2.sem(n) for n in ("in", "set", "v_tr", "v", "sp_lo", "sp_hi", "score", "att", "pv", "ohalf",
                                          "obig", "o", "o_tr", "ot", "mm", "hb", "out", "normed")}
            norm = Norm(core, s2, "n")
            NU = 2 * B
            with nc.Block() as block:
                @block.sync
                def _(sp):
                    sp.dma_start(wp[:, :], ins["L1_attn_WprojT"]).then_inc(sem["in"], 16)
                    sp.dma_start(bias[:, :, :], ins["L1_attn_bproj"].unsqueeze(0).partition_broadcast(P)).then_inc(sem["in"], 16)
                    sp.dma_start(head_mask[:, :], ins["head_mask"]).then_inc(sem["in"], 16)
                    sp.wait_ge(sem["in"], 48)

                def spread_half(eng, b, half):
                    hs = slice(UNIT * half, UNIT * half + UNIT)
                    one = spikes[:, 0, P * b:P * b + P].unsqueeze(1).broadcast_to((P, UNIT, P))
                    return eng.tensor_tensor(spread[:, b % 2, hs, :], one,
                                             mask_bf[:, hs].unsqueeze(2).broadcast_to((P, UNIT, P)), ALU.mult)

                @block.gpsimd
                def _(pool):
                    pool.wait_ge(sem["set"], 2)
                    pool.wait_ge(sem["in"], 48)
                    for b in range(B):
                        if b >= 2:
                            pool.wait_ge(sem["score"], 2 * (b - 1))
                        spread_half(nc.gpsimd, b, 1).then_inc(sem["sp_hi"], 1)
                        if b % G == 0:
                            c = b // G
                            nc.gpsimd.tensor_tensor(chunk(core.h, c), chunk(core.h, c),
                                                    bias[:, :, :].broadcast_to((P, G, P)), ALU.add).then_inc(sem["hb"], 1)
                        if b % G == 2 and b >= 2 * G:
                            norm.rstd(pool, b // G - 2, b // G % 2)
                    norm.rstd(pool, NCH - 2, 0)
                    norm.rstd(pool, NCH - 1, 1)

                @block.tensor
                def _(pe):
                    pe.wait_ge(sem["set"], 2)

                    def turn_v(c):
                        if c >= 1:
                            pe.wait_ge(sem["v"], c)
                        for g in range(G):
                            last = nc.tensor.transpose(ps_v[:, 0, P * g:P * g + P], spikes[:, 2, W * c + P * g:W * c + P * g + P],
                                                       ident_bf[:, :])
                        last.then_inc(sem["v_tr"], 1)

                    def scores(n):
                        b, half = n // 2, n % 2
                        pe.wait_ge(sem["sp_hi" if half else "sp_lo"], b + 1)
                        if n >= 2:
                            pe.wait_ge(sem["att"], n - 1)
                        nc.tensor.matmul(ps_s[:, half, :], spikes[:, 1, P * b:P * b + P],
                                         spread[:, b % 2, UNIT * half:UNIT * half + UNIT, :],
                                         start=True, stop=True).then_inc(sem["score"], 1)

                    def value_product(n):
                        b, half = n // 2, n % 2
                        pe.wait_ge(sem["att"], n + 1)
                        pe.wait_ge(sem["v"], b // G + 1)
                        if half == 0 and b >= 2:
                            pe.wait_ge(sem["ohalf"], b - 1)
                        for j in range(UNIT):
                            hd = slice(HD * (UNIT * half + j), HD * (UNIT * half + j + 1))
                            last = nc.tensor.matmul(ps_o[:, b % 2, hd], att[:, n % 2, j, :], v[:, b // G % 2, b % G, hd],
                                                    start=True, stop=True)
                        last.then_inc(sem["pv"], 1)

                    def turn_o(c):
                        pe.wait_ge(sem["o"], G * (c + 1))
                        if c >= 1:
                            pe.wait_ge(sem["ot"], c)
                        for g in range(G):
                            last = nc.tensor.transpose(ps_m[:, 0, P * g:P * g + P], o[:, c % 2, g, :], core.ident[:, :])
                        last.then_inc(sem["o_tr"], 1)

                    def project(c):
                        pe.wait_ge(sem["ot"], c + 1)
                        if c >= 1:
                            pe.wait_ge(sem["out"], c)
                        for g in range(G):
                            last = nc.tensor.matmul(ps_m[:, 1, P * g:P * g + P], ot[:, c % 2, P * g:P * g + P], wp[:, :],
                                                    start=True, stop=True)
                        last.then_inc(sem["mm"], 1)

                    turn_v(0)
                    pe.wait_ge(sem["in"], 48)
                    for n in range(NU + 2):
                        c, k = n // (2 * G), n % (2 * G)
                        if n < NU:
                            scores(n)
                            if k == 1 and c + 1 < NCH:
                                turn_v(c + 1)
                        if n >= 2:
                            value_product(n - 2)
                        if k == 5 and c >= 1:
                            turn_o(c - 1)
                        if k == 6 and c >= 1:
                            project(c - 1)
                    turn_o(NCH - 1)
                    project(NCH - 1)

                @block.scalar
                def _(act):
                    for n in range(NU + 3):
                        c, k = n // (2 * G), n % (2 * G)
                        m = n - 3
                        if m >= 0 and m % 2 == 1:
                            b = m // 2
                            act.wait_ge(sem["pv"], 2 * b + 2)
                            if b >= 2:
                                act.wait_ge(sem["obig"], b - 1)
                            nc.scalar.activation(ohalf[:, b % 2, :], ps_o[:, b % 2, 0:P], ACT.Relu, bias=tie_up[:, 0:1],
                                                 scale=HD ** -0.5).then_inc(sem["ohalf"], 1)
                        if k == 1 and n < NU and c + 1 < NCH or n == 0:
                            nxt = 0 if n == 0 else c + 1
                            act.wait_ge(sem["v_tr"], nxt + 1)
                            if nxt >= 2:
                                act.wait_ge(sem["pv"], 2 * G * (nxt - 1))
                            nc.scalar.copy(flat(v[:, nxt % 2, :, :]), ps_v[:, 0, 0:W]).then_inc(sem["v"], 1)
                        if k == 5 and c >= 1:
                            act.wait_ge(sem["o_tr"], c)
                            if c >= 3:
                                act.wait_ge(sem["mm"], c - 2)
                            nc.scalar.copy(ot[:, (c - 1) % 2, :], ps_m[:, 0, :]).then_inc(sem["ot"], 1)
                    act.wait_ge(sem["o_tr"], NCH)
                    act.wait_ge(sem["mm"], NCH - 2)
                    nc.scalar.copy(ot[:, (NCH - 1) % 2, :], ps_m[:, 0, :]).then_inc(sem["ot"], 1)

                @block.vector
                def _(dve):
                    ts = nc.vector.tensor_scalar
                    dve.wait_ge(sem["in"], 48)
                    nc.vector.tensor_copy(mask_bf[:, :], head_mask[:, :]).then_inc(sem["set"], 1)
                    nc.vector.tensor_copy(ident_bf[:, :], core.ident[:, :]).then_inc(sem["set"], 1)
                    dve.wait_ge(sem["set"], 2)

                    def spread_low(b):
                        if b >= 2:
                            dve.wait_ge(sem["score"], 2 * (b - 1))
                        spread_half(nc.vector, b, 0).then_inc(sem["sp_lo"], 1)

                    def clip(n):
                        dve.wait_ge(sem["score"], n + 1)
                        if n >= 2:
                            dve.wait_ge(sem["pv"], n - 1)
                        ts(att[:, n % 2, :, :], bank4(ps_s[:, n % 2, :]), 4.0, None, ALU.min).then_inc(sem["att"], 1)

                    def spike_o(b):
                        dve.wait_ge(sem["ohalf"], b + 1)
                        c = b // G
                        if c >= 2 and b % G == 0:
                            dve.wait_ge(sem["o_tr"], c - 1)
                        ts(obig[:, b % 2, :], ohalf[:, b % 2, :], 4.0, MAGIC, ALU.min, ALU.add).then_inc(sem["obig"], 1)
                        dve.wait_ge(sem["obig"], b + 1)
                        ts(o[:, c % 2, b % G, :], obig[:, b % 2, :], MAGIC, None, ALU.subtract).then_inc(sem["o"], 1)

                    def residual(c):
                        dve.wait_ge(sem["mm"], c + 1)
                        dve.wait_ge(sem["hb"], c + 1)
                        nc.vector.tensor_tensor(chunk(core.h, c), bank4(ps_m[:, 1, :]), chunk(core.h, c),
                                                ALU.add).then_inc(sem["out"], 1)

                    def statistics(c):
                        dve.wait_ge(sem["out"], c + 1)
                        norm.statistics(dve, chunk(core.h, c), c, c % 2)

                    def scale(c):
                        norm.scale(dve, chunk(core.x, c), chunk(core.h, c), c, c % 2).then_inc(sem["normed"], 1)

                    spread_low(0)
                    for n in range(NU + 4):
                        c, k = n // (2 * G), n % (2 * G)
                        if n < NU:
                            if n % 2 == 0 and n // 2 + 1 < B:
                                spread_low(n // 2 + 1)
                            clip(n)
                        m = n - 4
                        if m >= 0 and m % 2 == 1:
                            spike_o(m // 2)
                        if k == 7 and c >= 1:
                            residual(c - 1)
                        if n < NU and c >= 2:
                            if k == 0:
                                statistics(c - 2)
                            elif k == 6:
                                scale(c - 2)
                    statistics(NCH - 2)
                    residual(NCH - 1)
                    statistics(NCH - 1)
                    scale(NCH - 2)
                    scale(NCH - 1)
                    dve.wait_ge(sem["normed"], NCH)


LEVELS = 5
ENTROPY_LIMIT = 0.8


def stage_l2_attn(core):
    nc, ins = core.nc, core.ins
    with Stage(core, "l2a") as st:
        acc = st.sb("acc", [P, B, P])
        z, ws = st.sb("z", [P, B, HEADS]), st.sb("ws", [P, B, HEADS])
        weight = st.sb("weight", [P, 1])
        go = st.sb("go", [P, 1], I32)
        with Stage(core, "l2i") as s0:
            ready = s0.sem("ready")
            with nc.Block() as block:
                @block.vector
                def _(dve):
                    nc.vector.memset(acc[:, :, :], 0.0)
                    nc.vector.memset(weight[:, :], 1.0).then_inc(ready, 1)
                    dve.wait_ge(ready, 1)
                    nc.vector.tensor_copy(go[:, :], weight[:, :]).then_inc(ready, 1)
                    dve.wait_ge(ready, 2)
        with nc.Fori(0, LEVELS):
            alive = nc.values_load(go[0:1, 0:1], min_val=0, max_val=1)
            with nc.If(alive > 0):
                Attention(core, "l2l", core.x, "L2_attn_wq", "L2_attn_wk", "L2_attn_wv", True, float(P) ** -0.5,
                          bq="L2_attn_bq", bk="L2_attn_bk", bv="L2_attn_bv", dst=core.x, sums=(z, ws)).run()
                l2_level_end(core, acc, z, ws, weight, go)
        l2_out(core, acc)


def l2_level_end(core, acc, z, ws, weight, go):
    nc = core.nc
    with Stage(core, "l2e") as st:
        logz, rz, ent = (st.sb(n, [P, B, HEADS]) for n in ("logz", "rz", "ent"))
        total, under = st.sb("total", [P, 1]), st.sb("under", [P, 1])
        ones = st.sb("ones", [P, P])
        ps = st.ps("ps", [P, 512])
        log_done, chain, total_done, all_done = (st.sem(n) for n in ("log_done", "chain", "total_done", "all_done"))
        with nc.Block() as block:
            @block.scalar
            def _(act):
                nc.scalar.activation(logz[:, :, :], z[:, :, :], ACT.Ln).then_inc(log_done, 1)

            @block.tensor
            def _(pe):
                pe.wait_ge(total_done, 1)
                nc.tensor.matmul(ps[:, 0:1], ones[:, :], total[:, :], start=True, stop=True).then_inc(all_done, 1)

            @block.vector
            def _(dve):
                made = [0]

                def then(*i):
                    i[-1].then_inc(chain, 1)
                    made[0] += 1
                    dve.wait_ge(chain, made[0])

                nc.vector.memset(ones[:, :], 1.0)
                for c in range(NCH):
                    i = nc.vector.scalar_tensor_tensor(out=chunk(acc, c), in0=chunk(core.x, c), scalar=weight[:, 0:1],
                                                       in1=chunk(acc, c), op0=ALU.mult, op1=ALU.add)
                then(i, nc.vector.reciprocal(rz[:, :, :], z[:, :, :]))
                then(nc.vector.tensor_tensor(ent[:, :, :], ws[:, :, :], rz[:, :, :], ALU.mult))
                dve.wait_ge(log_done, 1)
                then(nc.vector.scalar_tensor_tensor(out=ent[:, :, :], in0=ent[:, :, :], scalar=-float(P) ** -0.5,
                                                    in1=logz[:, :, :], op0=ALU.mult, op1=ALU.add))
                nc.vector.tensor_reduce(total[:, :], flat(ent[:, :, :]), AX_X, ALU.add).then_inc(total_done, 1)
                dve.wait_ge(all_done, 1)
                mean = 1.0 / (B * P * HEADS * float(np.log(np.float32(P))))
                then(nc.vector.tensor_scalar(under[:, :], ps[:, 0:1], mean, ENTROPY_LIMIT, ALU.mult, ALU.is_lt))
                then(nc.vector.tensor_tensor(weight[:, :], weight[:, :], under[:, :], ALU.mult))
                then(nc.vector.tensor_copy(go[:, :], weight[:, :]))


def l2_out(core, acc):
    nc, ins = core.nc, core.ins
    with Stage(core, "l2o") as st:
        w, bias = st.sb("w", [P, P]), st.sb("bias", [P, 1, P])
        at = st.sb("at", [P, 2, W])
        ps_t, ps_o = st.ps("ps_t", [P, 2, 512]), st.ps("ps_o", [P, 2, 512])
        loaded, turned, copied, mm, biased, added = (st.sem(n) for n in ("loaded", "turned", "copied", "mm", "biased", "added"))
        norm, normed = Norm(core, st), st.sem("normed")
        with nc.Block() as block:
            @block.sync
            def _(sp):
                sp.dma_start(w[:, :], ins["L2_attn_w_out"]).then_inc(loaded, 16)
                sp.dma_start(bias[:, :, :], ins["L2_attn_b_out"].unsqueeze(0).partition_broadcast(P)).then_inc(loaded, 16)
                sp.wait_ge(loaded, 32)

            @block.tensor
            def _(pe):
                def turn(c):
                    if c >= 2:
                        pe.wait_ge(copied, c - 1)
                    for g in range(G):
                        last = nc.tensor.transpose(ps_t[:, c % 2, P * g:P * g + P], acc[:, G * c + g, :], core.ident[:, :])
                    last.then_inc(turned, 1)

                turn(0)
                pe.wait_ge(loaded, 32)
                for c in range(NCH):
                    if c + 1 < NCH:
                        turn(c + 1)
                    pe.wait_ge(copied, c + 1)
                    if c >= 2:
                        pe.wait_ge(added, c - 1)
                    for g in range(G):
                        last = nc.tensor.matmul(ps_o[:, c % 2, P * g:P * g + P], at[:, c % 2, P * g:P * g + P], w[:, :],
                                                start=True, stop=True)
                    last.then_inc(mm, 1)

            @block.scalar
            def _(act):
                for c in range(NCH):
                    act.wait_ge(turned, c + 1)
                    if c >= 2:
                        act.wait_ge(mm, c - 1)
                    nc.scalar.copy(at[:, c % 2, :], ps_t[:, c % 2, :]).then_inc(copied, 1)

            @block.gpsimd
            def _(pool):
                pool.wait_ge(loaded, 32)
                for c in range(NCH):
                    nc.gpsimd.tensor_tensor(chunk(core.h, c), chunk(core.h, c), bias[:, :, :].broadcast_to((P, G, P)),
                                            ALU.add).then_inc(biased, 1)
                    if c:
                        norm.rstd(pool, c - 1, (c - 1) % 2)
                norm.rstd(pool, NCH - 1, (NCH - 1) % 2)

            @block.vector
            def _(dve):
                def scale(c):
                    norm.scale(dve, chunk(core.x, c), chunk(core.h, c), c, c % 2).then_inc(normed, 1)

                for c in range(NCH):
                    dve.wait_ge(mm, c + 1)
                    dve.wait_ge(biased, c + 1)
                    nc.vector.tensor_tensor(chunk(core.h, c), bank4(ps_o[:, c % 2, :]), chunk(core.h, c), ALU.add).then_inc(added, 1)
                    dve.wait_ge(added, c + 1)
                    norm.statistics(dve, chunk(core.h, c), c, c % 2)
                    if c:
                        scale(c - 1)
                scale(NCH - 1)
                dve.wait_ge(normed, NCH)


def tower(nc, ins, out):
    with ExitStack() as ctx:
        core = Core(nc, ctx, ins)
        with Stage(core, "l0") as st:
            u = st.sb("u", [P, B, P])
            with Stage(core, "s4") as st2:
                kf, ids = st2.sb("kf", [P, 3, NL, P]), st2.sb("ids", [P, B], I32)
                stage_setup(core, ids)
                s4_kernels(core, kf, ids, u)
                stage_l0_attn(core, kf, u)
            stage_l0_ffn_l1_attn(core, u)
        stage_l1_ffn(core)
        stage_l2_attn(core)
        stage_l2_ffn_l3_attn(core)
        stage_l3_ffn(core, out)


def decay_table():
    gamma = 1.0 - 2.0 ** (-5.0 - np.arange(HEADS))
    rel = np.arange(P)[:, None] - np.arange(P)[None, :]
    table = np.where(rel[:, None, :] >= 0, gamma[None, :, None] ** np.maximum(rel, 0)[:, None, :], 0.0)
    return (table / np.sqrt(HD)).astype(np.float32)


PACKED = ("L0_ffn_w1", "L0_ffn_w2", "L0_ffn_b", "L1_ffn_W1", "L1_ffn_W2", "L1_ffn_b1", "L1_ffn_b2", "L2_ffn_W1",
          "L2_ffn_W2", "L2_ffn_b", "L2_ffn_gamma", "L3_ffn_re")


def host_layout(inputs):
    a = {k: np.ascontiguousarray(v) for k, v in inputs.items()}
    out = {}
    put = lambda name, v: out.__setitem__(name, np.ascontiguousarray(v))
    for name in ("x", "L0_tok_w", "L0_attn_s4_log_A_real", "L0_attn_s4_A_imag", "L0_attn_s4_C_re", "L0_attn_s4_C_im",
                 "L0_attn_s4_log_dt", "L0_attn_s4_D"):
        put(name, a[name])
    for name in ("s4_out_b", "ln1_w", "ln1_b", "ln2_w", "ln2_b", "ff_b1", "ff_b2"):
        put("L0_attn_" + name, a["L0_attn_" + name])
    put("s4_out_wT", a["L0_attn_s4_out_w"].reshape(NL, 2 * P, P).transpose(2, 0, 1))
    put("ff_w1T", a["L0_attn_ff_w1"].transpose(0, 2, 1))
    put("ff_w2T", a["L0_attn_ff_w2"].reshape(DEPTH, P, 4, P).transpose(0, 3, 2, 1))
    for name in a:
        if name.startswith(("L0_ffn", "L1", "L2", "L3")) and not name.startswith(PACKED):
            put(name, a[name])
    for name in ("wq", "wk", "wv", "wg"):
        put("L3_attn_" + name, a["L3_attn_" + name].T)
    by_feature = lambda t: t.reshape(t.shape[0], -1, P).transpose(0, 2, 1)
    put("L3_ffn_se_b1", by_feature(a["L3_ffn_se_b1"]))
    for layer, w1, b1, w2, rows in (("L0_ffn", "w1", "b1", "w2", ("b2",)), ("L1_ffn", "W1", "b1", "W2", ("b2",)),
                                    ("L2_ffn", "W1", "b1", "W2", ("b2", "gamma", "beta")),
                                    ("L3_ffn", "re_w1", "re_b1", "re_w2", ("re_b2",))):
        w1, b1, w2 = (a[f"{layer}_{n}"] for n in (w1, b1, w2))
        E = w1.shape[0]
        w2 = w2.reshape(E, -1, P, P).transpose(0, 2, 1, 3).reshape(E, P, -1)
        put(layer + "_packed", np.concatenate([w1, w2, by_feature(b1)], axis=2))
        put(layer + "_rows", np.stack([a[f"{layer}_{n}"] for n in rows], axis=1))
    put("L3_ffn_gate_wT", a["L3_ffn_gate_w"].T)
    put("iota_row", np.broadcast_to(np.arange(P, dtype=np.float32), (P, P)))
    put("token", (np.arange(B)[None, :] * P + np.arange(P)[:, None]).astype(np.float32))
    put("tri", np.triu(np.ones((P, P), np.float32), 1))
    put("L1_attn_WqkvT", a["L1_attn_Wqkv"].T)
    put("L1_attn_WprojT", a["L1_attn_Wproj"].T)
    for n, part in enumerate("qkv"):
        put("L2_attn_w" + part, a["L2_attn_w_qkv"][:, n * P:(n + 1) * P])
        put("L2_attn_b" + part, a["L2_attn_b_qkv"][n * P:(n + 1) * P])
    put("head_mask", (np.arange(P)[:, None] // HD == np.arange(HEADS)[None, :]).astype(np.float32))
    put("decay", decay_table())
    put("ident", np.eye(P, dtype=np.float32))
    put("dft", dft_tables())
    return out


def kernel(**inputs):
    import concourse.bacc as _bacc
    from concourse.bass_utils import run_bass_kernel_spmd as _run
    nc = _bacc.Bacc("TRN2", target_bir_lowering=False, num_devices=1)
    arrays, ins = {}, {}
    for name, a in host_layout(inputs).items():
        arrays[f"in_{name}_dram"] = a
        ins[name] = nc.dram_tensor(f"in_{name}_dram", a.shape, mybir.dt.from_np(a.dtype), kind="ExternalInput").ap()
    out = nc.dram_tensor("out_0_dram", (B, P, P), F32, kind="ExternalOutput").ap()
    tower(nc, ins, out)
    r = _run(nc, [arrays], core_ids=[0])
    return r.results[0]["out_0_dram"]
```
